# Optimizing a Trainium2 kernel written in Bass

```python
import numpy as np
import jax
import jax.numpy as jnp

def _softmax(x, axis=-1):
    return jax.nn.softmax(x, axis=axis)

def _gelu(x):
    return jax.nn.gelu(x, approximate=True)

def _silu(x):
    return jax.nn.silu(x)

def _sigmoid(x):
    return jax.nn.sigmoid(x)

def _layernorm(x, axis=-1, eps=1e-05):
    m = jnp.mean(x, axis=axis, keepdims=True)
    v = jnp.var(x, axis=axis, keepdims=True)
    return (x - m) / jnp.sqrt(v + eps)

def _scatter_add(tgt, idx, src, axis=0):
    return tgt.at[idx].add(src)

def _segment_sum(src, seg, n):
    return jax.ops.segment_sum(src, seg, n)
kernel_name = 'mk_early_fusion_embed_d1_tok_img512_r4_c27e4c'

def setup_inputs(seed: int=0):
    np.random.seed(seed)
    _w = jnp.asarray

    def _rec_inputs():
        import jax
        import jax.numpy as jnp
        _rk = jax.random.key(seed)
        x = -0.000147625 + 0.999875 * jax.random.normal(jax.random.fold_in(_rk, 1), (64, 3, 224, 224), jnp.float32)
        x_txt = jax.random.randint(jax.random.fold_in(_rk, 51), (64, 77), 0, 50, jnp.int32)
        return (x, x_txt)
    x, x_txt = _rec_inputs()

    def _L0_tok_setup():
        import jax, jax.numpy as jnp
        import numpy as np
        N_PATCHES = 8
        PATCH = 28
        C = 3
        IN_D = C * PATCH * PATCH
        HID = 128
        SEQ = N_PATCHES * N_PATCHES + 1

        def _positional_embedding(seq_len, dim):
            i = np.arange(seq_len)[:, None].astype(np.float32)
            j = np.arange(dim)[None, :].astype(np.float32)
            ang = i / np.power(100000.0, j / dim)
            pe = np.where(j % 2 == 0, np.sin(ang), np.cos(ang))
            return jnp.asarray(pe, dtype=jnp.float32)
        key = jax.random.key(seed)
        k1, k2, k3, k4 = jax.random.split(key, 4)
        B = 64
        X = jax.random.normal(k1, (B, C, 224, 224), dtype=jnp.float32)
        bound = 1.0 / np.sqrt(IN_D)
        W = jax.random.uniform(k2, (HID, IN_D), minval=-bound, maxval=bound, dtype=jnp.float32)
        b = jax.random.uniform(k3, (HID,), minval=-bound, maxval=bound, dtype=jnp.float32)
        class_token = jax.random.uniform(k4, (1, HID), dtype=jnp.float32)
        pos_embed = _positional_embedding(SEQ, HID)
        return {'X': X, 'W': W, 'b': b, 'class_token': class_token, 'pos_embed': pos_embed}
    _L0_tok_all = _L0_tok_setup()
    _L0_tok_in = {k: v for k, v in _L0_tok_all.items() if k in ('W', 'b', 'class_token', 'pos_embed')}
    del _L0_tok_all

    def _L0_txt_setup():
        import jax, jax.numpy as jnp
        import numpy as np
        D_MODEL = 128
        END_IDX = 2

        def _build_tree(tokens):
            B, T = tokens.shape
            cap = 2 * T + 2
            left2 = jnp.array([1.0, 0.0], jnp.float32)
            right2 = jnp.array([0.0, 1.0], jnp.float32)
            bidx = jnp.arange(B)
            X0 = jnp.zeros((B, T, D_MODEL), jnp.float32)
            par0 = jnp.zeros((B, cap), jnp.int32)
            lr0 = jnp.zeros((B, cap), jnp.int32)
            head0 = jnp.zeros((B,), jnp.int32)
            tail0 = jnp.zeros((B,), jnp.int32)

            def body(carry, t):
                X, par, lr, head, tail = carry
                parent = par[bidx, head]
                plr = lr[bidx, head]
                x_parent = X[bidx, parent]
                lrvec = jnp.where(plr[:, None] == 0, left2, right2)
                x_it = jnp.concatenate([lrvec, x_parent[:, :-2]], axis=1)
                x_it = jnp.where(t == 0, 0.0, x_it)
                X = X.at[bidx, t].set(x_it)
                tok = tokens[bidx, t]
                push = jnp.where(t == 0, True, tok != END_IDX)
                tval = jnp.full((B,), 0, jnp.int32) + jnp.int32(t)
                par = par.at[bidx, tail].set(tval).at[bidx, tail + 1].set(tval)
                lr = lr.at[bidx, tail].set(0).at[bidx, tail + 1].set(1)
                tail = tail + 2 * push.astype(jnp.int32)
                pop = (t > 0) & (tail - head > 1)
                head = head + pop.astype(jnp.int32)
                return ((X, par, lr, head, tail), None)
            (X, _, _, _, _), _ = jax.lax.scan(body, (X0, par0, lr0, head0, tail0), jnp.arange(T))
            return X
        key = jax.random.key(seed)
        tokens = jax.random.randint(key, (64, 256), 0, 50, dtype=jnp.int32)
        p = jnp.ones((1,), dtype=jnp.float32)
        return {'tokens': tokens, 'p': p}
    _L0_txt_all = _L0_txt_setup()
    _L0_txt_in = {k: v for k, v in _L0_txt_all.items() if k in ('p',)}
    del _L0_txt_all

    def _L0_attn_setup():
        import jax, jax.numpy as jnp
        import numpy as np
        B, S, IN, HD, H = (2, 512, 128, 32, 16)
        key = jax.random.key(seed)
        ks = jax.random.split(key, 9)
        sc = 0.02
        return {'x': jax.random.normal(ks[0], (B, S, IN), jnp.float32), 'Wl': jax.random.normal(ks[1], (H, IN, IN), jnp.float32) * sc, 'bl': jax.random.normal(ks[2], (H, IN), jnp.float32) * sc, 'Wq': jax.random.normal(ks[3], (H, IN, HD), jnp.float32) * sc, 'Wk': jax.random.normal(ks[4], (H, IN, HD), jnp.float32) * sc, 'Wv': jax.random.normal(ks[5], (H, IN, HD), jnp.float32) * sc, 'Wo': jax.random.normal(ks[6], (IN, H * HD), jnp.float32) * sc, 'bo': jax.random.normal(ks[7], (IN,), jnp.float32) * sc}
    _L0_attn_all = _L0_attn_setup()
    _L0_attn_in = {k: v for k, v in _L0_attn_all.items() if k in ('Wl', 'bl', 'Wq', 'Wk', 'Wv', 'Wo', 'bo')}
    del _L0_attn_all

    def _L0_ffn_setup():
        import jax, jax.numpy as jnp
        import numpy as np
        H = 128
        F = 512
        E = 16
        SHARED = 2
        TOP_K = 4
        B, S = (2, 512)

        def _mlp(x, w1, b1, w2, b2):
            return jax.nn.gelu(x @ w1 + b1, approximate=False) @ w2 + b2
        key = jax.random.key(seed)
        ks = jax.random.split(key, 10)
        sc = 0.02
        return {'hidden_states': jax.random.normal(ks[0], (B, S, H), dtype=jnp.float32), 'gate_w': jax.random.normal(ks[1], (E, H), dtype=jnp.float32) * sc, 're_w1': jax.random.normal(ks[2], (E, H, F), dtype=jnp.float32) * sc, 're_b1': jnp.zeros((E, F), dtype=jnp.float32), 're_w2': jax.random.normal(ks[3], (E, F, H), dtype=jnp.float32) * sc, 're_b2': jnp.zeros((E, H), dtype=jnp.float32), 'se_w1': jax.random.normal(ks[4], (SHARED, H, F), dtype=jnp.float32) * sc, 'se_b1': jnp.zeros((SHARED, F), dtype=jnp.float32), 'se_w2': jax.random.normal(ks[5], (SHARED, F, H), dtype=jnp.float32) * sc, 'se_b2': jnp.zeros((SHARED, H), dtype=jnp.float32)}
    _L0_ffn_all = _L0_ffn_setup()
    _L0_ffn_in = {k: v for k, v in _L0_ffn_all.items() if k in ('gate_w', 're_w1', 're_b1', 're_w2', 're_b2', 'se_w1', 'se_b1', 'se_w2', 'se_b2')}
    del _L0_ffn_all
    return {'x': x, 'x_txt': x_txt, 'L0_tok_W': _L0_tok_in['W'], 'L0_tok_b': _L0_tok_in['b'], 'L0_tok_class_token': _L0_tok_in['class_token'], 'L0_tok_pos_embed': _L0_tok_in['pos_embed'], 'L0_txt_p': _L0_txt_in['p'], 'L0_attn_Wl': _L0_attn_in['Wl'], 'L0_attn_bl': _L0_attn_in['bl'], 'L0_attn_Wq': _L0_attn_in['Wq'], 'L0_attn_Wk': _L0_attn_in['Wk'], 'L0_attn_Wv': _L0_attn_in['Wv'], 'L0_attn_Wo': _L0_attn_in['Wo'], 'L0_attn_bo': _L0_attn_in['bo'], 'L0_ffn_gate_w': _L0_ffn_in['gate_w'], 'L0_ffn_re_w1': _L0_ffn_in['re_w1'], 'L0_ffn_re_b1': _L0_ffn_in['re_b1'], 'L0_ffn_re_w2': _L0_ffn_in['re_w2'], 'L0_ffn_re_b2': _L0_ffn_in['re_b2'], 'L0_ffn_se_w1': _L0_ffn_in['se_w1'], 'L0_ffn_se_b1': _L0_ffn_in['se_b1'], 'L0_ffn_se_w2': _L0_ffn_in['se_w2'], 'L0_ffn_se_b2': _L0_ffn_in['se_b2']}

def reference(x, x_txt, L0_tok_W, L0_tok_b, L0_tok_class_token, L0_tok_pos_embed, L0_txt_p, L0_attn_Wl, L0_attn_bl, L0_attn_Wq, L0_attn_Wk, L0_attn_Wv, L0_attn_Wo, L0_attn_bo, L0_ffn_gate_w, L0_ffn_re_w1, L0_ffn_re_b1, L0_ffn_re_w2, L0_ffn_re_b2, L0_ffn_se_w1, L0_ffn_se_b1, L0_ffn_se_w2, L0_ffn_se_b2):
    import jax
    import jax.numpy as jnp

    def _L0_tok_ref(X, W, b, class_token, pos_embed):
        import jax, jax.numpy as jnp
        import numpy as np
        N_PATCHES = 8
        PATCH = 28
        C = 3
        IN_D = C * PATCH * PATCH
        HID = 128
        SEQ = N_PATCHES * N_PATCHES + 1

        def _positional_embedding(seq_len, dim):
            i = np.arange(seq_len)[:, None].astype(np.float32)
            j = np.arange(dim)[None, :].astype(np.float32)
            ang = i / np.power(100000.0, j / dim)
            pe = np.where(j % 2 == 0, np.sin(ang), np.cos(ang))
            return jnp.asarray(pe, dtype=jnp.float32)
        B = X.shape[0]
        patches = X.reshape(B, C, N_PATCHES, PATCH, N_PATCHES, PATCH)
        patches = patches.transpose(0, 2, 4, 1, 3, 5).reshape(B, N_PATCHES * N_PATCHES, IN_D)
        tokens = jnp.einsum('bpi,hi->bph', patches, W) + b
        cls = jnp.broadcast_to(class_token[None, :, :], (B, 1, HID))
        tokens = jnp.concatenate([cls, tokens], axis=1)
        return tokens * pos_embed[None, :, :]

    def _L0_txt_ref(tokens, p):
        import jax, jax.numpy as jnp
        import numpy as np
        D_MODEL = 128
        END_IDX = 2

        def _build_tree(tokens):
            B, T = tokens.shape
            cap = 2 * T + 2
            left2 = jnp.array([1.0, 0.0], jnp.float32)
            right2 = jnp.array([0.0, 1.0], jnp.float32)
            bidx = jnp.arange(B)
            X0 = jnp.zeros((B, T, D_MODEL), jnp.float32)
            par0 = jnp.zeros((B, cap), jnp.int32)
            lr0 = jnp.zeros((B, cap), jnp.int32)
            head0 = jnp.zeros((B,), jnp.int32)
            tail0 = jnp.zeros((B,), jnp.int32)

            def body(carry, t):
                X, par, lr, head, tail = carry
                parent = par[bidx, head]
                plr = lr[bidx, head]
                x_parent = X[bidx, parent]
                lrvec = jnp.where(plr[:, None] == 0, left2, right2)
                x_it = jnp.concatenate([lrvec, x_parent[:, :-2]], axis=1)
                x_it = jnp.where(t == 0, 0.0, x_it)
                X = X.at[bidx, t].set(x_it)
                tok = tokens[bidx, t]
                push = jnp.where(t == 0, True, tok != END_IDX)
                tval = jnp.full((B,), 0, jnp.int32) + jnp.int32(t)
                par = par.at[bidx, tail].set(tval).at[bidx, tail + 1].set(tval)
                lr = lr.at[bidx, tail].set(0).at[bidx, tail + 1].set(1)
                tail = tail + 2 * push.astype(jnp.int32)
                pop = (t > 0) & (tail - head > 1)
                head = head + pop.astype(jnp.int32)
                return ((X, par, lr, head, tail), None)
            (X, _, _, _, _), _ = jax.lax.scan(body, (X0, par0, lr0, head0, tail0), jnp.arange(T))
            return X
        X = _build_tree(tokens)
        poly = p ** jnp.arange(D_MODEL, dtype=jnp.float32)
        return X * poly

    def _L0_attn_ref(x, Wl, bl, Wq, Wk, Wv, Wo, bo):
        import jax, jax.numpy as jnp
        import numpy as np
        B, S, IN, HD, H = (2, 512, 128, 32, 16)
        b, s, _ = x.shape
        h, _, hd = Wq.shape
        xh = jnp.einsum('bsi,hoi->bhso', x, Wl) + bl[None, :, None, :]
        Q = jnp.einsum('bhsi,hid->bhsd', xh, Wq)
        K = jnp.einsum('bhsi,hid->bhsd', xh, Wk)
        V = jnp.einsum('bhsi,hid->bhsd', xh, Wv)
        scores = jnp.einsum('bhsd,bhtd->bhst', Q, K)
        causal = jnp.triu(jnp.ones((s, s), dtype=bool), k=1)
        scores = jnp.where(causal[None, None], -jnp.inf, scores)
        A = jax.nn.softmax(scores, axis=-1)
        F = jnp.einsum('bhst,bhtd->bhsd', A, V)
        cat = jnp.transpose(F, (0, 2, 1, 3)).reshape(b, s, h * hd)
        return cat @ Wo.T + bo

    def _L0_ffn_ref(hidden_states, gate_w, re_w1, re_b1, re_w2, re_b2, se_w1, se_b1, se_w2, se_b2):
        import jax, jax.numpy as jnp
        import numpy as np
        H = 128
        F = 512
        E = 16
        SHARED = 2
        TOP_K = 4
        B, S = (2, 512)

        def _mlp(x, w1, b1, w2, b2):
            return jax.nn.gelu(x @ w1 + b1, approximate=False) @ w2 + b2
        b, s, h = hidden_states.shape
        x = hidden_states.reshape(-1, h)
        gate_probs = jax.nn.softmax(x @ gate_w.T, axis=-1)
        top_v, top_i = jax.lax.top_k(gate_probs, TOP_K)
        top_v = jax.nn.softmax(top_v, axis=-1)
        combine = jnp.einsum('tk,tke->te', top_v, jax.nn.one_hot(top_i, E, dtype=x.dtype))
        routed = jnp.zeros_like(x)
        for e in range(E):
            routed = routed + combine[:, e:e + 1] * _mlp(x, re_w1[e], re_b1[e], re_w2[e], re_b2[e])
        shared = jnp.zeros_like(x)
        for j in range(SHARED):
            shared = shared + _mlp(x, se_w1[j], se_b1[j], se_w2[j], se_b2[j])
        shared = shared / SHARED
        return (routed + shared).reshape(b, s, h)
    h = _L0_tok_ref(x, L0_tok_W, L0_tok_b, L0_tok_class_token, L0_tok_pos_embed)
    h = jnp.concatenate([h, _L0_txt_ref(x_txt, L0_txt_p)], axis=1)
    h = h + _L0_attn_ref(_layernorm(h, axis=-1), L0_attn_Wl, L0_attn_bl, L0_attn_Wq, L0_attn_Wk, L0_attn_Wv, L0_attn_Wo, L0_attn_bo)
    h = h + _L0_ffn_ref(_layernorm(h, axis=-1), L0_ffn_gate_w, L0_ffn_re_w1, L0_ffn_re_b1, L0_ffn_re_w2, L0_ffn_re_b2, L0_ffn_se_w1, L0_ffn_se_b1, L0_ffn_se_w2, L0_ffn_se_b2)
    return h

_drawn_inputs = setup_inputs


def setup_inputs(seed=0):
    import zlib

    import numpy as np

    out = dict(_drawn_inputs(seed))
    spreads = {'L0_ffn_re_b1': (0.0, 0.1),
     'L0_ffn_re_b2': (0.0, 0.1),
     'L0_ffn_se_b1': (0.0, 0.1),
     'L0_ffn_se_b2': (0.0, 0.1)}
    factors = {'L0_attn_Wq': 8.0, 'L0_attn_Wk': 8.0}
    for name, (base, spread) in spreads.items():
        noise = np.random.default_rng([zlib.crc32(name.encode()), seed]).standard_normal(out[name].shape)
        drawn = base * np.exp(spread * noise) if base else spread * noise
        out[name] = jnp.asarray(drawn.astype(out[name].dtype))
    for name, factor in factors.items():
        out[name] = (out[name] * factor).astype(out[name].dtype)
    return out
```

```python
import concourse.bass as bass
from concourse import mybir
from contextlib import ExitStack

F32 = mybir.dt.float32
BF16 = mybir.dt.bfloat16
I32 = mybir.dt.int32
U32 = mybir.dt.uint32
ALU = mybir.AluOpType
ACT = mybir.ActivationFunctionType
AX = mybir.AxisListType

IMAGES, CHANNELS, SIDE = 64, 3, 224
GRID, PATCH = 8, 28
D = 128
PATCHES = GRID * GRID
TEXT = 77
SEQ = 1 + PATCHES + TEXT
TOKENS = IMAGES * SEQ
ROWS = CHANNELS * PATCH
END_TOKEN = 2
HEADS, HD = 16, 32
QUADS, QH = 4, 4
MAIN = 128
TAIL = SEQ - MAIN
EXPERTS, SHARED, HIDDEN, TOPK = 16, 2, 512, 4
ALL_EXPERTS = EXPERTS + SHARED
FB = HIDDEN // 128
TILES = TOKENS // 128
MASKED = -1e30
LN_EPS = 1e-5
TREE_LEVELS = 6


def build(nc, x, x_txt, tok_W, tok_b, tok_cls, tok_pos, txt_p, Wl, bl, Wq, Wk, Wv, Wo, bo,
          gate_w, re_w1, re_b1, re_w2, re_b2, se_w1, se_b1, se_w2, se_b2, out):
    ctx = ExitStack()
    with ctx:
        def sb(name, shape, dt=F32):
            return ctx.enter_context(nc.sbuf_tensor(name, shape, dt))

        def sem(name):
            return ctx.enter_context(nc.semaphore(name))

        bank = [ctx.enter_context(nc.psum_tensor(f"bank{i}", [128, 512], F32)) for i in range(8)]

        hT = sb("hT", [D, TOKENS])
        xT = sb("xT", [D, TOKENS + 2 * SEQ])
        W_ELEMS = ALL_EXPERTS * 2 * HIDDEN
        patch_wT = xT[0:ROWS, 5000:5000 + PATCH * D].rearrange("r (k d) -> r k d", k=PATCH)
        region = sb("region", [128, W_ELEMS])
        ident = sb("ident", [128, 128])
        identb = sb("identb", [128, 128], BF16)
        centre = sb("centre", [128, 128])
        mean_of = sb("mean_of", [128, 128])
        eps_col = sb("eps_col", [128, 1])
        posT = sb("posT", [D, 1 + PATCHES])
        patch_b = sb("patch_b", [D, 1])
        poly = sb("poly", [D, 1])
        qkv_w = sb("qkv_w", [D, 3, HEADS, HD])
        qkv_b = sb("qkv_b", [128, 3 * QUADS])
        woT = sb("woT", [128, QUADS, D])
        out_b = sb("out_b", [D, 1])
        head_rows = sb("head_rows", [128, QH])
        gate_wT = sb("gate_wT", [D, EXPERTS])
        b1T = sb("b1T", [128, ALL_EXPERTS * FB])
        b2_rows = sb("b2_rows", [EXPERTS, D])
        shared_b2 = sb("shared_b2", [D, 1])
        work = sb("work", [128, 9600])

        CHUNK_IMAGES = 4
        XT = CHUNK_IMAGES * GRID * SIDE
        x_tile = [region[0:ROWS, u * XT:(u + 1) * XT] for u in range(2)]
        o = 2 * XT
        wl_sb = region[:, o:o + HEADS * D].rearrange("p (h i) -> p h i", h=HEADS)
        o += HEADS * D
        wqkv_sb = region[:, o:o + HEADS * 3 * HD].rearrange("p (h c d) -> p h c d", h=HEADS, c=3)
        o += HEADS * 3 * HD
        wo_sb = region[:, o:o + HEADS * HD]
        assert o + HEADS * HD <= W_ELEMS

        tokens_in, patchw_in, attnw_in, ffnb_in = (sem(n) for n in ("tokens_in", "patchw_in", "attnw_in", "ffnb_in"))
        pool_const = sem("pool_const")
        dve_const = sem("dve_const")
        setup_mm = sem("setup_mm")
        setup_ev = sem("setup_ev")
        fold_mm = sem("fold_mm")
        fold_ev = sem("fold_ev")

        w_raw = hT[:, 0:CHANNELS * PATCH * PATCH]
        small = hT[:, 2400:2400 + 1024]
        pos_raw = small[0:1 + PATCHES, 0:128]
        cls_raw = small[0:1, 128:256]
        bl_raw = small[0:HEADS, 256:384]
        gate_raw = small[0:EXPERTS, 384:512]
        b1_raw = small[0:ALL_EXPERTS * FB, 512:640]
        sb2_raw = small[0:SHARED, 640:768]
        blT = small[:, 768:784]
        clsT_src = small[0:1, 800:928]
        bo_col = sb("bo_col", [D, 1])
        p_row = sb("p_row", [1, 1])
        poly_row = sb("poly_row", [1, D])
        posc = sb("posc", [D, 2])

        def setup_loads(sp):
            sp.dma_start(tok_i[:, :], x_txt).then_inc(tokens_in, 16)
            sp.dma_start(p_row[:, :], txt_p.rearrange("(a n) -> a n", a=1)).then_inc(tokens_in, 16)
            sp.dma_start(w_raw, tok_W).then_inc(patchw_in, 16)
            sp.dma_start(pos_raw, tok_pos).then_inc(patchw_in, 16)
            sp.dma_start(cls_raw, tok_cls).then_inc(patchw_in, 16)
            sp.dma_start(patch_b[:, :], tok_b.rearrange("(p a) -> p a", a=1)).then_inc(patchw_in, 16)
            sp.dma_start(wl_sb, Wl.rearrange("h o i -> o h i")).then_inc(attnw_in, 16)
            for c, w in enumerate((Wq, Wk, Wv)):
                sp.dma_start(wqkv_sb[:, :, c, :], w.rearrange("h i d -> i h d")).then_inc(attnw_in, 16)
            sp.dma_start(wo_sb, Wo).then_inc(attnw_in, 16)
            sp.dma_start(bl_raw, bl).then_inc(attnw_in, 16)
            sp.dma_start(bo_col[:, :], bo.rearrange("(p a) -> p a", a=1)).then_inc(attnw_in, 16)
            sp.dma_start(gate_raw, gate_w).then_inc(ffnb_in, 16)
            sp.dma_start(b1_raw[0:EXPERTS * FB, :], re_b1.rearrange("e (f p) -> (e f) p", p=128)).then_inc(ffnb_in, 16)
            sp.dma_start(b1_raw[EXPERTS * FB:ALL_EXPERTS * FB, :],
                         se_b1.rearrange("e (f p) -> (e f) p", p=128)).then_inc(ffnb_in, 16)
            sp.dma_start(b2_rows[:, :], re_b2).then_inc(ffnb_in, 16)
            sp.dma_start(sb2_raw, se_b2).then_inc(ffnb_in, 16)

        def setup_pool(pool):
            nc.gpsimd.memset(ident[:, :], 0.0).then_inc(pool_const, 1)
            pool.wait_ge(pool_const, 1)
            nc.gpsimd.affine_select(out=ident[:, :], in_=ident[:, :], compare_op=ALU.not_equal, fill=1.0,
                                    base=0, pattern=[[-1, 128]], channel_multiplier=1).then_inc(pool_const, 1)
            nc.gpsimd.memset(mean_of[:, :], 1.0 / D).then_inc(pool_const, 1)
            nc.gpsimd.memset(eps_col[:, :], LN_EPS).then_inc(pool_const, 1)
            pool.wait_ge(pool_const, 4)
            nc.gpsimd.tensor_copy(identb[:, :], ident[:, :]).then_inc(pool_const, 1)
            nc.gpsimd.tensor_tensor(centre[:, :], ident[:, :], mean_of[:, :], ALU.subtract).then_inc(pool_const, 1)
        POOL_CONST = 6

        W_BANKS = PATCH // 4

        def setup_pe(pe):
            pe.wait_ge(pool_const, POOL_CONST)
            pe.wait_ge(patchw_in, 64)
            wv = w_raw.rearrange("p (r c) -> p c r", c=PATCH)
            for j in range(W_BANKS):
                for k in range(4):
                    last = nc.tensor.transpose(bank[j][0:ROWS, k * 128:(k + 1) * 128], wv[:, 4 * j + k, :], ident[:, :])
                last.then_inc(setup_mm, 1)
            pe.wait_ge(dve_const, SETUP_ROWS)
            nc.tensor.transpose(bank[7][:, 0:65], pos_raw, ident[0:65, 0:65])
            nc.tensor.transpose(bank[7][:, 65:66], clsT_src, ident[0:1, 0:1])
            nc.tensor.transpose(bank[7][:, 66:67], poly_row[:, :], ident[0:1, 0:1])
            pe.wait_ge(attnw_in, 112)
            nc.tensor.transpose(bank[7][:, 68:84], bl_raw, ident[0:HEADS, 0:HEADS])
            pe.wait_ge(ffnb_in, 80)
            nc.tensor.transpose(bank[7][:, 84:100], gate_raw, ident[0:EXPERTS, 0:EXPERTS])
            nc.tensor.transpose(bank[7][:, 100:172], b1_raw, ident[0:ALL_EXPERTS * FB, 0:ALL_EXPERTS * FB])
            nc.tensor.transpose(bank[7][:, 172:174], sb2_raw, ident[0:SHARED, 0:SHARED]).then_inc(setup_mm, 1)
            pe.wait_ge(setup_ev, W_BANKS)
            for j in range(QUADS):
                for k in range(QH):
                    last = nc.tensor.matmul(bank[j][:, k * 96:(k + 1) * 96], wl_sb[:, 4 * j + k, :],
                                            wqkv_sb[:, 4 * j + k, :, :], start=True, stop=True)
                last.then_inc(fold_mm, 1)
            for k in range(QUADS):
                last = nc.tensor.transpose(bank[4][:, k * 128:(k + 1) * 128], wo_sb[:, k * 128:(k + 1) * 128], ident[:, :])
            last.then_inc(fold_mm, 1)
            pe.wait_ge(setup_ev, W_BANKS + 1)
            for c in range(3):
                for h in range(HEADS):
                    q = 32 * (h % QH)
                    last = nc.tensor.matmul(bank[5][q:q + 32, c * QUADS + h // QH:c * QUADS + h // QH + 1],
                                            wqkv_sb[:, h, c, :], blT[:, h:h + 1], start=True, stop=True)
            last.then_inc(fold_mm, 1)
            pe.wait_ge(fold_ev, QUADS + 2)
            for k in range(QUADS):
                last = nc.tensor.matmul(bank[6][:, 0:1], woT[:, k, :], qkv_b[:, 2 * QUADS + k:2 * QUADS + k + 1],
                                        start=(k == 0), stop=(k == QUADS - 1))
            last.then_inc(fold_mm, 1)

        SETUP_ROWS = 15

        def setup_dve_rows(dve):
            dve.wait_ge(tokens_in, 32)
            nc.vector.memset(poly_row[:, 0:1], 1.0).then_inc(dve_const, 1)
            nc.vector.tensor_copy(poly_row[:, 1:2], p_row[:, :]).then_inc(dve_const, 1)
            n, done = 2, 2
            while n < D:
                dve.wait_ge(dve_const, done)
                nc.vector.tensor_tensor(poly_row[:, n:n + 1], poly_row[:, n // 2:n // 2 + 1],
                                        poly_row[:, n // 2:n // 2 + 1], ALU.mult).then_inc(dve_pow, 1)
                dve.wait_ge(dve_pow, done - 1)
                nc.vector.tensor_scalar(poly_row[:, n + 1:2 * n], poly_row[:, 1:n], poly_row[:, n:n + 1], None,
                                        ALU.mult).then_inc(dve_const, 1)
                n, done = 2 * n, done + 1
            dve.wait_ge(patchw_in, 64)
            nc.vector.tensor_tensor(clsT_src, cls_raw, pos_raw[0:1, :], ALU.mult).then_inc(dve_const, 1)
            nc.vector.memset(head_rows[:, :], 0.0).then_inc(dve_const, 1)
            dve.wait_ge(dve_const, done + 2)
            for h in range(QH):
                nc.vector.memset(head_rows[32 * h:32 * h + 32, h:h + 1], 1.0).then_inc(dve_const, 1)
            nc.vector.memset(xT[:, TOKENS:], 0.0).then_inc(dve_const, 1)
            assert done + 3 + QH == SETUP_ROWS, done

        dve_pow = sem("dve_pow")

        def setup_dve(dve):
            for j in range(W_BANKS):
                dve.wait_ge(setup_mm, j + 1)
                nc.vector.tensor_copy(patch_wT[:, 4 * j:4 * j + 4, :],
                                      bank[j][0:ROWS, :].rearrange("p (k d) -> p k d", k=4)).then_inc(setup_ev, 1)
            dve.wait_ge(setup_mm, W_BANKS + 1)
            nc.vector.tensor_copy(blT, bank[7][:, 68:84]).then_inc(setup_ev, 1)
            nc.vector.tensor_copy(posT[:, :], bank[7][:, 0:65]).then_inc(setup_ev, 1)
            nc.vector.tensor_copy(posc[:, :], bank[7][:, 65:67]).then_inc(setup_ev, 1)
            nc.vector.tensor_copy(gate_wT[:, :], bank[7][:, 84:100]).then_inc(setup_ev, 1)
            nc.vector.tensor_copy(b1T[:, :], bank[7][:, 100:172]).then_inc(setup_ev, 1)
            nc.vector.reduce_sum(shared_b2[:, :], bank[7][:, 172:174], AX.X).then_inc(setup_ev, 1)
            dve.wait_ge(setup_ev, SETUP_EV - 1)
            nc.vector.tensor_scalar(shared_b2[:, :], shared_b2[:, :], 1.0 / SHARED, None, ALU.mult).then_inc(setup_ev, 1)
            for j in range(QUADS):
                dve.wait_ge(fold_mm, j + 1)
                nc.vector.tensor_copy(qkv_w[:, :, QH * j:QH * j + QH, :],
                                      bank[j][:, 0:QH * 96].rearrange("p (h c d) -> p c h d", h=QH, c=3)).then_inc(fold_ev, 1)
            dve.wait_ge(fold_mm, QUADS + 1)
            nc.vector.tensor_copy(woT[:, :, :], bank[4][:, :].rearrange("p (k d) -> p k d", k=QUADS)).then_inc(fold_ev, 1)
            dve.wait_ge(fold_mm, QUADS + 2)
            nc.vector.tensor_copy(qkv_b[:, :], bank[5][:, 0:3 * QUADS]).then_inc(fold_ev, 1)
            dve.wait_ge(fold_mm, QUADS + 3)
            nc.vector.tensor_tensor(out_b[:, :], bank[6][:, 0:1], bo_col[:, :], ALU.add).then_inc(fold_ev, 1)
        SETUP_EV = W_BANKS + 7
        FOLD_EV = QUADS + 3

        tok_i = sb("tok_i", [IMAGES, TEXT], I32)
        wk = [0]

        def carve(n, parts=128):
            a = work[0:parts, wk[0]:wk[0] + n]
            wk[0] += n
            return a
        tok_f = carve(TEXT, IMAGES)
        push = carve(TEXT, IMAGES)
        qlen = carve(TEXT, IMAGES)
        pushes = carve(TEXT, IMAGES)
        step = carve(TEXT, IMAGES)
        ones_row = carve(TEXT, IMAGES)
        tree_rows = carve(4 * TEXT, IMAGES).rearrange("p (k t) -> p k t", k=4)
        head_i = carve(TEXT, IMAGES).bitcast(I32)
        par_i = carve(TEXT, IMAGES).bitcast(I32)
        bit_i = carve(TEXT, IMAGES).bitcast(I32)
        tree_rows_b = carve(TEXT, IMAGES).bitcast(BF16).rearrange("p (k t) -> p k t", k=2)
        tree_cols = carve(4 * IMAGES, TEXT).rearrange("p (k b) -> p k b", k=4)
        lr_cols = carve(IMAGES, TEXT).bitcast(BF16).rearrange("p (b k) -> p b k", k=2)
        HALF = 4
        SW = TEXT + 128 + 1
        seq_t = [carve(HALF * SW // 2, TEXT).bitcast(BF16).rearrange("p (b c) -> p b c", c=SW) for _ in range(2)]
        par_t = [carve(HALF * 78 // 2, TEXT).bitcast(BF16).rearrange("p (b c) -> p b c", c=78) for _ in range(2)]
        tree_bc = xT[0:TEXT, 0:IMAGES * TEXT].bitcast(BF16).rearrange("p (k b t) -> p k b t", k=2, t=TEXT)
        tree_dram = nc.dram_tensor("tree_dram", (2, IMAGES, TEXT), BF16, kind="Internal").ap()

        tree_row = sem("tree_row")
        tree_out = sem("tree_out")
        tree_in = sem("tree_in")
        tree_colmm = sem("tree_colmm")
        tree_col = sem("tree_col")
        tree_start = [sem(f"tree_start{u}") for u in range(2)]
        tree_mm = [sem(f"tree_mm{u}") for u in range(2)]
        tree_ev = [sem(f"tree_ev{u}") for u in range(2)]
        tree_pw = [sem(f"tree_pw{u}") for u in range(2)]
        tree_h = [sem(f"tree_h{u}") for u in range(2)]

        def tree_rows_dve(dve):
            n = [0]

            def link(ins):
                n[0] += 1
                ins.then_inc(tree_row, 1)
                dve.wait_ge(tree_row, n[0])
            nc.vector.memset(ones_row, 1.0)
            link(nc.vector.tensor_copy(tok_f, tok_i[:, :]))
            link(nc.vector.tensor_scalar(push, tok_f, float(END_TOKEN), None, ALU.not_equal))
            link(nc.vector.memset(push[:, 0:1], 1.0))
            link(nc.vector.tensor_scalar(step, push, 2.0, -1.0, ALU.mult, ALU.add))
            link(nc.vector.memset(qlen[:, 0:1], 2.0))
            link(nc.vector.tensor_tensor_scan(qlen[:, 1:], step[:, 1:], ones_row[:, 1:], 2.0, ALU.add, ALU.max))
            link(nc.vector.tensor_tensor_scan(pushes, push, push, 0.0, ALU.add, ALU.max))
            link(nc.vector.memset(tree_rows[:, 0:1, :], 0.0))
            link(nc.vector.scalar_tensor_tensor(tree_rows[:, 0, 1:], pushes[:, 0:TEXT - 1], 2.0, qlen[:, 0:TEXT - 1],
                                                ALU.mult, ALU.subtract))
            link(nc.vector.tensor_copy(head_i, tree_rows[:, 0, :]))
            link(nc.vector.tensor_scalar(par_i, head_i, 1, None, ALU.arith_shift_right))
            link(nc.vector.tensor_scalar(bit_i, head_i, 1, None, ALU.bitwise_and))
            link(nc.vector.tensor_copy(tree_rows[:, 0, :], par_i))
            link(nc.vector.tensor_copy(tree_rows[:, 3, :], bit_i))
            link(nc.vector.tensor_scalar(tree_rows[:, 2, :], tree_rows[:, 3, :], -1.0, 1.0, ALU.mult, ALU.add))
            link(nc.vector.memset(tree_rows[:, 0, 0:1], -2.0))
            link(nc.vector.memset(tree_rows[:, 2, 0:1], 0.0))
            link(nc.vector.memset(tree_rows[:, 3, 0:1], 0.0))
            link(nc.vector.tensor_tensor(tree_rows[:, 1, :], push, pushes, ALU.mult))
            link(nc.vector.tensor_scalar(tree_rows[:, 1, :], tree_rows[:, 1, :], -1.0, None, ALU.add))
            link(nc.vector.tensor_copy(tree_rows_b, tree_rows[:, 0:2, :]))
            assert n[0] == TREE_ROW, n[0]
        TREE_ROW = 21

        def tree_sp(sp):
            sp.wait_ge(tree_row, TREE_ROW)
            sp.dma_start(tree_dram.rearrange("k b t -> b k t"), tree_rows_b).then_inc(tree_out, 16)
            sp.wait_ge(tree_out, 16)
            for k in range(2):
                src = tree_dram[k:k + 1, :, :].rearrange("k b t -> k (b t)").to_broadcast([TEXT, IMAGES * TEXT])
                sp.dma_start(xT[0:TEXT, 0:IMAGES * TEXT].bitcast(BF16)[:, k * IMAGES * TEXT:(k + 1) * IMAGES * TEXT],
                             src).then_inc(tree_in, 16)

        def tree_pe(pe):
            pe.wait_ge(pool_const, POOL_CONST)
            pe.wait_ge(tree_row, TREE_ROW)
            for k in range(4):
                last = nc.tensor.transpose(bank[0][0:TEXT, k * IMAGES:(k + 1) * IMAGES], tree_rows[:, k, :],
                                           ident[0:IMAGES, 0:IMAGES])
            last.then_inc(tree_colmm, 1)
            pe.wait_ge(tree_col, 2)
            with pe.Fori(0, IMAGES // (2 * HALF)) as i:
                for lv in range(TREE_LEVELS):
                    w = 2 << lv
                    lo, hi = (0, TEXT + w) if lv < TREE_LEVELS - 1 else (TEXT, TEXT + w)
                    for u in range(2):
                        if lv == 0:
                            pe.wait_ge(tree_start[u], 3 * (i + 1))
                            pe.wait_ge(tree_h[u], i + 1)
                        else:
                            pe.wait_ge(tree_ev[u], i * 11 + 2 * lv)
                            pe.wait_ge(tree_pw[u], i * 5 + lv)
                        for b in range(HALF):
                            last = nc.tensor.matmul(bank[2 * u][0:TEXT, b * (hi - lo):(b + 1) * (hi - lo)],
                                                    par_t[u][:, b, 0:TEXT], seq_t[u][:, b, lo:hi], start=True, stop=True)
                        if lv < TREE_LEVELS - 1:
                            for b in range(HALF):
                                last = nc.tensor.matmul(bank[2 * u + 1][0:TEXT, b * TEXT:(b + 1) * TEXT],
                                                        seq_t[u][:, b, 0:TEXT], par_t[u][:, b, 0:TEXT], start=True, stop=True)
                        last.then_inc(tree_mm[u], 1)
                for u in range(2):
                    pe.wait_ge(tree_ev[u], i * 11 + 11)
                    for b in range(HALF):
                        last = nc.tensor.matmul(bank[2 * u + 1][:, b * TEXT:(b + 1) * TEXT], seq_t[u][:, b, TEXT:TEXT + D],
                                                identb[0:TEXT, 0:TEXT], start=True, stop=True)
                    last.then_inc(tree_mm[u], 1)

        hT_img = hT[:, :].rearrange("p (b s) -> p b s", s=SEQ)

        def tree_dve(dve):
            for u in range(2):
                dve.sem_inc(tree_h[u], 1)
            dve.wait_ge(tree_colmm, 1)
            nc.vector.tensor_copy(tree_cols, bank[0][0:TEXT, 0:4 * IMAGES].rearrange("p (k b) -> p k b", k=4)).then_inc(tree_col, 1)
            dve.wait_ge(tree_col, 1)
            nc.vector.tensor_copy(lr_cols, tree_cols[:, 2:4, :].rearrange("p k b -> p b k")).then_inc(tree_col, 1)
            dve.wait_ge(tree_col, 2)
            dve.wait_ge(tree_in, 32)
            dve.wait_ge(setup_ev, SETUP_EV)
            dve.wait_ge(fold_ev, FOLD_EV)
            with dve.Fori(0, IMAGES // (2 * HALF)) as i:
                for u in range(2):
                    b0 = i * (2 * HALF) + u * HALF
                    nc.vector.tensor_tensor(par_t[u][:, :, 0:TEXT], tree_bc[:, 0, bass.ds(b0, HALF), :],
                                            tree_cols[:, 1, bass.ds(b0, HALF)].unsqueeze(2).to_broadcast([TEXT, HALF, TEXT]),
                                            ALU.is_equal).then_inc(tree_start[u], 1)
                    nc.vector.tensor_tensor(seq_t[u][:, :, 0:TEXT], tree_bc[:, 1, bass.ds(b0, HALF), :],
                                            tree_cols[:, 0, bass.ds(b0, HALF)].unsqueeze(2).to_broadcast([TEXT, HALF, TEXT]),
                                            ALU.is_equal).then_inc(tree_start[u], 1)
                    nc.vector.tensor_copy(seq_t[u][:, :, TEXT:TEXT + 2], lr_cols[:, bass.ds(b0, HALF), :]).then_inc(tree_start[u], 1)
                for lv in range(TREE_LEVELS):
                    w = 2 << lv
                    for u in range(2):
                        dve.wait_ge(tree_mm[u], i * 7 + lv + 1)
                        if lv < TREE_LEVELS - 1:
                            src = bank[2 * u][0:TEXT, 0:HALF * (TEXT + w)].rearrange("p (b c) -> p b c", b=HALF)
                            nc.vector.tensor_copy(seq_t[u][:, :, 0:TEXT], src[:, :, 0:TEXT]).then_inc(tree_ev[u], 1)
                            nc.vector.tensor_copy(seq_t[u][:, :, TEXT + w:TEXT + 2 * w],
                                                  src[:, :, TEXT:TEXT + w]).then_inc(tree_ev[u], 1)
                        else:
                            src = bank[2 * u][0:TEXT, 0:HALF * w].rearrange("p (b c) -> p b c", b=HALF)
                            nc.vector.tensor_copy(seq_t[u][:, :, TEXT + w:TEXT + 2 * w], src).then_inc(tree_ev[u], 1)
                for u in range(2):
                    dve.wait_ge(tree_mm[u], i * 7 + 7)
                    nc.vector.tensor_scalar(hT_img[:, bass.ds(i * (2 * HALF) + u * HALF, HALF), 1 + PATCHES:SEQ],
                                            bank[2 * u + 1][:, 0:HALF * TEXT].rearrange("p (b t) -> p b t", b=HALF),
                                            posc[:, 1:2], None, ALU.mult).then_inc(tree_h[u], 1)

        def tree_act(act):
            with act.Fori(0, IMAGES // (2 * HALF)) as i:
                for lv in range(TREE_LEVELS - 1):
                    for u in range(2):
                        act.wait_ge(tree_mm[u], i * 7 + lv + 1)
                        nc.scalar.copy(par_t[u][:, :, 0:TEXT],
                                       bank[2 * u + 1][0:TEXT, 0:HALF * TEXT].rearrange("p (b t) -> p b t", b=HALF)).then_inc(tree_pw[u], 1)

        CHUNKS = IMAGES // CHUNK_IMAGES
        CP = CHUNK_IMAGES * PATCHES
        x_in = [sem(f"x_in{u}") for u in range(2)]
        patch_mm = [sem(f"patch_mm{u}") for u in range(2)]
        patch_ev = [sem(f"patch_ev{u}") for u in range(2)]
        x_v = x.rearrange("b c (g r) w -> b c r g w", r=PATCH)

        def patch_sp(sp):
            def load(u, b0):
                for b in range(CHUNK_IMAGES):
                    for c in range(CHANNELS):
                        sp.dma_start(x_tile[u][c * PATCH:(c + 1) * PATCH, b * GRID * SIDE:(b + 1) * GRID * SIDE],
                                     x_v[bass.ds(b0 + b, 1), c, :, :, :]).then_inc(x_in[u], 16)
            for u in range(2):
                load(u, u * CHUNK_IMAGES)
            with sp.Fori(1, CHUNKS // 2) as i:
                for u in range(2):
                    sp.wait_ge(patch_mm[u], i)
                    load(u, i * (2 * CHUNK_IMAGES) + u * CHUNK_IMAGES)

        def patch_pe(pe):
            with pe.Fori(0, CHUNKS // 2) as i:
                for u in range(2):
                    pe.wait_ge(x_in[u], (i + 1) * (16 * CHANNELS * CHUNK_IMAGES))
                    pe.wait_ge(patch_ev[u], i + 1)
                    xv = x_tile[u].rearrange("r (n k) -> r k n", k=PATCH)
                    for k in range(PATCH):
                        last = nc.tensor.matmul(bank[4 + u][:, 0:CP], patch_wT[:, k, :], xv[:, k, :],
                                                start=(k == 0), stop=(k == PATCH - 1))
                    last.then_inc(patch_mm[u], 1)

        def patch_dve(dve):
            dve.sem_inc(patch_ev[0], 1)
            dve.sem_inc(patch_ev[1], 1)
            nc.vector.tensor_copy(hT_img[:, :, 0:1].rearrange("p b s -> p (b s)"),
                                  posc[:, 0:1].to_broadcast([D, IMAGES])).then_inc(cls_done, 1)
            with dve.Fori(0, CHUNKS // 2) as i:
                for u in range(2):
                    dve.wait_ge(patch_mm[u], i + 1)
                    nc.vector.scalar_tensor_tensor(
                        hT_img[:, bass.ds(i * (2 * CHUNK_IMAGES) + u * CHUNK_IMAGES, CHUNK_IMAGES), 1:1 + PATCHES],
                        bank[4 + u][:, 0:CP].rearrange("p (b t) -> p b t", b=CHUNK_IMAGES), patch_b[:, :],
                        posT[:, 1:1 + PATCHES].unsqueeze(1).to_broadcast([D, CHUNK_IMAGES, PATCHES]),
                        ALU.add, ALU.mult).then_inc(patch_ev[u], 1)
        cls_done = sem("cls_done")

        LW = 2 * SEQ
        LCHUNKS = TOKENS // LW

        class Norm:
            def __init__(self, name):
                self.centred, self.copied, self.squared, self.var, self.sd, self.rs, self.done = (
                    [sem(f"{name}_{n}{u}") for u in range(2)] for n in ("centred", "copied", "squared", "var", "sd", "rs", "done"))
                self.cx, self.sq, self.sdev, self.rstd = (
                    [work[:, (2 * k + u) * LW:(2 * k + u + 1) * LW] for u in range(2)] for k in range(4))

            def pe(self, pe):
                with pe.Fori(0, LCHUNKS // 2) as i:
                    for u in range(2):
                        pe.wait_ge(self.copied[u], i + 1)
                        nc.tensor.matmul(bank[u][:, 0:LW], centre[:, :], hT[:, bass.ds(i * (2 * LW) + u * LW, LW)],
                                         start=True, stop=True).then_inc(self.centred[u], 1)
                    for u in range(2):
                        pe.wait_ge(self.squared[u], i + 1)
                        pe.wait_ge(self.sd[u], i + 1)
                        nc.tensor.matmul(bank[2 + u][:, 0:LW], mean_of[:, :], self.sq[u], start=True, stop=True).then_inc(self.var[u], 1)

            def act(self, act):
                for u in range(2):
                    act.sem_inc(self.copied[u], 1)
                    act.sem_inc(self.sd[u], 1)
                with act.Fori(0, LCHUNKS // 2) as i:
                    for u in range(2):
                        act.wait_ge(self.centred[u], i + 1)
                        act.wait_ge(self.done[u], i + 1)
                        nc.scalar.copy(self.cx[u], bank[u][:, 0:LW]).then_inc(self.copied[u], 1)
                    for u in range(2):
                        act.wait_ge(self.var[u], i + 1)
                        nc.scalar.activation(self.sdev[u], bank[2 + u][:, 0:LW], ACT.Sqrt, bias=eps_col[:, :]).then_inc(self.sd[u], 1)

            def pool(self, pool):
                with pool.Fori(0, LCHUNKS // 2) as i:
                    for u in range(2):
                        pool.wait_ge(self.copied[u], i + 2)
                        nc.gpsimd.tensor_tensor(self.sq[u], self.cx[u], self.cx[u], ALU.mult).then_inc(self.squared[u], 1)

            def dve(self, dve):
                for u in range(2):
                    dve.sem_inc(self.done[u], 1)
                with dve.Fori(0, LCHUNKS // 2) as i:
                    for u in range(2):
                        dve.wait_ge(self.sd[u], i + 2)
                        nc.vector.reciprocal(self.rstd[u], self.sdev[u]).then_inc(self.rs[u], 1)
                    for u in range(2):
                        dve.wait_ge(self.rs[u], i + 1)
                        nc.vector.tensor_tensor(xT[:, bass.ds(i * (2 * LW) + u * LW, LW)], self.cx[u], self.rstd[u],
                                                ALU.mult).then_inc(self.done[u], 1)

        norm1 = Norm("norm1")
        norm2 = Norm("norm2")

        wk[0] = 0
        xs = [carve(SEQ) for _ in range(2)]
        qk = [carve(8 * SEQ).rearrange("p (k s) -> p k s", k=8) for _ in range(2)]
        v_main = [carve(HEADS * HD) for _ in range(2)]
        v_tail = [carve(HEADS * HD, TAIL) for _ in range(2)]
        nmax = [carve(HEADS) for _ in range(2)]
        rsum = [carve(HEADS) for _ in range(2)]
        rinv = carve(HEADS)
        probs = [carve(QH * MAIN) for _ in range(2)]
        probsT = [carve(QH * MAIN) for _ in range(2)]
        attn = carve(HEADS * HD)
        catT = carve(QUADS * SEQ).rearrange("p (g s) -> p g s", g=QUADS)
        TR = QH * TAIL
        nmax_t = carve(QUADS, TR)
        rsum_t = carve(QUADS, TR)
        rinv_t = carve(QUADS, TR)
        probs_t = carve(QUADS * SEQ, TR).rearrange("p (g s) -> p g s", g=QUADS)
        probsT_a = carve(QUADS * TR).rearrange("p (g r) -> p g r", g=QUADS)
        probsT_b = carve(QUADS * TR, TAIL).rearrange("p (g r) -> p g r", g=QUADS)
        assert wk[0] <= 9600, wk[0]
        QZ_AT = W_ELEMS - 2 * HEADS * SEQ
        qz = [region[:, QZ_AT + u * HEADS * MAIN:QZ_AT + (u + 1) * HEADS * MAIN].rearrange("p (g h s) -> p g h s", g=QUADS, h=QH)
              for u in range(2)]
        QT_AT = QZ_AT + 2 * HEADS * MAIN
        qz_t = [region[:, QT_AT + u * HEADS * TAIL:QT_AT + (u + 1) * HEADS * TAIL].rearrange("p (g h s) -> p g h s", g=QUADS, h=QH)
                for u in range(2)]
        mask_main = sb("mask_main", [128, QH, MAIN], BF16)
        mask_tail = sb("mask_tail", [TR, 2, SEQ], BF16)

        mask_ready, mask_dma = sem("mask_ready"), sem("mask_dma")
        qk_mm, qk_ev, v_mm, v_ev = sem("qk_mm"), sem("qk_ev"), sem("v_mm"), sem("v_ev")
        xs_ready, qz_ready = sem("xs_ready"), sem("qz_ready")
        s_mm, max_done, exp_done, t_mm, t_ev, f_mm, norm_done = (sem(n) for n in (
            "s_mm", "max_done", "exp_done", "t_mm", "t_ev", "f_mm", "norm_done"))
        st_mm, maxt_done, expt_done, normt_done, tt_mm, tt_ev, tf_mm, tf_ev = (sem(n) for n in (
            "st_mm", "maxt_done", "expt_done", "normt_done", "tt_mm", "tt_ev", "tf_mm", "tf_ev"))
        ft_mm, ft_ev, o_mm, resid = sem("ft_mm"), sem("ft_ev"), sem("o_mm"), sem("resid")
        rinv_done, rinvt_done = sem("rinv_done"), sem("rinvt_done")

        passed = sem("passed")

        def settle(eng):
            eng.sem_inc(passed, 1)

        def at(i, u, per, c):
            return i * (2 * per) + (u * per + c)

        def attn_masks_pool(pool):
            nc.gpsimd.memset(mask_main[:, :, :], 0.0).then_inc(mask_ready, 1)
            nc.gpsimd.memset(mask_tail[:, :, :], 0.0).then_inc(mask_ready, 1)
            pool.wait_ge(mask_ready, 2)
            nc.gpsimd.affine_select(out=mask_main[:, :, :], in_=mask_main[:, :, :], compare_op=ALU.is_ge, fill=MASKED,
                                    base=0, pattern=[[0, QH], [-1, MAIN]], channel_multiplier=1).then_inc(mask_ready, 1)
            pool.wait_ge(mask_ready, 3)
            for h in range(QH):
                for k in range(2):
                    pool.dma_start(mask_tail[h * TAIL:(h + 1) * TAIL, k, MAIN:SEQ],
                                   mask_main[0:TAIL, 0, 0:TAIL]).then_inc(mask_dma, 16)
        MASK_DMA = 16 * 2 * QH

        def qk_fill(pe, u, j, b):
            for k in range(3 * j, min(3 * j + 3, 8)):
                c, g = divmod(k, QUADS)
                last = nc.tensor.matmul(b[:, (k - 3 * j) * SEQ:(k - 3 * j + 1) * SEQ],
                                        qkv_w[:, c, QH * g:QH * g + QH, :], xs[u], start=True, stop=True)
            last.then_inc(qk_mm, 1)

        def v_fill(pe, u, part, b):
            lo, n = ((0, MAIN), (MAIN, TAIL))[part]
            nc.tensor.matmul(b[0:n, :], xs[u][:, lo:lo + n], qkv_w[:, 2, :, :], start=True, stop=True).then_inc(v_mm, 1)

        def s_fill(pe, u, g):
            nc.tensor.matmul(bank[g % 2][:, :], identb[:, :], mask_main[:, :, :], start=True, stop=False)
            for h in range(QH):
                last = nc.tensor.matmul(bank[g % 2][:, h * MAIN:(h + 1) * MAIN], qz[u][:, g, h, 0:MAIN],
                                        qk[u][:, QUADS + g, 0:MAIN], start=False, stop=(h == QH - 1))
            last.then_inc(s_mm, 1)

        def attn_pe(pe):
            pe.wait_ge(mask_dma, MASK_DMA)
            pe.wait_ge(fold_ev, FOLD_EV)
            pe.wait_ge(xs_ready, 1)
            qk_fill(pe, 0, 0, bank[5])
            qk_fill(pe, 0, 1, bank[6])
            pe.wait_ge(qk_ev, 1)
            qk_fill(pe, 0, 2, bank[5])
            pe.wait_ge(qk_ev, 2)
            v_fill(pe, 0, 0, bank[6])
            pe.wait_ge(qk_ev, 3)
            v_fill(pe, 0, 1, bank[5])
            pe.wait_ge(qz_ready, 8)
            s_fill(pe, 0, 0)
            s_fill(pe, 0, 1)
            with pe.Fori(0, IMAGES // 2) as i:
                for u in range(2):
                    w = 1 - u

                    def st_fill(p):
                        settle(pe)
                        nc.tensor.matmul(bank[7][0:TR, 0:2 * SEQ], identb[0:TR, 0:TR], mask_tail[:, :, :], start=True, stop=False)
                        for k in range(2):
                            last = nc.tensor.matmul(bank[7][0:TR, k * SEQ:(k + 1) * SEQ], qz_t[u][:, 2 * p + k, :, :],
                                                    qk[u][:, QUADS + 2 * p + k, :], start=False, stop=(k == 1))
                        last.then_inc(st_mm, 1)

                    def t_fill(g):
                        pe.wait_ge(exp_done, at(i, u, 16, 4 * g + 4))
                        pe.wait_ge(t_ev, at(i, u, 4, g - 2 + 4 + 1))
                        for h in range(QH):
                            last = nc.tensor.transpose(bank[2 + g % 2][:, h * MAIN:(h + 1) * MAIN],
                                                       probs[g % 2][:, h * MAIN:(h + 1) * MAIN], ident[:, :])
                        last.then_inc(t_mm, 1)

                    def f_fill(g):
                        pe.wait_ge(t_ev, at(i, u, 4, g + 4 + 1))
                        if g == 0:
                            pe.wait_ge(resid, at(i, u, 1, 1))
                            pe.wait_ge(v_ev, at(i, u, 2, 1))
                        for h in range(QH):
                            c = (QH * g + h) * HD
                            last = nc.tensor.matmul(bank[4][:, c:c + HD], probsT[g % 2][:, h * MAIN:(h + 1) * MAIN],
                                                    v_main[u][:, c:c + HD], start=True, stop=True)
                        last.then_inc(f_mm, 1)

                    def tt_fill(p):
                        settle(pe)
                        for k in range(2):
                            g = 2 * p + k
                            nc.tensor.transpose(bank[6][:, k * TR:(k + 1) * TR], probs_t[:, g, 0:MAIN], ident[0:TR, 0:TR])
                            last = nc.tensor.transpose(bank[6][0:TAIL, (2 + k) * TR:(3 + k) * TR], probs_t[:, g, MAIN:SEQ],
                                                       ident[0:TR, 0:TR])
                        last.then_inc(tt_mm, 1)

                    pe.wait_ge(expt_done, at(i, u, 4, 4))
                    st_fill(0)
                    pe.wait_ge(xs_ready, at(i, u, 1, 2))
                    pe.wait_ge(v_ev, at(i, u, 2, 2))
                    pe.wait_ge(tf_ev, at(i, u, 4, 4))
                    qk_fill(pe, w, 0, bank[5])
                    pe.wait_ge(tt_ev, at(i, u, 4, 4))
                    qk_fill(pe, w, 1, bank[6])
                    t_fill(0)
                    s_fill(pe, u, 2)
                    f_fill(0)
                    pe.wait_ge(qk_ev, at(i, u, 3, 4))
                    qk_fill(pe, w, 2, bank[5])
                    pe.wait_ge(qk_ev, at(i, u, 3, 5))
                    v_fill(pe, w, 0, bank[6])
                    t_fill(1)
                    s_fill(pe, u, 3)
                    pe.wait_ge(expt_done, at(i, u, 4, 2 + 4))
                    st_fill(1)
                    f_fill(1)
                    pe.wait_ge(qk_ev, at(i, u, 3, 6))
                    v_fill(pe, w, 1, bank[5])
                    t_fill(2)
                    pe.wait_ge(normt_done, at(i, u, 2, 1))
                    pe.wait_ge(v_ev, at(i, u, 2, 3))
                    tt_fill(0)
                    f_fill(2)
                    t_fill(3)
                    pe.wait_ge(normt_done, at(i, u, 2, 2))
                    pe.wait_ge(tt_ev, at(i, u, 4, 2 + 4))
                    tt_fill(1)
                    f_fill(3)
                    pe.wait_ge(qz_ready, at(i, u, 8, 16))
                    s_fill(pe, w, 0)
                    pe.wait_ge(norm_done, at(i, u, 1, 2))
                    for g in range(QUADS):
                        last = nc.tensor.transpose(bank[4][:, g * 128:(g + 1) * 128], attn[:, g * 128:(g + 1) * 128], ident[:, :])
                    last.then_inc(ft_mm, 1)
                    pe.wait_ge(v_ev, at(i, u, 2, 4))
                    pe.wait_ge(tt_ev, at(i, u, 4, 4 + 4))
                    for g in range(QUADS):
                        nc.tensor.matmul(bank[5][:, g * TR:(g + 1) * TR], v_main[u][:, g * 128:(g + 1) * 128], probsT_a[:, g, :],
                                         start=True, stop=False)
                        last = nc.tensor.matmul(bank[5][:, g * TR:(g + 1) * TR], v_tail[u][:, g * 128:(g + 1) * 128],
                                                probsT_b[:, g, :], start=False, stop=True)
                    last.then_inc(tf_mm, 1)
                    s_fill(pe, w, 1)
                    pe.wait_ge(ft_ev, at(i, u, 1, 1))
                    pe.wait_ge(tf_ev, at(i, u, 4, 8))
                    for g in range(QUADS):
                        last = nc.tensor.matmul(bank[4][:, 0:SEQ], woT[:, g, :], catT[:, g, :], start=(g == 0), stop=(g == QUADS - 1))
                    last.then_inc(o_mm, 1)

        def attn_pool(pool):
            def stage(u, at_col):
                nc.gpsimd.tensor_copy(xs[u], xT[:, at_col]).then_inc(xs_ready, 1)

            def spread(u):
                for h in range(QH):
                    nc.gpsimd.tensor_scalar(qz[u][:, :, h, :], qk[u][:, 0:QUADS, 0:MAIN], head_rows[:, h:h + 1], 0.0, ALU.mult, ALU.add).then_inc(qz_ready, 1)
                    nc.gpsimd.tensor_scalar(qz_t[u][:, :, h, :], qk[u][:, 0:QUADS, MAIN:SEQ], head_rows[:, h:h + 1], 0.0, ALU.mult, ALU.add).then_inc(qz_ready, 1)
            for u in range(2):
                pool.wait_ge(norm1.done[u], LCHUNKS // 2 + 1)
            stage(0, slice(0, SEQ))
            stage(1, slice(SEQ, 2 * SEQ))
            pool.wait_ge(dve_const, SETUP_ROWS)
            pool.wait_ge(qk_ev, 3)
            spread(0)
            with pool.Fori(0, IMAGES // 2) as i:
                for u in range(2):
                    pool.wait_ge(v_mm, at(i, u, 2, 2))
                    settle(pool)
                    stage(u, bass.ds(i * (2 * SEQ) + (u + 2) * SEQ, SEQ))
                    pool.wait_ge(qk_ev, at(i, u, 3, 5))
                    settle(pool)
                    spread(1 - u)

        def attn_act(act):
            def v_evac(u, part, b):
                n = (MAIN, TAIL)[part]
                nc.scalar.copy((v_main, v_tail)[part][u][0:n, :], b[0:n, :]).then_inc(v_ev, 1)
            act.wait_ge(v_mm, 1)
            v_evac(0, 0, bank[6])
            act.wait_ge(v_mm, 2)
            v_evac(0, 1, bank[5])
            with act.Fori(0, IMAGES // 2) as i:
                for u in range(2):
                    def exps(g):
                        act.wait_ge(max_done, at(i, u, 4, g + 1))
                        act.wait_ge(t_mm, at(i, u, 4, g - 2 + 4 + 1))
                        for h in range(QH):
                            n = QH * g + h
                            nc.scalar.activation(probs[g % 2][:, h * MAIN:(h + 1) * MAIN], bank[g % 2][:, h * MAIN:(h + 1) * MAIN],
                                                 ACT.Exp, bias=nmax[u][:, n:n + 1], accum_out=rsum[u][:, n:n + 1]).then_inc(exp_done, 1)

                    def tail_exps(p):
                        act.wait_ge(maxt_done, at(i, u, 2, p + 1))
                        act.wait_ge(tt_mm, at(i, u, 2, p + 1))
                        for k in range(2):
                            g = 2 * p + k
                            nc.scalar.activation(probs_t[:, g, :], bank[7][0:TR, k * SEQ:(k + 1) * SEQ], ACT.Exp,
                                                 bias=nmax_t[:, g:g + 1], accum_out=rsum_t[:, g:g + 1]).then_inc(expt_done, 1)
                    exps(0)
                    exps(1)
                    tail_exps(0)
                    act.wait_ge(v_mm, at(i, u, 2, 3))
                    v_evac(1 - u, 0, bank[6])
                    exps(2)
                    exps(3)
                    tail_exps(1)
                    act.wait_ge(v_mm, at(i, u, 2, 4))
                    v_evac(1 - u, 1, bank[5])
                    act.wait_ge(ft_mm, at(i, u, 1, 1))
                    act.wait_ge(o_mm, at(i, u, 1, 1))
                    nc.scalar.copy(catT[:, :, 0:MAIN], bank[4][:, :].rearrange("p (g s) -> p g s", g=QUADS)).then_inc(ft_ev, 1)

        def attn_dve(dve):
            dve.sem_inc(t_ev, 4)
            dve.sem_inc(t_mm, 4)
            dve.sem_inc(tt_mm, 2)
            dve.sem_inc(expt_done, 4)
            dve.sem_inc(f_mm, 4)
            dve.sem_inc(tf_mm, 1)
            dve.sem_inc(tt_ev, 4)
            dve.sem_inc(tf_ev, 4)
            dve.sem_inc(norm_done, 1)
            dve.sem_inc(resid, 1)
            dve.sem_inc(o_mm, 1)

            def qk_evac(u, j, b):
                n = min(3, 8 - 3 * j)
                nc.vector.tensor_tensor(qk[u][:, 3 * j:3 * j + n, :], b[:, 0:n * SEQ].rearrange("p (k s) -> p k s", k=n),
                                        qkv_b[:, 3 * j:3 * j + n].unsqueeze(2).to_broadcast([128, n, SEQ]),
                                        ALU.add).then_inc(qk_ev, 1)
            for j in range(3):
                dve.wait_ge(qk_mm, j + 1)
                qk_evac(0, j, bank[5 + j % 2])

            def maxes_into(u, g):
                nc.vector.tensor_reduce(nmax[u][:, QH * g:QH * g + QH], bank[g % 2][:, :].rearrange("p (h s) -> p h s", h=QH),
                                        AX.X, ALU.max, negate=True).then_inc(max_done, 1)
            for g in range(2):
                dve.wait_ge(s_mm, g + 1)
                maxes_into(0, g)
            with dve.Fori(0, IMAGES // 2) as i:
                for u in range(2):
                    def maxes(g):
                        dve.wait_ge(s_mm, at(i, u, 4, g + 1))
                        maxes_into(u if g < QUADS else 1 - u, g % QUADS)

                    def tail_maxes(p):
                        dve.wait_ge(st_mm, at(i, u, 2, p + 1))
                        nc.vector.tensor_reduce(nmax_t[:, 2 * p:2 * p + 2], bank[7][0:TR, 0:2 * SEQ].rearrange("p (k s) -> p k s", k=2),
                                                AX.X, ALU.max, negate=True).then_inc(maxt_done, 1)

                    def tail_inv(p):
                        dve.wait_ge(expt_done, at(i, u, 4, 2 * p + 2 + 4))
                        nc.vector.reciprocal(rinv_t[:, 2 * p:2 * p + 2], rsum_t[:, 2 * p:2 * p + 2]).then_inc(rinvt_done, 1)

                    def tail_norm(p):
                        dve.wait_ge(rinvt_done, at(i, u, 2, p + 1))
                        t = probs_t[:, 2 * p:2 * p + 2, :]
                        nc.vector.tensor_tensor(t, t, rinv_t[:, 2 * p:2 * p + 2].unsqueeze(2).to_broadcast([TR, 2, SEQ]),
                                                ALU.mult).then_inc(normt_done, 1)

                    def t_evac(g):
                        dve.wait_ge(t_mm, at(i, u, 4, g + 1 + 4))
                        dve.wait_ge(f_mm, at(i, u, 4, g - 2 + 4 + 1))
                        nc.vector.tensor_copy(probsT[g % 2], bank[2 + g % 2][:, :]).then_inc(t_ev, 1)

                    def tt_evac(p):
                        dve.wait_ge(tt_mm, at(i, u, 2, p + 1 + 2))
                        if p == 0:
                            dve.wait_ge(tf_mm, at(i, u, 1, 1))
                        nc.vector.tensor_copy(probsT_a[:, 2 * p:2 * p + 2, :],
                                              bank[6][:, 0:2 * TR].rearrange("p (k r) -> p k r", k=2)).then_inc(tt_ev, 1)
                        nc.vector.tensor_copy(probsT_b[:, 2 * p:2 * p + 2, :],
                                              bank[6][0:TAIL, 2 * TR:4 * TR].rearrange("p (k r) -> p k r", k=2)).then_inc(tt_ev, 1)
                    tail_maxes(0)
                    dve.wait_ge(qk_mm, at(i, u, 3, 4))
                    qk_evac(1 - u, 0, bank[5])
                    dve.wait_ge(qk_mm, at(i, u, 3, 5))
                    qk_evac(1 - u, 1, bank[6])
                    tail_inv(0)
                    t_evac(0)
                    maxes(2)
                    tail_norm(0)
                    dve.wait_ge(qk_mm, at(i, u, 3, 6))
                    qk_evac(1 - u, 2, bank[5])
                    t_evac(1)
                    maxes(3)
                    tail_maxes(1)
                    t_evac(2)
                    tail_inv(1)
                    tt_evac(0)
                    tail_norm(1)
                    t_evac(3)
                    tt_evac(1)
                    dve.wait_ge(exp_done, at(i, u, 16, 16))
                    nc.vector.reciprocal(rinv, rsum[u]).then_inc(rinv_done, 1)
                    dve.wait_ge(rinv_done, at(i, u, 1, 1))
                    dve.wait_ge(f_mm, at(i, u, 4, 4 + 4))
                    nc.vector.tensor_tensor(attn.rearrange("p (h d) -> p h d", d=HD), bank[4][:, :].rearrange("p (h d) -> p h d", d=HD),
                                            rinv.unsqueeze(2).to_broadcast([MAIN, HEADS, HD]), ALU.mult).then_inc(norm_done, 1)
                    maxes(4)
                    dve.wait_ge(tf_mm, at(i, u, 1, 1 + 1))
                    for h in range(QH):
                        nc.vector.tensor_copy(catT[32 * h:32 * h + 32, :, MAIN:SEQ],
                                              bank[5][32 * h:32 * h + 32, 0:QUADS * TR].rearrange("p (g h s) -> p g h s", g=QUADS, h=QH)[:, :, h, :]
                                              ).then_inc(tf_ev, 1)
                    maxes(5)
                    dve.wait_ge(o_mm, at(i, u, 1, 1 + 1))
                    here = hT[:, bass.ds(i * (2 * SEQ) + u * SEQ, SEQ)]
                    nc.vector.scalar_tensor_tensor(here, bank[4][:, 0:SEQ], out_b[:, :], here, ALU.add, ALU.add).then_inc(resid, 1)

        w1_sb = region[:, 0:ALL_EXPERTS * HIDDEN].rearrange("p (e f) -> p e f", e=ALL_EXPERTS)
        w2_sb = region[:, ALL_EXPERTS * HIDDEN:W_ELEMS].rearrange("p (e k h) -> p e k h", e=ALL_EXPERTS, k=FB)
        ffnw_in = sem("ffnw_in")

        LATE = (QZ_AT - ALL_EXPERTS * HIDDEN) // HIDDEN

        def experts_sp(sp):
            for u in range(2):
                sp.wait_ge(patch_mm[u], CHUNKS // 2)
            sp.wait_ge(fold_mm, QUADS + 3)

            def w2_of(e):
                return (re_w2[e, :, :] if e < EXPERTS else se_w2[e - EXPERTS, :, :]).rearrange("(k p) h -> p k h", p=128)
            for e in range(ALL_EXPERTS):
                w1 = re_w1[e, :, :] if e < EXPERTS else se_w1[e - EXPERTS, :, :]
                sp.dma_start(w1_sb[:, e, :], w1).then_inc(ffnw_in, 16)
            for e in range(LATE):
                sp.dma_start(w2_sb[:, e, :, :], w2_of(e)).then_inc(ffnw_in, 16)
            sp.wait_ge(o_mm, IMAGES + 1)
            for e in range(LATE, ALL_EXPERTS):
                sp.dma_start(w2_sb[:, e, :, :], w2_of(e)).then_inc(ffnw_in, 16)
            for j in range(CGROUPS):
                sp.wait_ge(comb_ev, j + 1)
                m = min(CT, TILES - j * CT) * 128
                sp.dma_start(comb_dram[:, j * CT * 128:j * CT * 128 + m], combT[j % 2][:, 0:m]).then_inc(comb_out[j % 2], 16)
            for u in range(2):
                sp.wait_ge(comb_out[u], 16 * (-(-(CGROUPS - u) // 2)))
            with sp.Fori(0, LCHUNKS) as i:
                sp.wait_ge(o_mul, i * EXPERTS + 1)
                sp.dma_start(comb_chunk, comb_dram[:, bass.ds(i * LW, LW)]).then_inc(spread_in, 16)
                for e in range(EXPERTS):
                    sp.dma_start(spread_c[:, e, :], comb_dram[e:e + 1, bass.ds(i * LW, LW)].to_broadcast([128, LW])).then_inc(spread_in, 16)
        FFNW_IN = 32 * ALL_EXPERTS

        TE = TILES * EXPERTS
        wk[0] = 8 * LW
        logits = carve(TE).rearrange("p (t e) -> p t e", e=EXPERTS)
        combine = carve(TE).rearrange("p (t e) -> p t e", e=EXPERTS)
        hit = carve(TE).rearrange("p (t e) -> p t e", e=EXPERTS)
        top_v = carve(TILES * 8).rearrange("p (t k) -> p t k", k=8)
        top_i = carve(TILES * 8).rearrange("p (t k) -> p t k", k=8).bitcast(U32)
        top_w = carve(TILES * TOPK).rearrange("p (t k) -> p t k", k=TOPK)
        top_f = carve(TILES * TOPK).rearrange("p (t k) -> p t k", k=TOPK)
        row1 = carve(TILES)
        row2 = carve(TILES)
        e_iota = carve(EXPERTS)
        assert wk[0] <= 9600, wk[0]
        combT = [work[0:EXPERTS, u * 512:(u + 1) * 512] for u in range(2)]
        comb_dram = nc.dram_tensor("comb_dram", (EXPERTS, TOKENS), F32, kind="Internal").ap()
        spread_in = sem("spread_in")
        comb_out = [sem(f"comb_out{u}") for u in range(2)]

        gate_mm, gate_ev, gate_v, gate_e, sel_ready, comb_mm, comb_ev = (sem(n) for n in (
            "gate_mm", "gate_ev", "gate_v", "gate_e", "sel_ready", "comb_mm", "comb_ev"))
        GB = 512 // EXPERTS
        GBANKS = -(-TILES // GB)
        CT = 4
        CGROUPS = -(-TILES // CT)

        def gate_pe(pe):
            for u in range(2):
                pe.wait_ge(norm2.done[u], LCHUNKS // 2 + 1)
            for j in range(GBANKS):
                for t in range(j * GB, min((j + 1) * GB, TILES)):
                    last = nc.tensor.matmul(bank[4 + j][:, (t - j * GB) * EXPERTS:(t - j * GB + 1) * EXPERTS],
                                            xT[:, t * 128:(t + 1) * 128], gate_wT[:, :], start=True, stop=True)
                last.then_inc(gate_mm, 1)
            pe.wait_ge(gate_v, GATE_V)
            for j in range(CGROUPS):
                if j >= 2:
                    pe.wait_ge(comb_ev, j - 1)
                for t in range(j * CT, min((j + 1) * CT, TILES)):
                    last = nc.tensor.transpose(bank[j % 2][0:EXPERTS, (t - j * CT) * 128:(t - j * CT + 1) * 128],
                                               combine[:, t, :], ident[:, :])
                last.then_inc(comb_mm, 1)

        GATE_V = 9 + 2 * TILES + 2 + 4 * 3 + 1

        def gate_pool(pool):
            nc.gpsimd.iota(e_iota, pattern=[[1, EXPERTS]], base=0, channel_multiplier=0,
                           allow_small_or_imprecise_dtypes=True).then_inc(sel_ready, 1)

        def gate_dve(dve):
            n = [0]

            def link(ins):
                n[0] += 1
                ins.then_inc(gate_v, 1)
                dve.wait_ge(gate_v, n[0])
            for j in range(GBANKS):
                dve.wait_ge(gate_mm, j + 1)
                m = min(GB, TILES - j * GB)
                link(nc.vector.tensor_copy(logits[:, j * GB:j * GB + m, :],
                                           bank[4 + j][:, 0:m * EXPERTS].rearrange("p (t e) -> p t e", e=EXPERTS)))
            bc = [128, TILES, EXPERTS]
            link(nc.vector.tensor_reduce(row1, logits, AX.X, ALU.max))
            link(nc.vector.tensor_tensor(logits, logits, row1.unsqueeze(2).to_broadcast(bc), ALU.subtract))
            dve.wait_ge(gate_e, 1)
            link(nc.vector.tensor_reduce(row1, logits, AX.X, ALU.add))
            link(nc.vector.reciprocal(row2, row1))
            link(nc.vector.tensor_tensor(logits, logits, row2.unsqueeze(2).to_broadcast(bc), ALU.mult))
            for t in range(TILES):
                n[0] += 1
                nc.vector.max(top_v[:, t, :], logits[:, t, :]).then_inc(gate_v, 1)
            dve.wait_ge(gate_v, n[0])
            for t in range(TILES):
                n[0] += 1
                nc.vector.max_index(top_i[:, t, :], top_v[:, t, :], logits[:, t, :]).then_inc(gate_v, 1)
            dve.wait_ge(gate_v, n[0])
            link(nc.vector.tensor_tensor(top_w, top_v[:, :, 0:TOPK], top_v[:, :, 0:1].to_broadcast([128, TILES, TOPK]), ALU.subtract))
            dve.wait_ge(gate_e, 2)
            link(nc.vector.tensor_reduce(row1, top_w, AX.X, ALU.add))
            link(nc.vector.reciprocal(row2, row1))
            n[0] += 1
            nc.vector.tensor_tensor(top_w, top_w, row2.unsqueeze(2).to_broadcast([128, TILES, TOPK]), ALU.mult).then_inc(gate_v, 1)
            link(nc.vector.tensor_copy(top_f, top_i[:, :, 0:TOPK]))
            dve.wait_ge(sel_ready, 1)
            for k in range(TOPK):
                link(nc.vector.tensor_tensor(hit, top_f[:, :, k:k + 1].to_broadcast(bc), e_iota.unsqueeze(1).to_broadcast(bc), ALU.is_equal))
                tgt = combine if k == 0 else hit
                link(nc.vector.tensor_tensor(tgt, hit, top_w[:, :, k:k + 1].to_broadcast(bc), ALU.mult))
                if k:
                    link(nc.vector.tensor_tensor(combine, combine, hit, ALU.add))

        def gate_act(act):
            act.wait_ge(gate_v, GBANKS + 2)
            nc.scalar.activation(logits, logits, ACT.Exp).then_inc(gate_e, 1)
            act.wait_ge(gate_v, GBANKS + 5 + 2 * TILES + 1)
            nc.scalar.activation(top_w, top_w, ACT.Exp).then_inc(gate_e, 1)
            for j in range(CGROUPS):
                act.wait_ge(comb_mm, j + 1)
                m = min(CT, TILES - j * CT) * 128
                if j >= 2:
                    act.wait_ge(comb_out[j % 2], 16 * (j // 2))
                nc.scalar.copy(combT[j % 2][:, 0:m], bank[j % 2][0:EXPERTS, 0:m]).then_inc(comb_ev, 1)
        GATE_V = GBANKS + 5 + 2 * TILES + 1 + 2 + 2 + 2 + 3 * 3

        wk[0] = 0
        spread_c = carve(EXPERTS * LW).rearrange("p (e s) -> p e s", e=EXPERTS)
        act_h = [carve(FB * LW).rearrange("p (k s) -> p k s", k=FB) for _ in range(2)]
        scaled = [carve(LW) for _ in range(2)]
        comb_chunk = carve(LW, EXPERTS)
        h_mm, h_act, o_done, o_ev, o_mul, b_mm, b_ev = (sem(n) for n in (
            "h_mm", "h_act", "o_done", "o_ev", "o_mul", "b_mm", "b_ev"))
        NE = ALL_EXPERTS
        OUTS = EXPERTS + 1

        def ffn_pe(pe):
            pe.wait_ge(ffnw_in, FFNW_IN)
            pe.wait_ge(comb_ev, CGROUPS)
            with pe.Fori(0, LCHUNKS) as i:
                here = bass.ds(i * LW, LW)

                def hidden(e):
                    for k in range(FB):
                        pe.wait_ge(h_act, i * (NE * FB) + (e - 1) * FB + k + 1 + FB)
                        nc.tensor.matmul(bank[k][:, 0:LW], w1_sb[:, e, k * 128:(k + 1) * 128], xT[:, here],
                                         start=True, stop=True).then_inc(h_mm, 1)
                hidden(0)
                pe.wait_ge(spread_in, (i + 1) * (16 * EXPERTS + 16))
                pe.wait_ge(b_ev, i + 1)
                nc.tensor.matmul(bank[6][:, 0:LW], b2_rows[:, :], comb_chunk, start=True, stop=True).then_inc(b_mm, 1)
                for e in range(NE):
                    if e < NE - 1:
                        hidden(e + 1)
                    n = min(e, EXPERTS)
                    if e <= EXPERTS:
                        pe.wait_ge(o_ev, i * OUTS + (n + 1 if n else 2))
                    for k in range(FB):
                        pe.wait_ge(h_act, i * (NE * FB) + e * FB + k + 1 + FB)
                        last = nc.tensor.matmul(bank[4 + n % 2][:, 0:LW], w2_sb[:, e, k, :], act_h[e % 2][:, k, :],
                                                start=(k == 0 and e <= EXPERTS), stop=(k == FB - 1 and e != EXPERTS))
                    last.then_inc(o_done, 1)

        def ffn_act(act):
            act.sem_inc(h_act, FB)
            with act.Fori(0, LCHUNKS) as i:
                for e in range(NE):
                    for k in range(FB):
                        act.wait_ge(h_mm, i * (NE * FB) + e * FB + k + 1)
                        if k == 0:
                            act.wait_ge(o_done, i * NE + e - 2 + 1 + 2)
                        nc.scalar.activation(act_h[e % 2][:, k, :], bank[k][:, 0:LW], ACT.Gelu,
                                             bias=b1T[:, e * FB + k:e * FB + k + 1]).then_inc(h_act, 1)

        def ffn_dve(dve):
            dve.sem_inc(o_done, 2)
            dve.sem_inc(o_ev, 2)
            dve.sem_inc(o_mul, 1)
            dve.sem_inc(b_ev, 1)
            with dve.Fori(0, LCHUNKS) as i:
                here = hT[:, bass.ds(i * LW, LW)]
                dve.wait_ge(b_mm, i + 1)
                dve.wait_ge(o_ev, i * OUTS + 2)
                nc.vector.scalar_tensor_tensor(here, bank[6][:, 0:LW], shared_b2[:, :], here, ALU.add, ALU.add).then_inc(b_ev, 1)
                dve.wait_ge(spread_in, (i + 1) * (16 * EXPERTS + 16))
                for e in range(EXPERTS):
                    dve.wait_ge(o_done, i * NE + e + 1 + 2)
                    nc.vector.tensor_tensor(scaled[e % 2], bank[4 + e % 2][:, 0:LW], spread_c[:, e, :], ALU.mult).then_inc(o_mul, 1)
                    dve.wait_ge(o_mul, i * EXPERTS + e + 1 + 1)
                    if e == 0:
                        dve.wait_ge(b_ev, i + 2)
                    else:
                        dve.wait_ge(o_ev, i * OUTS + e + 2)
                    nc.vector.tensor_tensor(here, here, scaled[e % 2], ALU.add).then_inc(o_ev, 1)
                dve.wait_ge(o_done, i * NE + NE + 2)
                dve.wait_ge(o_ev, i * OUTS + EXPERTS + 2)
                nc.vector.scalar_tensor_tensor(here, bank[4][:, 0:LW], 1.0 / SHARED, here, ALU.mult, ALU.add).then_inc(o_ev, 1)

        out_rows = out.rearrange("b s d -> (b s) d")
        OR = 4
        obuf = [work[:, 7500 + r * CT * 128:7500 + (r + 1) * CT * 128] for r in range(OR)]
        y_mm, y_ev = sem("y_mm"), sem("y_ev")
        y_out = [sem(f"y_out{r}") for r in range(OR)]

        def out_pe(pe, ready, value):
            pe.wait_ge(ready, value)
            for j in range(CGROUPS):
                if j >= 2:
                    pe.wait_ge(y_ev, j - 1)
                for t in range(j * CT, min((j + 1) * CT, TILES)):
                    last = nc.tensor.transpose(bank[j % 2][:, (t - j * CT) * 128:(t - j * CT + 1) * 128],
                                               hT[:, t * 128:(t + 1) * 128], ident[:, :])
                last.then_inc(y_mm, 1)

        def out_dve(dve):
            for j in range(CGROUPS):
                dve.wait_ge(y_mm, j + 1)
                if j >= OR:
                    dve.wait_ge(y_out[j % OR], 16 * (j // OR))
                m = min(CT, TILES - j * CT) * 128
                nc.vector.tensor_copy(obuf[j % OR][:, 0:m], bank[j % 2][:, 0:m]).then_inc(y_ev, 1)

        def out_sp(sp):
            for j in range(CGROUPS):
                sp.wait_ge(y_ev, j + 1)
                m = min(CT, TILES - j * CT)
                sp.dma_start(out_rows[j * CT * 128:(j * CT + m) * 128, :].rearrange("(k p) d -> p k d", p=128),
                             obuf[j % OR][:, 0:m * 128].rearrange("p (k d) -> p k d", k=m)).then_inc(y_out[j % OR], 16)
            for r in range(OR):
                sp.wait_ge(y_out[r], 16 * (-(-(CGROUPS - r) // OR)))

        block = ctx.enter_context(nc.Block())

        @block.sync
        def _(sp):
            setup_loads(sp)
            tree_sp(sp)
            patch_sp(sp)
            experts_sp(sp)
            out_sp(sp)

        @block.gpsimd
        def _(pool):
            setup_pool(pool)
            attn_masks_pool(pool)
            norm1.pool(pool)
            attn_pool(pool)
            norm2.pool(pool)
            pool.wait_ge(resid, IMAGES + 1)
            gate_pool(pool)

        @block.scalar
        def _(act):
            tree_act(act)
            norm1.act(act)
            attn_act(act)
            norm2.act(act)
            gate_act(act)
            ffn_act(act)

        @block.vector
        def _(dve):
            setup_dve_rows(dve)
            tree_rows_dve(dve)
            setup_dve(dve)
            tree_dve(dve)
            patch_dve(dve)
            dve.wait_ge(cls_done, 1)
            norm1.dve(dve)
            attn_dve(dve)
            norm2.dve(dve)
            gate_dve(dve)
            ffn_dve(dve)
            out_dve(dve)

        @block.tensor
        def _(pe):
            setup_pe(pe)
            tree_pe(pe)
            patch_pe(pe)
            for u in range(2):
                pe.wait_ge(tree_h[u], IMAGES // (2 * HALF) + 1)
                pe.wait_ge(patch_ev[u], CHUNKS // 2 + 1)
            pe.wait_ge(cls_done, 1)
            norm1.pe(pe)
            attn_pe(pe)
            pe.wait_ge(resid, IMAGES + 1)
            norm2.pe(pe)
            gate_pe(pe)
            ffn_pe(pe)
            out_pe(pe, o_ev, OUTS * LCHUNKS + 2)


_INS = ['x', 'x_txt', 'L0_tok_W', 'L0_tok_b', 'L0_tok_class_token', 'L0_tok_pos_embed', 'L0_txt_p', 'L0_attn_Wl',
        'L0_attn_bl', 'L0_attn_Wq', 'L0_attn_Wk', 'L0_attn_Wv', 'L0_attn_Wo', 'L0_attn_bo', 'L0_ffn_gate_w',
        'L0_ffn_re_w1', 'L0_ffn_re_b1', 'L0_ffn_re_w2', 'L0_ffn_re_b2', 'L0_ffn_se_w1', 'L0_ffn_se_b1',
        'L0_ffn_se_w2', 'L0_ffn_se_b2']


def kernel(**inputs):
    import numpy as _np
    import concourse.bacc as _bacc
    from concourse import mybir as _mybir
    from concourse.bass_utils import run_bass_kernel_spmd as _run

    nc = _bacc.Bacc("TRN2", target_bir_lowering=False, num_devices=1)
    arrays, args = {}, []
    for name in _INS:
        a = _np.ascontiguousarray(inputs[name])
        arrays[f"in_{name}_dram"] = a
        args.append(nc.dram_tensor(f"in_{name}_dram", a.shape, _mybir.dt.from_np(a.dtype), kind="ExternalInput").ap())
    args.append(nc.dram_tensor("out_0_dram", (IMAGES, SEQ, D), _mybir.dt.float32, kind="ExternalOutput").ap())
    build(nc, *args)
    r = _run(nc, [arrays], core_ids=[0])
    return r.results[0]["out_0_dram"]
```

```python
import concourse.bass as bass
from concourse import mybir
from contextlib import ExitStack

F32 = mybir.dt.float32
BF16 = mybir.dt.bfloat16
I32 = mybir.dt.int32
U32 = mybir.dt.uint32
ALU = mybir.AluOpType
ACT = mybir.ActivationFunctionType
AX = mybir.AxisListType

IMAGES, CHANNELS, SIDE = 64, 3, 224
GRID, PATCH = 8, 28
D = 128
PATCHES = GRID * GRID
TEXT = 77
SEQ = 1 + PATCHES + TEXT
TOKENS = IMAGES * SEQ
ROWS = CHANNELS * PATCH
END_TOKEN = 2
HEADS, HD = 16, 32
QUADS, QH = 4, 4
MAIN = 128
TAIL = SEQ - MAIN
EXPERTS, SHARED, HIDDEN, TOPK = 16, 2, 512, 4
ALL_EXPERTS = EXPERTS + SHARED
FB = HIDDEN // 128
TILES = TOKENS // 128
PASS = 2 * 128
PASSES = -(-TOKENS // PASS)
PADDED = PASSES * PASS
DISPATCHED = PADDED // 128
STEPS = 6
SLOT_TILES = -(-(TOKENS * TOPK // 128 + EXPERTS) // STEPS) * STEPS
FILL_TILES = SLOT_TILES + 4
FILLS = 16
SLOTS = FILL_TILES * 128
ASSIGNED = PADDED * TOPK
ROW = D + 1
MASKED = -1e30
LN_EPS = 1e-5
TREE_LEVELS = 6


def build(nc, x, x_txt, tok_W, tok_b, tok_cls, tok_pos, txt_p, Wl, bl, Wq, Wk, Wv, Wo, bo,
          gate_w, re_w1, re_b1, re_w2, re_b2, se_w1, se_b1, se_w2, se_b2, out):
    ctx = ExitStack()
    with ctx:
        def sb(name, shape, dt=F32):
            return ctx.enter_context(nc.sbuf_tensor(name, shape, dt))

        def sem(name):
            return ctx.enter_context(nc.semaphore(name))

        bank = [ctx.enter_context(nc.psum_tensor(f"bank{i}", [128, 512], F32)) for i in range(8)]

        hT = sb("hT", [D, PADDED])
        xT = sb("xT", [D, TOKENS + 2 * SEQ])
        EW = 2 * HIDDEN + FB
        W_ELEMS = ALL_EXPERTS * EW
        patch_wT = xT[0:ROWS, 5000:5000 + PATCH * D].rearrange("r (k d) -> r k d", k=PATCH)
        region = sb("region", [128, W_ELEMS])
        ident = sb("ident", [128, 128])
        identb = sb("identb", [128, 128], BF16)
        centre = sb("centre", [128, 128])
        mean_of = sb("mean_of", [128, 128])
        eps_col = sb("eps_col", [128, 1])
        posT = sb("posT", [D, 1 + PATCHES])
        patch_b = sb("patch_b", [D, 1])
        poly = sb("poly", [D, 1])
        qkv_w = sb("qkv_w", [D, 3, HEADS, HD])
        qkv_b = sb("qkv_b", [128, 3 * QUADS])
        woT = sb("woT", [128, QUADS, D])
        out_b = sb("out_b", [D, 1])
        head_rows = sb("head_rows", [128, QH])
        gate_wT = sb("gate_wT", [D, EXPERTS])
        b1T = sb("b1T", [128, ALL_EXPERTS * FB])
        b2_rows = sb("b2_rows", [ALL_EXPERTS, D])
        work = sb("work", [128, 9600])

        CHUNK_IMAGES = 4
        XT = CHUNK_IMAGES * GRID * SIDE
        x_tile = [region[0:ROWS, u * XT:(u + 1) * XT] for u in range(2)]
        o = 2 * XT
        wl_sb = region[:, o:o + HEADS * D].rearrange("p (h i) -> p h i", h=HEADS)
        o += HEADS * D
        wqkv_sb = region[:, o:o + HEADS * 3 * HD].rearrange("p (h c d) -> p h c d", h=HEADS, c=3)
        o += HEADS * 3 * HD
        wo_sb = region[:, o:o + HEADS * HD]
        assert o + HEADS * HD <= W_ELEMS

        tokens_in, patchw_in, attnw_in, ffnb_in = (sem(n) for n in ("tokens_in", "patchw_in", "attnw_in", "ffnb_in"))
        pool_const = sem("pool_const")
        dve_const = sem("dve_const")
        setup_mm = sem("setup_mm")
        setup_ev = sem("setup_ev")
        fold_mm = sem("fold_mm")
        fold_ev = sem("fold_ev")

        w_raw = hT[:, 0:CHANNELS * PATCH * PATCH]
        small = hT[:, 2400:2400 + 1024]
        pos_raw = small[0:1 + PATCHES, 0:128]
        cls_raw = small[0:1, 128:256]
        bl_raw = small[0:HEADS, 256:384]
        gate_raw = small[0:EXPERTS, 384:512]
        b1_raw = small[0:ALL_EXPERTS * FB, 512:640]
        blT = small[:, 768:784]
        clsT_src = small[0:1, 800:928]
        bo_col = sb("bo_col", [D, 1])
        p_row = sb("p_row", [1, 1])
        poly_row = sb("poly_row", [1, D])
        posc = sb("posc", [D, 2])

        def setup_loads(sp):
            sp.dma_start(tok_i[:, :], x_txt).then_inc(tokens_in, 16)
            sp.dma_start(p_row[:, :], txt_p.rearrange("(a n) -> a n", a=1)).then_inc(tokens_in, 16)
            sp.dma_start(w_raw, tok_W).then_inc(patchw_in, 16)
            sp.dma_start(pos_raw, tok_pos).then_inc(patchw_in, 16)
            sp.dma_start(cls_raw, tok_cls).then_inc(patchw_in, 16)
            sp.dma_start(patch_b[:, :], tok_b.rearrange("(p a) -> p a", a=1)).then_inc(patchw_in, 16)
            sp.dma_start(wl_sb, Wl.rearrange("h o i -> o h i")).then_inc(attnw_in, 16)
            for c, w in enumerate((Wq, Wk, Wv)):
                sp.dma_start(wqkv_sb[:, :, c, :], w.rearrange("h i d -> i h d")).then_inc(attnw_in, 16)
            sp.dma_start(wo_sb, Wo).then_inc(attnw_in, 16)
            sp.dma_start(bl_raw, bl).then_inc(attnw_in, 16)
            sp.dma_start(bo_col[:, :], bo.rearrange("(p a) -> p a", a=1)).then_inc(attnw_in, 16)
            sp.dma_start(gate_raw, gate_w).then_inc(ffnb_in, 16)
            sp.dma_start(b1_raw[0:EXPERTS * FB, :], re_b1.rearrange("e (f p) -> (e f) p", p=128)).then_inc(ffnb_in, 16)
            sp.dma_start(b1_raw[EXPERTS * FB:ALL_EXPERTS * FB, :],
                         se_b1.rearrange("e (f p) -> (e f) p", p=128)).then_inc(ffnb_in, 16)
            sp.dma_start(b2_rows[0:EXPERTS, :], re_b2).then_inc(ffnb_in, 16)
            sp.dma_start(b2_rows[EXPERTS:ALL_EXPERTS, :], se_b2).then_inc(ffnb_in, 16)

        def setup_pool(pool):
            nc.gpsimd.memset(ident[:, :], 0.0).then_inc(pool_const, 1)
            pool.wait_ge(pool_const, 1)
            nc.gpsimd.affine_select(out=ident[:, :], in_=ident[:, :], compare_op=ALU.not_equal, fill=1.0,
                                    base=0, pattern=[[-1, 128]], channel_multiplier=1).then_inc(pool_const, 1)
            nc.gpsimd.memset(mean_of[:, :], 1.0 / D).then_inc(pool_const, 1)
            nc.gpsimd.memset(eps_col[:, :], LN_EPS).then_inc(pool_const, 1)
            pool.wait_ge(pool_const, 4)
            nc.gpsimd.tensor_copy(identb[:, :], ident[:, :]).then_inc(pool_const, 1)
            nc.gpsimd.tensor_tensor(centre[:, :], ident[:, :], mean_of[:, :], ALU.subtract).then_inc(pool_const, 1)
        POOL_CONST = 6

        W_BANKS = PATCH // 4

        def setup_pe(pe):
            pe.wait_ge(pool_const, POOL_CONST)
            pe.wait_ge(patchw_in, 64)
            wv = w_raw.rearrange("p (r c) -> p c r", c=PATCH)
            for j in range(W_BANKS):
                for k in range(4):
                    last = nc.tensor.transpose(bank[j][0:ROWS, k * 128:(k + 1) * 128], wv[:, 4 * j + k, :], ident[:, :])
                last.then_inc(setup_mm, 1)
            pe.wait_ge(dve_const, SETUP_ROWS)
            nc.tensor.transpose(bank[7][:, 0:65], pos_raw, ident[0:65, 0:65])
            nc.tensor.transpose(bank[7][:, 65:66], clsT_src, ident[0:1, 0:1])
            nc.tensor.transpose(bank[7][:, 66:67], poly_row[:, :], ident[0:1, 0:1])
            pe.wait_ge(attnw_in, 112)
            nc.tensor.transpose(bank[7][:, 68:84], bl_raw, ident[0:HEADS, 0:HEADS])
            pe.wait_ge(ffnb_in, 80)
            nc.tensor.transpose(bank[7][:, 84:100], gate_raw, ident[0:EXPERTS, 0:EXPERTS])
            nc.tensor.transpose(bank[7][:, 100:172], b1_raw, ident[0:ALL_EXPERTS * FB, 0:ALL_EXPERTS * FB]).then_inc(setup_mm, 1)
            pe.wait_ge(setup_ev, W_BANKS)
            for j in range(QUADS):
                for k in range(QH):
                    last = nc.tensor.matmul(bank[j][:, k * 96:(k + 1) * 96], wl_sb[:, 4 * j + k, :],
                                            wqkv_sb[:, 4 * j + k, :, :], start=True, stop=True)
                last.then_inc(fold_mm, 1)
            for k in range(QUADS):
                last = nc.tensor.transpose(bank[4][:, k * 128:(k + 1) * 128], wo_sb[:, k * 128:(k + 1) * 128], ident[:, :])
            last.then_inc(fold_mm, 1)
            pe.wait_ge(setup_ev, W_BANKS + 1)
            for c in range(3):
                for h in range(HEADS):
                    q = 32 * (h % QH)
                    last = nc.tensor.matmul(bank[5][q:q + 32, c * QUADS + h // QH:c * QUADS + h // QH + 1],
                                            wqkv_sb[:, h, c, :], blT[:, h:h + 1], start=True, stop=True)
            last.then_inc(fold_mm, 1)
            pe.wait_ge(fold_ev, QUADS + 2)
            for k in range(QUADS):
                last = nc.tensor.matmul(bank[6][:, 0:1], woT[:, k, :], qkv_b[:, 2 * QUADS + k:2 * QUADS + k + 1],
                                        start=(k == 0), stop=(k == QUADS - 1))
            last.then_inc(fold_mm, 1)

        SETUP_ROWS = 16

        def setup_dve_rows(dve):
            dve.wait_ge(tokens_in, 32)
            nc.vector.memset(poly_row[:, 0:1], 1.0).then_inc(dve_const, 1)
            nc.vector.tensor_copy(poly_row[:, 1:2], p_row[:, :]).then_inc(dve_const, 1)
            n, done = 2, 2
            while n < D:
                dve.wait_ge(dve_const, done)
                nc.vector.tensor_tensor(poly_row[:, n:n + 1], poly_row[:, n // 2:n // 2 + 1],
                                        poly_row[:, n // 2:n // 2 + 1], ALU.mult).then_inc(dve_pow, 1)
                dve.wait_ge(dve_pow, done - 1)
                nc.vector.tensor_scalar(poly_row[:, n + 1:2 * n], poly_row[:, 1:n], poly_row[:, n:n + 1], None,
                                        ALU.mult).then_inc(dve_const, 1)
                n, done = 2 * n, done + 1
            dve.wait_ge(patchw_in, 64)
            nc.vector.tensor_tensor(clsT_src, cls_raw, pos_raw[0:1, :], ALU.mult).then_inc(dve_const, 1)
            nc.vector.memset(head_rows[:, :], 0.0).then_inc(dve_const, 1)
            dve.wait_ge(dve_const, done + 2)
            for h in range(QH):
                nc.vector.memset(head_rows[32 * h:32 * h + 32, h:h + 1], 1.0).then_inc(dve_const, 1)
            nc.vector.memset(xT[:, TOKENS:], 0.0).then_inc(dve_const, 1)
            nc.vector.memset(hT[:, TOKENS:], 0.0).then_inc(dve_const, 1)
            assert done + 4 + QH == SETUP_ROWS, done

        dve_pow = sem("dve_pow")

        def setup_dve(dve):
            for j in range(W_BANKS):
                dve.wait_ge(setup_mm, j + 1)
                nc.vector.tensor_copy(patch_wT[:, 4 * j:4 * j + 4, :],
                                      bank[j][0:ROWS, :].rearrange("p (k d) -> p k d", k=4)).then_inc(setup_ev, 1)
            dve.wait_ge(setup_mm, W_BANKS + 1)
            nc.vector.tensor_copy(blT, bank[7][:, 68:84]).then_inc(setup_ev, 1)
            nc.vector.tensor_copy(posT[:, :], bank[7][:, 0:65]).then_inc(setup_ev, 1)
            nc.vector.tensor_copy(posc[:, :], bank[7][:, 65:67]).then_inc(setup_ev, 1)
            nc.vector.tensor_copy(gate_wT[:, :], bank[7][:, 84:100]).then_inc(setup_ev, 1)
            nc.vector.tensor_copy(b1T[:, :], bank[7][:, 100:172]).then_inc(setup_ev, 1)
            for j in range(QUADS):
                dve.wait_ge(fold_mm, j + 1)
                nc.vector.tensor_copy(qkv_w[:, :, QH * j:QH * j + QH, :],
                                      bank[j][:, 0:QH * 96].rearrange("p (h c d) -> p c h d", h=QH, c=3)).then_inc(fold_ev, 1)
            dve.wait_ge(fold_mm, QUADS + 1)
            nc.vector.tensor_copy(woT[:, :, :], bank[4][:, :].rearrange("p (k d) -> p k d", k=QUADS)).then_inc(fold_ev, 1)
            dve.wait_ge(fold_mm, QUADS + 2)
            nc.vector.tensor_copy(qkv_b[:, :], bank[5][:, 0:3 * QUADS]).then_inc(fold_ev, 1)
            dve.wait_ge(fold_mm, QUADS + 3)
            nc.vector.tensor_tensor(out_b[:, :], bank[6][:, 0:1], bo_col[:, :], ALU.add).then_inc(fold_ev, 1)
        SETUP_EV = W_BANKS + 5
        FOLD_EV = QUADS + 3

        tok_i = sb("tok_i", [IMAGES, TEXT], I32)
        wk = [0]

        def carve(n, parts=128):
            a = work[0:parts, wk[0]:wk[0] + n]
            wk[0] += n
            return a
        tok_f = carve(TEXT, IMAGES)
        push = carve(TEXT, IMAGES)
        qlen = carve(TEXT, IMAGES)
        pushes = carve(TEXT, IMAGES)
        step = carve(TEXT, IMAGES)
        ones_row = carve(TEXT, IMAGES)
        tree_rows = carve(4 * TEXT, IMAGES).rearrange("p (k t) -> p k t", k=4)
        head_i = carve(TEXT, IMAGES).bitcast(I32)
        par_i = carve(TEXT, IMAGES).bitcast(I32)
        bit_i = carve(TEXT, IMAGES).bitcast(I32)
        tree_rows_b = carve(TEXT, IMAGES).bitcast(BF16).rearrange("p (k t) -> p k t", k=2)
        tree_cols = carve(4 * IMAGES, TEXT).rearrange("p (k b) -> p k b", k=4)
        lr_cols = carve(IMAGES, TEXT).bitcast(BF16).rearrange("p (b k) -> p b k", k=2)
        HALF = 4
        SW = TEXT + 128 + 1
        seq_t = [carve(HALF * SW // 2, TEXT).bitcast(BF16).rearrange("p (b c) -> p b c", c=SW) for _ in range(2)]
        par_t = [carve(HALF * 78 // 2, TEXT).bitcast(BF16).rearrange("p (b c) -> p b c", c=78) for _ in range(2)]
        tree_bc = xT[0:TEXT, 0:IMAGES * TEXT].bitcast(BF16).rearrange("p (k b t) -> p k b t", k=2, t=TEXT)
        tree_dram = nc.dram_tensor("tree_dram", (2, IMAGES, TEXT), BF16, kind="Internal").ap()

        tree_row = sem("tree_row")
        tree_out = sem("tree_out")
        tree_in = sem("tree_in")
        tree_colmm = sem("tree_colmm")
        tree_col = sem("tree_col")
        tree_start = [sem(f"tree_start{u}") for u in range(2)]
        tree_mm = [sem(f"tree_mm{u}") for u in range(2)]
        tree_ev = [sem(f"tree_ev{u}") for u in range(2)]
        tree_pw = [sem(f"tree_pw{u}") for u in range(2)]
        tree_h = [sem(f"tree_h{u}") for u in range(2)]

        def tree_rows_dve(dve):
            n = [0]

            def link(ins):
                n[0] += 1
                ins.then_inc(tree_row, 1)
                dve.wait_ge(tree_row, n[0])
            nc.vector.memset(ones_row, 1.0)
            link(nc.vector.tensor_copy(tok_f, tok_i[:, :]))
            link(nc.vector.tensor_scalar(push, tok_f, float(END_TOKEN), None, ALU.not_equal))
            link(nc.vector.memset(push[:, 0:1], 1.0))
            link(nc.vector.tensor_scalar(step, push, 2.0, -1.0, ALU.mult, ALU.add))
            link(nc.vector.memset(qlen[:, 0:1], 2.0))
            link(nc.vector.tensor_tensor_scan(qlen[:, 1:], step[:, 1:], ones_row[:, 1:], 2.0, ALU.add, ALU.max))
            link(nc.vector.tensor_tensor_scan(pushes, push, push, 0.0, ALU.add, ALU.max))
            link(nc.vector.memset(tree_rows[:, 0:1, :], 0.0))
            link(nc.vector.scalar_tensor_tensor(tree_rows[:, 0, 1:], pushes[:, 0:TEXT - 1], 2.0, qlen[:, 0:TEXT - 1],
                                                ALU.mult, ALU.subtract))
            link(nc.vector.tensor_copy(head_i, tree_rows[:, 0, :]))
            link(nc.vector.tensor_scalar(par_i, head_i, 1, None, ALU.arith_shift_right))
            link(nc.vector.tensor_scalar(bit_i, head_i, 1, None, ALU.bitwise_and))
            link(nc.vector.tensor_copy(tree_rows[:, 0, :], par_i))
            link(nc.vector.tensor_copy(tree_rows[:, 3, :], bit_i))
            link(nc.vector.tensor_scalar(tree_rows[:, 2, :], tree_rows[:, 3, :], -1.0, 1.0, ALU.mult, ALU.add))
            link(nc.vector.memset(tree_rows[:, 0, 0:1], -2.0))
            link(nc.vector.memset(tree_rows[:, 2, 0:1], 0.0))
            link(nc.vector.memset(tree_rows[:, 3, 0:1], 0.0))
            link(nc.vector.tensor_tensor(tree_rows[:, 1, :], push, pushes, ALU.mult))
            link(nc.vector.tensor_scalar(tree_rows[:, 1, :], tree_rows[:, 1, :], -1.0, None, ALU.add))
            link(nc.vector.tensor_copy(tree_rows_b, tree_rows[:, 0:2, :]))
            assert n[0] == TREE_ROW, n[0]
        TREE_ROW = 21

        def tree_sp(sp):
            sp.wait_ge(tree_row, TREE_ROW)
            sp.dma_start(tree_dram.rearrange("k b t -> b k t"), tree_rows_b).then_inc(tree_out, 16)
            sp.wait_ge(tree_out, 16)
            for k in range(2):
                src = tree_dram[k:k + 1, :, :].rearrange("k b t -> k (b t)").to_broadcast([TEXT, IMAGES * TEXT])
                sp.dma_start(xT[0:TEXT, 0:IMAGES * TEXT].bitcast(BF16)[:, k * IMAGES * TEXT:(k + 1) * IMAGES * TEXT],
                             src).then_inc(tree_in, 16)

        def tree_pe(pe):
            pe.wait_ge(pool_const, POOL_CONST)
            pe.wait_ge(tree_row, TREE_ROW)
            for k in range(4):
                last = nc.tensor.transpose(bank[0][0:TEXT, k * IMAGES:(k + 1) * IMAGES], tree_rows[:, k, :],
                                           ident[0:IMAGES, 0:IMAGES])
            last.then_inc(tree_colmm, 1)
            pe.wait_ge(tree_col, 2)
            with pe.Fori(0, IMAGES // (2 * HALF)) as i:
                for lv in range(TREE_LEVELS):
                    w = 2 << lv
                    lo, hi = (0, TEXT + w) if lv < TREE_LEVELS - 1 else (TEXT, TEXT + w)
                    for u in range(2):
                        if lv == 0:
                            pe.wait_ge(tree_start[u], 3 * (i + 1))
                            pe.wait_ge(tree_h[u], i + 1)
                        else:
                            pe.wait_ge(tree_ev[u], i * 11 + 2 * lv)
                            pe.wait_ge(tree_pw[u], i * 5 + lv)
                        for b in range(HALF):
                            last = nc.tensor.matmul(bank[2 * u][0:TEXT, b * (hi - lo):(b + 1) * (hi - lo)],
                                                    par_t[u][:, b, 0:TEXT], seq_t[u][:, b, lo:hi], start=True, stop=True)
                        if lv < TREE_LEVELS - 1:
                            for b in range(HALF):
                                last = nc.tensor.matmul(bank[2 * u + 1][0:TEXT, b * TEXT:(b + 1) * TEXT],
                                                        seq_t[u][:, b, 0:TEXT], par_t[u][:, b, 0:TEXT], start=True, stop=True)
                        last.then_inc(tree_mm[u], 1)
                for u in range(2):
                    pe.wait_ge(tree_ev[u], i * 11 + 11)
                    for b in range(HALF):
                        last = nc.tensor.matmul(bank[2 * u + 1][:, b * TEXT:(b + 1) * TEXT], seq_t[u][:, b, TEXT:TEXT + D],
                                                identb[0:TEXT, 0:TEXT], start=True, stop=True)
                    last.then_inc(tree_mm[u], 1)

        hT_img = hT[:, 0:TOKENS].rearrange("p (b s) -> p b s", s=SEQ)

        def tree_dve(dve):
            for u in range(2):
                dve.sem_inc(tree_h[u], 1)
            dve.wait_ge(tree_colmm, 1)
            nc.vector.tensor_copy(tree_cols, bank[0][0:TEXT, 0:4 * IMAGES].rearrange("p (k b) -> p k b", k=4)).then_inc(tree_col, 1)
            dve.wait_ge(tree_col, 1)
            nc.vector.tensor_copy(lr_cols, tree_cols[:, 2:4, :].rearrange("p k b -> p b k")).then_inc(tree_col, 1)
            dve.wait_ge(tree_col, 2)
            dve.wait_ge(tree_in, 32)
            dve.wait_ge(setup_ev, SETUP_EV)
            dve.wait_ge(fold_ev, FOLD_EV)
            with dve.Fori(0, IMAGES // (2 * HALF)) as i:
                for u in range(2):
                    b0 = i * (2 * HALF) + u * HALF
                    nc.vector.tensor_tensor(par_t[u][:, :, 0:TEXT], tree_bc[:, 0, bass.ds(b0, HALF), :],
                                            tree_cols[:, 1, bass.ds(b0, HALF)].unsqueeze(2).to_broadcast([TEXT, HALF, TEXT]),
                                            ALU.is_equal).then_inc(tree_start[u], 1)
                    nc.vector.tensor_tensor(seq_t[u][:, :, 0:TEXT], tree_bc[:, 1, bass.ds(b0, HALF), :],
                                            tree_cols[:, 0, bass.ds(b0, HALF)].unsqueeze(2).to_broadcast([TEXT, HALF, TEXT]),
                                            ALU.is_equal).then_inc(tree_start[u], 1)
                    nc.vector.tensor_copy(seq_t[u][:, :, TEXT:TEXT + 2], lr_cols[:, bass.ds(b0, HALF), :]).then_inc(tree_start[u], 1)
                for lv in range(TREE_LEVELS):
                    w = 2 << lv
                    for u in range(2):
                        dve.wait_ge(tree_mm[u], i * 7 + lv + 1)
                        if lv < TREE_LEVELS - 1:
                            src = bank[2 * u][0:TEXT, 0:HALF * (TEXT + w)].rearrange("p (b c) -> p b c", b=HALF)
                            nc.vector.tensor_copy(seq_t[u][:, :, 0:TEXT], src[:, :, 0:TEXT]).then_inc(tree_ev[u], 1)
                            nc.vector.tensor_copy(seq_t[u][:, :, TEXT + w:TEXT + 2 * w],
                                                  src[:, :, TEXT:TEXT + w]).then_inc(tree_ev[u], 1)
                        else:
                            src = bank[2 * u][0:TEXT, 0:HALF * w].rearrange("p (b c) -> p b c", b=HALF)
                            nc.vector.tensor_copy(seq_t[u][:, :, TEXT + w:TEXT + 2 * w], src).then_inc(tree_ev[u], 1)
                for u in range(2):
                    dve.wait_ge(tree_mm[u], i * 7 + 7)
                    nc.vector.tensor_scalar(hT_img[:, bass.ds(i * (2 * HALF) + u * HALF, HALF), 1 + PATCHES:SEQ],
                                            bank[2 * u + 1][:, 0:HALF * TEXT].rearrange("p (b t) -> p b t", b=HALF),
                                            posc[:, 1:2], None, ALU.mult).then_inc(tree_h[u], 1)

        def tree_act(act):
            with act.Fori(0, IMAGES // (2 * HALF)) as i:
                for lv in range(TREE_LEVELS - 1):
                    for u in range(2):
                        act.wait_ge(tree_mm[u], i * 7 + lv + 1)
                        nc.scalar.copy(par_t[u][:, :, 0:TEXT],
                                       bank[2 * u + 1][0:TEXT, 0:HALF * TEXT].rearrange("p (b t) -> p b t", b=HALF)).then_inc(tree_pw[u], 1)

        CHUNKS = IMAGES // CHUNK_IMAGES
        CP = CHUNK_IMAGES * PATCHES
        x_in = [sem(f"x_in{u}") for u in range(2)]
        patch_mm = [sem(f"patch_mm{u}") for u in range(2)]
        patch_ev = [sem(f"patch_ev{u}") for u in range(2)]
        x_v = x.rearrange("b c (g r) w -> b c r g w", r=PATCH)

        def patch_sp(sp):
            def load(u, b0):
                for b in range(CHUNK_IMAGES):
                    for c in range(CHANNELS):
                        sp.dma_start(x_tile[u][c * PATCH:(c + 1) * PATCH, b * GRID * SIDE:(b + 1) * GRID * SIDE],
                                     x_v[bass.ds(b0 + b, 1), c, :, :, :]).then_inc(x_in[u], 16)
            for u in range(2):
                load(u, u * CHUNK_IMAGES)
            with sp.Fori(1, CHUNKS // 2) as i:
                for u in range(2):
                    sp.wait_ge(patch_mm[u], i)
                    load(u, i * (2 * CHUNK_IMAGES) + u * CHUNK_IMAGES)

        def patch_pe(pe):
            with pe.Fori(0, CHUNKS // 2) as i:
                for u in range(2):
                    pe.wait_ge(x_in[u], (i + 1) * (16 * CHANNELS * CHUNK_IMAGES))
                    pe.wait_ge(patch_ev[u], i + 1)
                    xv = x_tile[u].rearrange("r (n k) -> r k n", k=PATCH)
                    for k in range(PATCH):
                        last = nc.tensor.matmul(bank[4 + u][:, 0:CP], patch_wT[:, k, :], xv[:, k, :],
                                                start=(k == 0), stop=(k == PATCH - 1))
                    last.then_inc(patch_mm[u], 1)

        def patch_dve(dve):
            dve.sem_inc(patch_ev[0], 1)
            dve.sem_inc(patch_ev[1], 1)
            nc.vector.tensor_copy(hT_img[:, :, 0:1].rearrange("p b s -> p (b s)"),
                                  posc[:, 0:1].to_broadcast([D, IMAGES])).then_inc(cls_done, 1)
            with dve.Fori(0, CHUNKS // 2) as i:
                for u in range(2):
                    dve.wait_ge(patch_mm[u], i + 1)
                    nc.vector.scalar_tensor_tensor(
                        hT_img[:, bass.ds(i * (2 * CHUNK_IMAGES) + u * CHUNK_IMAGES, CHUNK_IMAGES), 1:1 + PATCHES],
                        bank[4 + u][:, 0:CP].rearrange("p (b t) -> p b t", b=CHUNK_IMAGES), patch_b[:, :],
                        posT[:, 1:1 + PATCHES].unsqueeze(1).to_broadcast([D, CHUNK_IMAGES, PATCHES]),
                        ALU.add, ALU.mult).then_inc(patch_ev[u], 1)
        cls_done = sem("cls_done")

        slot_rows = nc.dram_tensor("slot_rows", (SLOTS + 128 * TOPK, ROW), F32, kind="Internal").ap()
        FT = FILL_TILES // FILLS
        fill = [work[:, r * FT * ROW:(r + 1) * FT * ROW].rearrange("p (j c) -> p j c", c=ROW) for r in range(2)]
        fill_ready = sem("fill_ready")
        fill_out = [sem(f"fill_out{r}") for r in range(2)]
        FILL_OUT = 16 * (FILLS // 2)

        def fill_pool(pool):
            for u in range(2):
                pool.wait_ge(tree_h[u], IMAGES // (2 * HALF) + 1)
            for r in range(2):
                nc.gpsimd.memset(fill[r], 0.0).then_inc(fill_ready, 1)
            rows = slot_rows[0:SLOTS, :].rearrange("(p j) c -> p j c", p=128)
            for f in range(FILLS):
                r = f % 2
                if f >= 2:
                    pool.wait_ge(fill_out[r], 16 * (f // 2))
                pool.wait_ge(fill_ready, 2 + f)
                nc.gpsimd.iota(fill[r].bitcast(I32)[:, :, D], pattern=[[1, FT]], base=ASSIGNED + f * FT,
                               channel_multiplier=FILL_TILES).then_inc(fill_ready, 1)
                pool.wait_ge(fill_ready, 3 + f)
                pool.dma_start(rows[:, f * FT:(f + 1) * FT, :], fill[r]).then_inc(fill_out[r], 16)

        LW = 2 * SEQ
        LCHUNKS = TOKENS // LW

        class Norm:
            def __init__(self, name):
                self.centred, self.copied, self.squared, self.var, self.sd, self.rs, self.done = (
                    [sem(f"{name}_{n}{u}") for u in range(2)] for n in ("centred", "copied", "squared", "var", "sd", "rs", "done"))
                self.cx, self.sq, self.sdev, self.rstd = (
                    [work[:, (2 * k + u) * LW:(2 * k + u + 1) * LW] for u in range(2)] for k in range(4))

            def pe(self, pe):
                with pe.Fori(0, LCHUNKS // 2) as i:
                    for u in range(2):
                        pe.wait_ge(self.copied[u], i + 1)
                        nc.tensor.matmul(bank[u][:, 0:LW], centre[:, :], hT[:, bass.ds(i * (2 * LW) + u * LW, LW)],
                                         start=True, stop=True).then_inc(self.centred[u], 1)
                    for u in range(2):
                        pe.wait_ge(self.squared[u], i + 1)
                        pe.wait_ge(self.sd[u], i + 1)
                        nc.tensor.matmul(bank[2 + u][:, 0:LW], mean_of[:, :], self.sq[u], start=True, stop=True).then_inc(self.var[u], 1)

            def act(self, act):
                for u in range(2):
                    act.wait_ge(fill_out[u], FILL_OUT)
                    act.sem_inc(self.copied[u], 1)
                    act.sem_inc(self.sd[u], 1)
                with act.Fori(0, LCHUNKS // 2) as i:
                    for u in range(2):
                        act.wait_ge(self.centred[u], i + 1)
                        act.wait_ge(self.done[u], i + 1)
                        nc.scalar.copy(self.cx[u], bank[u][:, 0:LW]).then_inc(self.copied[u], 1)
                    for u in range(2):
                        act.wait_ge(self.var[u], i + 1)
                        nc.scalar.activation(self.sdev[u], bank[2 + u][:, 0:LW], ACT.Sqrt, bias=eps_col[:, :]).then_inc(self.sd[u], 1)

            def pool(self, pool):
                with pool.Fori(0, LCHUNKS // 2) as i:
                    for u in range(2):
                        pool.wait_ge(self.copied[u], i + 2)
                        nc.gpsimd.tensor_tensor(self.sq[u], self.cx[u], self.cx[u], ALU.mult).then_inc(self.squared[u], 1)

            def dve(self, dve):
                for u in range(2):
                    dve.sem_inc(self.done[u], 1)
                with dve.Fori(0, LCHUNKS // 2) as i:
                    for u in range(2):
                        dve.wait_ge(self.sd[u], i + 2)
                        nc.vector.reciprocal(self.rstd[u], self.sdev[u]).then_inc(self.rs[u], 1)
                    for u in range(2):
                        dve.wait_ge(self.rs[u], i + 1)
                        nc.vector.tensor_tensor(xT[:, bass.ds(i * (2 * LW) + u * LW, LW)], self.cx[u], self.rstd[u],
                                                ALU.mult).then_inc(self.done[u], 1)

        norm1 = Norm("norm1")
        norm2 = Norm("norm2")

        wk[0] = 0
        xs = [carve(SEQ) for _ in range(2)]
        qk = [carve(8 * SEQ).rearrange("p (k s) -> p k s", k=8) for _ in range(2)]
        v_main = [carve(HEADS * HD) for _ in range(2)]
        v_tail = [carve(HEADS * HD, TAIL) for _ in range(2)]
        nmax = [carve(HEADS) for _ in range(2)]
        rsum = [carve(HEADS) for _ in range(2)]
        rinv = carve(HEADS)
        probs = [carve(QH * MAIN) for _ in range(2)]
        probsT = [carve(QH * MAIN) for _ in range(2)]
        attn = carve(HEADS * HD)
        catT = carve(QUADS * SEQ).rearrange("p (g s) -> p g s", g=QUADS)
        TR = QH * TAIL
        nmax_t = carve(QUADS, TR)
        rsum_t = carve(QUADS, TR)
        rinv_t = carve(QUADS, TR)
        probs_t = carve(QUADS * SEQ, TR).rearrange("p (g s) -> p g s", g=QUADS)
        probsT_a = carve(QUADS * TR).rearrange("p (g r) -> p g r", g=QUADS)
        probsT_b = carve(QUADS * TR, TAIL).rearrange("p (g r) -> p g r", g=QUADS)
        assert wk[0] <= 9600, wk[0]
        QZ_AT = W_ELEMS - 2 * HEADS * SEQ
        qz = [region[:, QZ_AT + u * HEADS * MAIN:QZ_AT + (u + 1) * HEADS * MAIN].rearrange("p (g h s) -> p g h s", g=QUADS, h=QH)
              for u in range(2)]
        QT_AT = QZ_AT + 2 * HEADS * MAIN
        qz_t = [region[:, QT_AT + u * HEADS * TAIL:QT_AT + (u + 1) * HEADS * TAIL].rearrange("p (g h s) -> p g h s", g=QUADS, h=QH)
                for u in range(2)]
        mask_main = sb("mask_main", [128, QH, MAIN], BF16)
        mask_tail = sb("mask_tail", [TR, 2, SEQ], BF16)

        mask_ready, mask_dma = sem("mask_ready"), sem("mask_dma")
        qk_mm, qk_ev, v_mm, v_ev = sem("qk_mm"), sem("qk_ev"), sem("v_mm"), sem("v_ev")
        xs_ready, qz_ready = sem("xs_ready"), sem("qz_ready")
        s_mm, max_done, exp_done, t_mm, t_ev, f_mm, norm_done = (sem(n) for n in (
            "s_mm", "max_done", "exp_done", "t_mm", "t_ev", "f_mm", "norm_done"))
        st_mm, maxt_done, expt_done, normt_done, tt_mm, tt_ev, tf_mm, tf_ev = (sem(n) for n in (
            "st_mm", "maxt_done", "expt_done", "normt_done", "tt_mm", "tt_ev", "tf_mm", "tf_ev"))
        ft_mm, ft_ev, o_mm, resid = sem("ft_mm"), sem("ft_ev"), sem("o_mm"), sem("resid")
        rinv_done, rinvt_done = sem("rinv_done"), sem("rinvt_done")

        passed = sem("passed")

        def settle(eng):
            eng.sem_inc(passed, 1)

        def at(i, u, per, c):
            return i * (2 * per) + (u * per + c)

        def attn_masks_pool(pool):
            nc.gpsimd.memset(mask_main[:, :, :], 0.0).then_inc(mask_ready, 1)
            nc.gpsimd.memset(mask_tail[:, :, :], 0.0).then_inc(mask_ready, 1)
            pool.wait_ge(mask_ready, 2)
            nc.gpsimd.affine_select(out=mask_main[:, :, :], in_=mask_main[:, :, :], compare_op=ALU.is_ge, fill=MASKED,
                                    base=0, pattern=[[0, QH], [-1, MAIN]], channel_multiplier=1).then_inc(mask_ready, 1)
            pool.wait_ge(mask_ready, 3)
            for h in range(QH):
                for k in range(2):
                    pool.dma_start(mask_tail[h * TAIL:(h + 1) * TAIL, k, MAIN:SEQ],
                                   mask_main[0:TAIL, 0, 0:TAIL]).then_inc(mask_dma, 16)
        MASK_DMA = 16 * 2 * QH

        def qk_fill(pe, u, j, b):
            for k in range(3 * j, min(3 * j + 3, 8)):
                c, g = divmod(k, QUADS)
                last = nc.tensor.matmul(b[:, (k - 3 * j) * SEQ:(k - 3 * j + 1) * SEQ],
                                        qkv_w[:, c, QH * g:QH * g + QH, :], xs[u], start=True, stop=True)
            last.then_inc(qk_mm, 1)

        def v_fill(pe, u, part, b):
            lo, n = ((0, MAIN), (MAIN, TAIL))[part]
            nc.tensor.matmul(b[0:n, :], xs[u][:, lo:lo + n], qkv_w[:, 2, :, :], start=True, stop=True).then_inc(v_mm, 1)

        def s_fill(pe, u, g):
            nc.tensor.matmul(bank[g % 2][:, :], identb[:, :], mask_main[:, :, :], start=True, stop=False)
            for h in range(QH):
                last = nc.tensor.matmul(bank[g % 2][:, h * MAIN:(h + 1) * MAIN], qz[u][:, g, h, 0:MAIN],
                                        qk[u][:, QUADS + g, 0:MAIN], start=False, stop=(h == QH - 1))
            last.then_inc(s_mm, 1)

        def attn_pe(pe):
            pe.wait_ge(mask_dma, MASK_DMA)
            pe.wait_ge(fold_ev, FOLD_EV)
            pe.wait_ge(xs_ready, 1)
            qk_fill(pe, 0, 0, bank[5])
            qk_fill(pe, 0, 1, bank[6])
            pe.wait_ge(qk_ev, 1)
            qk_fill(pe, 0, 2, bank[5])
            pe.wait_ge(qk_ev, 2)
            v_fill(pe, 0, 0, bank[6])
            pe.wait_ge(qk_ev, 3)
            v_fill(pe, 0, 1, bank[5])
            pe.wait_ge(qz_ready, 8)
            s_fill(pe, 0, 0)
            s_fill(pe, 0, 1)
            with pe.Fori(0, IMAGES // 2) as i:
                for u in range(2):
                    w = 1 - u

                    def st_fill(p):
                        settle(pe)
                        nc.tensor.matmul(bank[7][0:TR, 0:2 * SEQ], identb[0:TR, 0:TR], mask_tail[:, :, :], start=True, stop=False)
                        for k in range(2):
                            last = nc.tensor.matmul(bank[7][0:TR, k * SEQ:(k + 1) * SEQ], qz_t[u][:, 2 * p + k, :, :],
                                                    qk[u][:, QUADS + 2 * p + k, :], start=False, stop=(k == 1))
                        last.then_inc(st_mm, 1)

                    def t_fill(g):
                        pe.wait_ge(exp_done, at(i, u, 16, 4 * g + 4))
                        pe.wait_ge(t_ev, at(i, u, 4, g - 2 + 4 + 1))
                        for h in range(QH):
                            last = nc.tensor.transpose(bank[2 + g % 2][:, h * MAIN:(h + 1) * MAIN],
                                                       probs[g % 2][:, h * MAIN:(h + 1) * MAIN], ident[:, :])
                        last.then_inc(t_mm, 1)

                    def f_fill(g):
                        pe.wait_ge(t_ev, at(i, u, 4, g + 4 + 1))
                        if g == 0:
                            pe.wait_ge(resid, at(i, u, 1, 1))
                            pe.wait_ge(v_ev, at(i, u, 2, 1))
                        for h in range(QH):
                            c = (QH * g + h) * HD
                            last = nc.tensor.matmul(bank[4][:, c:c + HD], probsT[g % 2][:, h * MAIN:(h + 1) * MAIN],
                                                    v_main[u][:, c:c + HD], start=True, stop=True)
                        last.then_inc(f_mm, 1)

                    def tt_fill(p):
                        settle(pe)
                        for k in range(2):
                            g = 2 * p + k
                            nc.tensor.transpose(bank[6][:, k * TR:(k + 1) * TR], probs_t[:, g, 0:MAIN], ident[0:TR, 0:TR])
                            last = nc.tensor.transpose(bank[6][0:TAIL, (2 + k) * TR:(3 + k) * TR], probs_t[:, g, MAIN:SEQ],
                                                       ident[0:TR, 0:TR])
                        last.then_inc(tt_mm, 1)

                    pe.wait_ge(expt_done, at(i, u, 4, 4))
                    st_fill(0)
                    pe.wait_ge(xs_ready, at(i, u, 1, 2))
                    pe.wait_ge(v_ev, at(i, u, 2, 2))
                    pe.wait_ge(tf_ev, at(i, u, 4, 4))
                    qk_fill(pe, w, 0, bank[5])
                    pe.wait_ge(tt_ev, at(i, u, 4, 4))
                    qk_fill(pe, w, 1, bank[6])
                    t_fill(0)
                    s_fill(pe, u, 2)
                    f_fill(0)
                    pe.wait_ge(qk_ev, at(i, u, 3, 4))
                    qk_fill(pe, w, 2, bank[5])
                    pe.wait_ge(qk_ev, at(i, u, 3, 5))
                    v_fill(pe, w, 0, bank[6])
                    t_fill(1)
                    s_fill(pe, u, 3)
                    pe.wait_ge(expt_done, at(i, u, 4, 2 + 4))
                    st_fill(1)
                    f_fill(1)
                    pe.wait_ge(qk_ev, at(i, u, 3, 6))
                    v_fill(pe, w, 1, bank[5])
                    t_fill(2)
                    pe.wait_ge(normt_done, at(i, u, 2, 1))
                    pe.wait_ge(v_ev, at(i, u, 2, 3))
                    tt_fill(0)
                    f_fill(2)
                    t_fill(3)
                    pe.wait_ge(normt_done, at(i, u, 2, 2))
                    pe.wait_ge(tt_ev, at(i, u, 4, 2 + 4))
                    tt_fill(1)
                    f_fill(3)
                    pe.wait_ge(qz_ready, at(i, u, 8, 16))
                    s_fill(pe, w, 0)
                    pe.wait_ge(norm_done, at(i, u, 1, 2))
                    for g in range(QUADS):
                        last = nc.tensor.transpose(bank[4][:, g * 128:(g + 1) * 128], attn[:, g * 128:(g + 1) * 128], ident[:, :])
                    last.then_inc(ft_mm, 1)
                    pe.wait_ge(v_ev, at(i, u, 2, 4))
                    pe.wait_ge(tt_ev, at(i, u, 4, 4 + 4))
                    for g in range(QUADS):
                        nc.tensor.matmul(bank[5][:, g * TR:(g + 1) * TR], v_main[u][:, g * 128:(g + 1) * 128], probsT_a[:, g, :],
                                         start=True, stop=False)
                        last = nc.tensor.matmul(bank[5][:, g * TR:(g + 1) * TR], v_tail[u][:, g * 128:(g + 1) * 128],
                                                probsT_b[:, g, :], start=False, stop=True)
                    last.then_inc(tf_mm, 1)
                    s_fill(pe, w, 1)
                    pe.wait_ge(ft_ev, at(i, u, 1, 1))
                    pe.wait_ge(tf_ev, at(i, u, 4, 8))
                    for g in range(QUADS):
                        last = nc.tensor.matmul(bank[4][:, 0:SEQ], woT[:, g, :], catT[:, g, :], start=(g == 0), stop=(g == QUADS - 1))
                    last.then_inc(o_mm, 1)

        def attn_pool(pool):
            def stage(u, at_col):
                nc.gpsimd.tensor_copy(xs[u], xT[:, at_col]).then_inc(xs_ready, 1)

            def spread(u):
                for h in range(QH):
                    nc.gpsimd.tensor_scalar(qz[u][:, :, h, :], qk[u][:, 0:QUADS, 0:MAIN], head_rows[:, h:h + 1], 0.0, ALU.mult, ALU.add).then_inc(qz_ready, 1)
                    nc.gpsimd.tensor_scalar(qz_t[u][:, :, h, :], qk[u][:, 0:QUADS, MAIN:SEQ], head_rows[:, h:h + 1], 0.0, ALU.mult, ALU.add).then_inc(qz_ready, 1)
            for u in range(2):
                pool.wait_ge(norm1.done[u], LCHUNKS // 2 + 1)
            stage(0, slice(0, SEQ))
            stage(1, slice(SEQ, 2 * SEQ))
            pool.wait_ge(dve_const, SETUP_ROWS)
            pool.wait_ge(qk_ev, 3)
            spread(0)
            with pool.Fori(0, IMAGES // 2) as i:
                for u in range(2):
                    pool.wait_ge(v_mm, at(i, u, 2, 2))
                    settle(pool)
                    stage(u, bass.ds(i * (2 * SEQ) + (u + 2) * SEQ, SEQ))
                    pool.wait_ge(qk_ev, at(i, u, 3, 5))
                    settle(pool)
                    spread(1 - u)

        def attn_act(act):
            def v_evac(u, part, b):
                n = (MAIN, TAIL)[part]
                nc.scalar.copy((v_main, v_tail)[part][u][0:n, :], b[0:n, :]).then_inc(v_ev, 1)
            act.wait_ge(v_mm, 1)
            v_evac(0, 0, bank[6])
            act.wait_ge(v_mm, 2)
            v_evac(0, 1, bank[5])
            with act.Fori(0, IMAGES // 2) as i:
                for u in range(2):
                    def exps(g):
                        act.wait_ge(max_done, at(i, u, 4, g + 1))
                        act.wait_ge(t_mm, at(i, u, 4, g - 2 + 4 + 1))
                        for h in range(QH):
                            n = QH * g + h
                            nc.scalar.activation(probs[g % 2][:, h * MAIN:(h + 1) * MAIN], bank[g % 2][:, h * MAIN:(h + 1) * MAIN],
                                                 ACT.Exp, bias=nmax[u][:, n:n + 1], accum_out=rsum[u][:, n:n + 1]).then_inc(exp_done, 1)

                    def tail_exps(p):
                        act.wait_ge(maxt_done, at(i, u, 2, p + 1))
                        act.wait_ge(tt_mm, at(i, u, 2, p + 1))
                        for k in range(2):
                            g = 2 * p + k
                            nc.scalar.activation(probs_t[:, g, :], bank[7][0:TR, k * SEQ:(k + 1) * SEQ], ACT.Exp,
                                                 bias=nmax_t[:, g:g + 1], accum_out=rsum_t[:, g:g + 1]).then_inc(expt_done, 1)
                    exps(0)
                    exps(1)
                    tail_exps(0)
                    act.wait_ge(v_mm, at(i, u, 2, 3))
                    v_evac(1 - u, 0, bank[6])
                    exps(2)
                    exps(3)
                    tail_exps(1)
                    act.wait_ge(v_mm, at(i, u, 2, 4))
                    v_evac(1 - u, 1, bank[5])
                    act.wait_ge(ft_mm, at(i, u, 1, 1))
                    act.wait_ge(o_mm, at(i, u, 1, 1))
                    nc.scalar.copy(catT[:, :, 0:MAIN], bank[4][:, :].rearrange("p (g s) -> p g s", g=QUADS)).then_inc(ft_ev, 1)

        def attn_dve(dve):
            dve.sem_inc(t_ev, 4)
            dve.sem_inc(t_mm, 4)
            dve.sem_inc(tt_mm, 2)
            dve.sem_inc(expt_done, 4)
            dve.sem_inc(f_mm, 4)
            dve.sem_inc(tf_mm, 1)
            dve.sem_inc(tt_ev, 4)
            dve.sem_inc(tf_ev, 4)
            dve.sem_inc(norm_done, 1)
            dve.sem_inc(resid, 1)
            dve.sem_inc(o_mm, 1)

            def qk_evac(u, j, b):
                n = min(3, 8 - 3 * j)
                nc.vector.tensor_tensor(qk[u][:, 3 * j:3 * j + n, :], b[:, 0:n * SEQ].rearrange("p (k s) -> p k s", k=n),
                                        qkv_b[:, 3 * j:3 * j + n].unsqueeze(2).to_broadcast([128, n, SEQ]),
                                        ALU.add).then_inc(qk_ev, 1)
            for j in range(3):
                dve.wait_ge(qk_mm, j + 1)
                qk_evac(0, j, bank[5 + j % 2])

            def maxes_into(u, g):
                nc.vector.tensor_reduce(nmax[u][:, QH * g:QH * g + QH], bank[g % 2][:, :].rearrange("p (h s) -> p h s", h=QH),
                                        AX.X, ALU.max, negate=True).then_inc(max_done, 1)
            for g in range(2):
                dve.wait_ge(s_mm, g + 1)
                maxes_into(0, g)
            with dve.Fori(0, IMAGES // 2) as i:
                for u in range(2):
                    def maxes(g):
                        dve.wait_ge(s_mm, at(i, u, 4, g + 1))
                        maxes_into(u if g < QUADS else 1 - u, g % QUADS)

                    def tail_maxes(p):
                        dve.wait_ge(st_mm, at(i, u, 2, p + 1))
                        nc.vector.tensor_reduce(nmax_t[:, 2 * p:2 * p + 2], bank[7][0:TR, 0:2 * SEQ].rearrange("p (k s) -> p k s", k=2),
                                                AX.X, ALU.max, negate=True).then_inc(maxt_done, 1)

                    def tail_inv(p):
                        dve.wait_ge(expt_done, at(i, u, 4, 2 * p + 2 + 4))
                        nc.vector.reciprocal(rinv_t[:, 2 * p:2 * p + 2], rsum_t[:, 2 * p:2 * p + 2]).then_inc(rinvt_done, 1)

                    def tail_norm(p):
                        dve.wait_ge(rinvt_done, at(i, u, 2, p + 1))
                        t = probs_t[:, 2 * p:2 * p + 2, :]
                        nc.vector.tensor_tensor(t, t, rinv_t[:, 2 * p:2 * p + 2].unsqueeze(2).to_broadcast([TR, 2, SEQ]),
                                                ALU.mult).then_inc(normt_done, 1)

                    def t_evac(g):
                        dve.wait_ge(t_mm, at(i, u, 4, g + 1 + 4))
                        dve.wait_ge(f_mm, at(i, u, 4, g - 2 + 4 + 1))
                        nc.vector.tensor_copy(probsT[g % 2], bank[2 + g % 2][:, :]).then_inc(t_ev, 1)

                    def tt_evac(p):
                        dve.wait_ge(tt_mm, at(i, u, 2, p + 1 + 2))
                        if p == 0:
                            dve.wait_ge(tf_mm, at(i, u, 1, 1))
                        nc.vector.tensor_copy(probsT_a[:, 2 * p:2 * p + 2, :],
                                              bank[6][:, 0:2 * TR].rearrange("p (k r) -> p k r", k=2)).then_inc(tt_ev, 1)
                        nc.vector.tensor_copy(probsT_b[:, 2 * p:2 * p + 2, :],
                                              bank[6][0:TAIL, 2 * TR:4 * TR].rearrange("p (k r) -> p k r", k=2)).then_inc(tt_ev, 1)
                    tail_maxes(0)
                    dve.wait_ge(qk_mm, at(i, u, 3, 4))
                    qk_evac(1 - u, 0, bank[5])
                    dve.wait_ge(qk_mm, at(i, u, 3, 5))
                    qk_evac(1 - u, 1, bank[6])
                    tail_inv(0)
                    t_evac(0)
                    maxes(2)
                    tail_norm(0)
                    dve.wait_ge(qk_mm, at(i, u, 3, 6))
                    qk_evac(1 - u, 2, bank[5])
                    t_evac(1)
                    maxes(3)
                    tail_maxes(1)
                    t_evac(2)
                    tail_inv(1)
                    tt_evac(0)
                    tail_norm(1)
                    t_evac(3)
                    tt_evac(1)
                    dve.wait_ge(exp_done, at(i, u, 16, 16))
                    nc.vector.reciprocal(rinv, rsum[u]).then_inc(rinv_done, 1)
                    dve.wait_ge(rinv_done, at(i, u, 1, 1))
                    dve.wait_ge(f_mm, at(i, u, 4, 4 + 4))
                    nc.vector.tensor_tensor(attn.rearrange("p (h d) -> p h d", d=HD), bank[4][:, :].rearrange("p (h d) -> p h d", d=HD),
                                            rinv.unsqueeze(2).to_broadcast([MAIN, HEADS, HD]), ALU.mult).then_inc(norm_done, 1)
                    maxes(4)
                    dve.wait_ge(tf_mm, at(i, u, 1, 1 + 1))
                    for h in range(QH):
                        nc.vector.tensor_copy(catT[32 * h:32 * h + 32, :, MAIN:SEQ],
                                              bank[5][32 * h:32 * h + 32, 0:QUADS * TR].rearrange("p (g h s) -> p g h s", g=QUADS, h=QH)[:, :, h, :]
                                              ).then_inc(tf_ev, 1)
                    maxes(5)
                    dve.wait_ge(o_mm, at(i, u, 1, 1 + 1))
                    here = hT[:, bass.ds(i * (2 * SEQ) + u * SEQ, SEQ)]
                    nc.vector.scalar_tensor_tensor(here, bank[4][:, 0:SEQ], out_b[:, :], here, ALU.add, ALU.add).then_inc(resid, 1)

        expert_w = region[:, :].rearrange("p (e w) -> p e w", w=EW)
        LATE = QZ_AT // EW
        early_w, late_w, bias_w = sem("early_w"), sem("late_w"), sem("bias_w")
        EARLY_W, LATE_W, BIAS_W = 32 * LATE, 32 * (ALL_EXPERTS - LATE), 2

        def w1_blocks(w, k):
            return w[:, k * 128:(k + 1) * 128]

        def w2_blocks(w, k):
            return w[:, HIDDEN + k * 128:HIDDEN + (k + 1) * 128]

        def weights_sp(sp):
            for u in range(2):
                sp.wait_ge(patch_mm[u], CHUNKS // 2)
            sp.wait_ge(fold_mm, QUADS + 3)
            for e in range(ALL_EXPERTS):
                if e == LATE:
                    sp.wait_ge(o_mm, IMAGES + 1)
                got = early_w if e < LATE else late_w
                w1, w2 = (se_w1[e, :, :], se_w2[e, :, :]) if e < SHARED else (re_w1[e - SHARED, :, :], re_w2[e - SHARED, :, :])
                sp.dma_start(expert_w[:, e, 0:HIDDEN], w1).then_inc(got, 16)
                sp.dma_start(expert_w[:, e, HIDDEN:2 * HIDDEN].rearrange("p (k h) -> p k h", k=FB),
                             w2.rearrange("(k p) h -> p k h", p=128)).then_inc(got, 16)

        TE = TILES * EXPERTS
        KEEP = 2 * TE // 2 + TILES * TOPK + 2 * DISPATCHED * TOPK + 2 * FILL_TILES + EXPERTS + 128
        wk[0] = 9600 - KEEP
        combine = carve(TE).rearrange("p (t e) -> p t e", e=EXPERTS)
        top_w = carve(TILES * TOPK).rearrange("p (t k) -> p t k", k=TOPK)
        slot_of = carve(DISPATCHED * TOPK).bitcast(I32).rearrange("p (t k) -> p t k", k=TOPK)
        row_of = carve(DISPATCHED * TOPK).bitcast(I32).rearrange("p (t k) -> p t k", k=TOPK)
        expert_of = carve(FILL_TILES).bitcast(I32)
        tile_iota = carve(FILL_TILES)
        e_iota = carve(EXPERTS)
        before = carve(64).bitcast(BF16)
        ones_b = carve(64).bitcast(BF16)
        assert wk[0] <= 9600, wk[0]
        wk[0] = 0
        logits = carve(TE).rearrange("p (t e) -> p t e", e=EXPERTS)
        hit = carve(TE).rearrange("p (t e) -> p t e", e=EXPERTS)
        slots = carve(TE).rearrange("p (t e) -> p t e", e=EXPERTS)
        counts = carve(TE).rearrange("p (e t) -> p e t", e=EXPERTS)
        running = logits.rearrange("p t e -> p (t e)").rearrange("p (e t) -> p e t", e=EXPERTS)
        chosen = carve(TE // 2).bitcast(BF16)
        top_flat = carve(TILES * 8)
        top_v = top_flat.rearrange("p (t k) -> p t k", k=8)
        top_i = carve(TILES * 8).rearrange("p (t k) -> p t k", k=8).bitcast(U32)
        top_f = carve(TILES * TOPK).rearrange("p (t k) -> p t k", k=TOPK)
        row1 = carve(TILES)
        row2 = carve(TILES)
        ends, starts, n_tiles, last_tile, tiles_f = (carve(EXPERTS) for _ in range(5))
        n_up, n_shift = (carve(EXPERTS).bitcast(I32) for _ in range(2))
        expert_f = top_flat[:, 0:FILL_TILES]
        assert wk[0] <= 9600 - KEEP, (wk[0], 9600 - KEEP)

        gate_mm, gate_v, gate_e, tables_ready, chosen_ready, rank_mm, gate_done = (sem(n) for n in (
            "gate_mm", "gate_v", "gate_e", "tables_ready", "chosen_ready", "rank_mm", "gate_done"))
        GB = 512 // EXPERTS
        GBANKS = -(-TILES // GB)
        CT = 4
        CGROUPS = -(-TILES // CT)
        GATE_TABLES = 9

        def gate_pe(pe):
            for u in range(2):
                pe.wait_ge(norm2.done[u], LCHUNKS // 2 + 1)
            for j in range(GBANKS):
                for t in range(j * GB, min((j + 1) * GB, TILES)):
                    last = nc.tensor.matmul(bank[4 + j][:, (t - j * GB) * EXPERTS:(t - j * GB + 1) * EXPERTS],
                                            xT[:, t * 128:(t + 1) * 128], gate_wT[:, :], start=True, stop=True)
                last.then_inc(gate_mm, 1)
            pe.wait_ge(tables_ready, GATE_TABLES)
            pe.wait_ge(chosen_ready, 1)
            for b, lhs in ((0, before), (3, ones_b)):
                for j in range(GBANKS):
                    n = min(GB, TILES - j * GB) * EXPERTS
                    last = nc.tensor.matmul(bank[b + j][:, 0:n], lhs, chosen[:, j * GB * EXPERTS:j * GB * EXPERTS + n],
                                            start=True, stop=True)
            last.then_inc(rank_mm, 1)

        def gate_pool(pool):
            pool.wait_ge(resid, IMAGES + 1)
            pool.wait_ge(o_mm, IMAGES + 1)
            nc.gpsimd.iota(e_iota, pattern=[[1, EXPERTS]], base=0, channel_multiplier=0,
                           allow_small_or_imprecise_dtypes=True).then_inc(tables_ready, 1)
            nc.gpsimd.iota(tile_iota, pattern=[[1, FILL_TILES]], base=0, channel_multiplier=0,
                           allow_small_or_imprecise_dtypes=True).then_inc(tables_ready, 1)
            nc.gpsimd.iota(row_of, pattern=[[128 * TOPK, DISPATCHED], [1, TOPK]], base=0,
                           channel_multiplier=TOPK).then_inc(tables_ready, 1)
            nc.gpsimd.iota(slot_of[:, TILES:DISPATCHED, :], pattern=[[0, DISPATCHED - TILES], [1, TOPK]], base=SLOTS,
                           channel_multiplier=TOPK).then_inc(tables_ready, 1)
            nc.gpsimd.memset(ones_b, 1.0).then_inc(tables_ready, 1)
            nc.gpsimd.memset(before, 1.0).then_inc(tables_ready, 1)
            pool.wait_ge(tables_ready, 6)
            nc.gpsimd.affine_select(out=before, in_=before, compare_op=ALU.is_gt, fill=0.0, base=0,
                                    pattern=[[1, 128]], channel_multiplier=-1).then_inc(tables_ready, 1)
            b1 = b1T[:, :].rearrange("p (e k) -> p e k", k=FB)
            nc.gpsimd.tensor_copy(expert_w[:, SHARED:, 2 * HIDDEN:], b1[:, 0:EXPERTS, :]).then_inc(tables_ready, 1)
            nc.gpsimd.tensor_copy(expert_w[:, 0:SHARED, 2 * HIDDEN:], b1[:, EXPERTS:, :]).then_inc(tables_ready, 1)

        def gate_dve(dve):
            n = [0]

            def link(ins):
                n[0] += 1
                ins.then_inc(gate_v, 1)
                dve.wait_ge(gate_v, n[0])
            for j in range(GBANKS):
                dve.wait_ge(gate_mm, j + 1)
                m = min(GB, TILES - j * GB)
                link(nc.vector.tensor_copy(logits[:, j * GB:j * GB + m, :],
                                           bank[4 + j][:, 0:m * EXPERTS].rearrange("p (t e) -> p t e", e=EXPERTS)))
            bc = [128, TILES, EXPERTS]
            link(nc.vector.tensor_reduce(row1, logits, AX.X, ALU.max))
            link(nc.vector.tensor_tensor(logits, logits, row1.unsqueeze(2).to_broadcast(bc), ALU.subtract))
            dve.wait_ge(gate_e, 1)
            link(nc.vector.tensor_reduce(row1, logits, AX.X, ALU.add))
            link(nc.vector.reciprocal(row2, row1))
            link(nc.vector.tensor_tensor(logits, logits, row2.unsqueeze(2).to_broadcast(bc), ALU.mult))
            for t in range(TILES):
                n[0] += 1
                nc.vector.max(top_v[:, t, :], logits[:, t, :]).then_inc(gate_v, 1)
            dve.wait_ge(gate_v, n[0])
            for t in range(TILES):
                n[0] += 1
                nc.vector.max_index(top_i[:, t, :], top_v[:, t, :], logits[:, t, :]).then_inc(gate_v, 1)
            dve.wait_ge(gate_v, n[0])
            link(nc.vector.tensor_tensor(top_w, top_v[:, :, 0:TOPK], top_v[:, :, 0:1].to_broadcast([128, TILES, TOPK]), ALU.subtract))
            dve.wait_ge(gate_e, 2)
            link(nc.vector.tensor_reduce(row1, top_w, AX.X, ALU.add))
            link(nc.vector.reciprocal(row2, row1))
            link(nc.vector.tensor_tensor(top_w, top_w, row2.unsqueeze(2).to_broadcast([128, TILES, TOPK]), ALU.mult))
            link(nc.vector.tensor_copy(top_f, top_i[:, :, 0:TOPK]))
            dve.wait_ge(tables_ready, GATE_TABLES)

            def hits(k):
                link(nc.vector.tensor_tensor(hit, top_f[:, :, k:k + 1].to_broadcast(bc), e_iota.unsqueeze(1).to_broadcast(bc), ALU.is_equal))
            for k in range(TOPK):
                hits(k)
                tgt = combine if k == 0 else hit
                link(nc.vector.tensor_tensor(tgt, hit, top_w[:, :, k:k + 1].to_broadcast(bc), ALU.mult))
                if k:
                    link(nc.vector.tensor_tensor(combine, combine, hit, ALU.add))
            nc.vector.tensor_scalar(chosen.rearrange("p (t e) -> p t e", e=EXPERTS), combine, 0.0, None, ALU.is_gt).then_inc(chosen_ready, 1)
            dve.wait_ge(rank_mm, 1)
            for j in range(GBANKS):
                m = min(GB, TILES - j * GB)
                link(nc.vector.tensor_copy(counts[:, :, j * GB:j * GB + m].rearrange("p e t -> p t e"),
                                           bank[3 + j][:, 0:m * EXPERTS].rearrange("p (t e) -> p t e", e=EXPERTS)))
            flat = counts.rearrange("p e t -> p (e t)")
            link(nc.vector.tensor_tensor_scan(running.rearrange("p e t -> p (e t)"), flat, flat, 0.0, ALU.add, ALU.max))
            ends3, starts3 = ends.unsqueeze(2), starts.unsqueeze(2)
            link(nc.vector.memset(starts, 0.0))
            link(nc.vector.tensor_copy(starts3[:, 1:EXPERTS, :], running[:, 0:EXPERTS - 1, TILES - 1:TILES]))
            link(nc.vector.tensor_copy(ends3, running[:, :, TILES - 1:TILES]))
            link(nc.vector.tensor_tensor(n_tiles, ends, starts, ALU.subtract))
            link(nc.vector.tensor_scalar(n_up, n_tiles, 127.0, None, ALU.add))
            link(nc.vector.tensor_scalar(n_shift, n_up, 7, None, ALU.arith_shift_right))
            link(nc.vector.tensor_copy(tiles_f, n_shift))
            link(nc.vector.tensor_tensor_scan(last_tile, tiles_f, tiles_f, 0.0, ALU.add, ALU.max))
            link(nc.vector.tensor_tensor(running, running, counts, ALU.subtract))
            link(nc.vector.tensor_tensor(n_tiles, last_tile, tiles_f, ALU.subtract))
            link(nc.vector.scalar_tensor_tensor(starts, n_tiles, 128.0, starts, ALU.mult, ALU.subtract))
            link(nc.vector.tensor_tensor(running, running, starts3.to_broadcast([128, EXPERTS, TILES]), ALU.add))
            for j in range(GBANKS):
                m = min(GB, TILES - j * GB)
                link(nc.vector.tensor_tensor(slots[:, j * GB:j * GB + m, :],
                                             bank[j][:, 0:m * EXPERTS].rearrange("p (t e) -> p t e", e=EXPERTS),
                                             running[:, :, j * GB:j * GB + m].rearrange("p e t -> p t e"), ALU.add))
            for k in range(TOPK):
                hits(k)
                link(nc.vector.tensor_tensor(hit, hit, slots, ALU.mult))
                link(nc.vector.tensor_reduce(row1, hit, AX.X, ALU.add))
                link(nc.vector.tensor_copy(slot_of[:, 0:TILES, k:k + 1], row1.unsqueeze(2)))
            link(nc.vector.memset(expert_f, float(SHARED)))
            for e in range(EXPERTS - 1):
                link(nc.vector.scalar_tensor_tensor(expert_f, tile_iota, last_tile[:, e:e + 1], expert_f, ALU.is_ge, ALU.add))
            link(nc.vector.tensor_copy(expert_of, expert_f))
            nc.vector.memset(row1, 0.0).then_inc(gate_done, 1)

        def gate_act(act):
            act.wait_ge(gate_v, GBANKS + 2)
            nc.scalar.activation(logits, logits, ACT.Exp).then_inc(gate_e, 1)
            act.wait_ge(gate_v, GBANKS + 5 + 2 * TILES + 1)
            nc.scalar.activation(top_w, top_w, ACT.Exp).then_inc(gate_e, 1)

        wk[0] = 0
        x_pass = [carve(PASS) for _ in range(2)]
        act_s = [carve(FB * PASS).rearrange("p (k s) -> p k s", k=FB) for _ in range(SHARED)]
        send = [carve(TOPK * ROW).rearrange("p (k c) -> p k c", k=TOPK) for _ in range(2)]
        send_to = [carve(TOPK).bitcast(U32) for _ in range(2)]
        assert wk[0] <= 9600 - KEEP
        pass_in, sh_mm, sh_act, sh_out, sh_add = (sem(n) for n in ("pass_in", "sh_mm", "sh_act", "sh_out", "sh_add"))
        turn_mm = [sem(f"turn_mm{a}") for a in range(2)]
        send_row = [sem(f"send_row{a}") for a in range(2)]
        sent = [sem(f"sent{a}") for a in range(2)]
        HIDDENS = SHARED * FB

        def shared_act(act):
            act.wait_ge(gate_done, 1)
            with act.Fori(0, PASSES // 2) as i:
                for v in range(2):
                    act.wait_ge(sh_mm, i * (2 * HIDDENS) + (v + 1) * HIDDENS)
                    nc.scalar.copy(x_pass[v], xT[:, bass.ds(i * (2 * PASS) + v * PASS, PASS)]).then_inc(pass_in, 1)
                    for e in range(SHARED):
                        for k in range(FB):
                            act.wait_ge(sh_mm, i * (2 * HIDDENS) + (v * HIDDENS + e * FB + k + 1 + 2 * HIDDENS))
                            if k == 0:
                                act.wait_ge(sh_out, i * (2 * SHARED) + (v * SHARED + e + 1))
                            nc.scalar.activation(act_s[e][:, k, :], bank[k][:, 0:PASS], ACT.Gelu,
                                                 bias=b1T[:, (EXPERTS + e) * FB + k:(EXPERTS + e) * FB + k + 1]).then_inc(sh_act, 1)

        def shared_pe(pe):
            pe.wait_ge(early_w, EARLY_W)
            with pe.Fori(0, PASSES // 2) as i:
                for v in range(2):
                    pe.wait_ge(pass_in, i * 2 + v + 1)
                    for a in range(2):
                        pe.wait_ge(send_row[a], i * 6 + (3 * v + 3))
                        nc.tensor.transpose(bank[6 + a][:, 0:128], x_pass[v][:, a * 128:(a + 1) * 128], ident[:, :]).then_inc(turn_mm[a], 1)
                    for e in range(SHARED):
                        for k in range(FB):
                            pe.wait_ge(sh_act, i * (2 * HIDDENS) + (v * HIDDENS + e * FB + k + 1))
                            nc.tensor.matmul(bank[k][:, 0:PASS], w1_blocks(expert_w[:, e, :], k), x_pass[v],
                                             start=True, stop=True).then_inc(sh_mm, 1)
                    pe.wait_ge(sh_add, i * 2 + v + 1)
                    for e in range(SHARED):
                        for k in range(FB):
                            pe.wait_ge(sh_act, i * (2 * HIDDENS) + (v * HIDDENS + e * FB + k + 1 + FB))
                            last = nc.tensor.matmul(bank[4 + v][:, 0:PASS], w2_blocks(expert_w[:, e, :], k), act_s[e][:, k, :],
                                                    start=(e == 0 and k == 0), stop=(e == SHARED - 1 and k == FB - 1))
                        last.then_inc(sh_out, 1)

        def shared_dve(dve):
            dve.sem_inc(sh_mm, 2 * HIDDENS)
            dve.sem_inc(sh_act, FB)
            dve.sem_inc(sh_out, SHARED)
            dve.sem_inc(sh_add, 2)
            for a in range(2):
                dve.sem_inc(send_row[a], 3)
            def turn(i, first):
                for v in range(2):
                    for a in range(2):
                        tile = bass.ds(i * 4 + (2 * v + a), 1)
                        if not first or v:
                            dve.wait_ge(sent[a], i * (2 * 16 * TOPK) + v * (16 * TOPK))
                        dve.wait_ge(turn_mm[a], i * 2 + v + 1)
                        nc.vector.tensor_copy(send[a][:, :, 0:D], bank[6 + a][:, 0:128].unsqueeze(1).to_broadcast([128, TOPK, D])).then_inc(send_row[a], 1)
                        nc.vector.tensor_copy(send[a].bitcast(I32)[:, :, D:ROW].rearrange("p k c -> p c k"), row_of[:, tile, :]).then_inc(send_row[a], 1)
                        nc.vector.tensor_copy(send_to[a].unsqueeze(1), slot_of[:, tile, :]).then_inc(send_row[a], 1)
                    dve.wait_ge(sh_out, i * (2 * SHARED) + ((v + 1) * SHARED + SHARED))
                    here = hT[:, bass.ds(i * (2 * PASS) + v * PASS, PASS)]
                    nc.vector.scalar_tensor_tensor(here, bank[4 + v][:, 0:PASS], 1.0 / SHARED, here, ALU.mult, ALU.add).then_inc(sh_add, 1)
            turn(0, True)
            with dve.Fori(1, PASSES // 2) as i:
                turn(i, False)

        def dispatch_pool(pool):
            for r in range(2):
                pool.wait_ge(fill_out[r], FILL_OUT)
            with pool.Fori(0, PASSES // 2) as i:
                for v in range(2):
                    for a in range(2):
                        pool.wait_ge(send_row[a], i * 6 + (3 * v + 6))
                        settle(pool)
                        for k in range(TOPK):
                            nc.gpsimd.indirect_dma_start(slot_rows, bass.IndirectOffsetOnAxis(ap=send_to[a][:, k:k + 1], axis=0),
                                                         send[a][:, k, :], None).then_inc(sent[a], 16)
        SENT = 16 * TOPK * PASSES

        xk = [0]

        def carve_x(n, parts=128):
            a = xT[0:parts, xk[0]:xk[0] + n]
            xk[0] += n
            return a
        slot_x = [carve_x(ROW) for _ in range(STEPS)]
        slot_xT = [carve_x(128) for _ in range(2)]
        tile_w = [carve_x(EW) for _ in range(3)]
        act_r = [carve_x(FB * 128).rearrange("p (k s) -> p k s", k=FB) for _ in range(2)]
        y_row = [carve_x(D) for _ in range(STEPS)]
        y_to = [carve_x(1).bitcast(U32) for _ in range(STEPS)]
        assert xk[0] <= TOKENS
        routed_rows = nc.dram_tensor("routed_rows", (ASSIGNED + SLOTS, D), F32, kind="Internal").ap()
        slot_in = [sem(f"slot_in{r}") for r in range(STEPS)]
        y_sent = [sem(f"y_sent{r}") for r in range(STEPS)]
        turned, turn_ev, to_ready, w_ready, r_mm, r_act, r_out, r_ev = (sem(n) for n in (
            "turned", "turn_ev", "to_ready", "w_ready", "r_mm", "r_act", "r_out", "r_ev"))
        TURNS = SLOT_TILES // STEPS

        def routed_sp(sp):
            def load(r, first):
                sp.dma_start(slot_x[r], slot_rows[bass.ds(first * 128, 128), :]).then_inc(slot_in[r], 16)
            for a in range(2):
                sp.wait_ge(sent[a], SENT)
            sp.wait_ge(pass_in, PASSES)
            for r in range(STEPS):
                load(r, r)
            with sp.Fori(0, TURNS - 1) as i:
                for r in range(STEPS):
                    sp.wait_ge(turn_ev, i * STEPS + r + 1)
                    sp.wait_ge(to_ready, i * STEPS + r + 1)
                    load(r, i * STEPS + (STEPS + r))
            for r in range(2):
                sp.wait_ge(turn_ev, (TURNS - 1) * STEPS + r + 1)
                sp.wait_ge(to_ready, (TURNS - 1) * STEPS + r + 1)
                load(r, SLOT_TILES + r)

        def routed_pe(pe):
            def turn(c, got):
                pe.wait_ge(slot_in[c % STEPS], got)
                nc.tensor.transpose(bank[c % 2][:, 0:128], slot_x[c % STEPS][:, 0:D], ident[:, :]).then_inc(turned, 1)

            def hidden(c):
                for k in range(FB):
                    last = nc.tensor.matmul(bank[2 + c % 2][:, k * 128:(k + 1) * 128], w1_blocks(tile_w[c % 3], k), slot_xT[c % 2],
                                            start=True, stop=True)
                last.then_inc(r_mm, 1)
            turn(0, 16)
            turn(1, 16)
            pe.wait_ge(turn_ev, 1)
            pe.wait_ge(w_ready, 1)
            hidden(0)
            with pe.Fori(0, TURNS) as i:
                for u in range(STEPS):
                    pe.wait_ge(turn_ev, i * STEPS + u + 1)
                    turn(u + 2, (i + (u + 2) // STEPS) * 16 + 16)
                    pe.wait_ge(turn_ev, i * STEPS + u + 2)
                    pe.wait_ge(w_ready, i * STEPS + u + 2)
                    pe.wait_ge(r_act, i * (STEPS * FB) + (u * FB + FB))
                    hidden(u + 1)
                    pe.wait_ge(r_ev, i * STEPS + u + 1)
                    for k in range(FB):
                        pe.wait_ge(r_act, i * (STEPS * FB) + (u * FB + k + 1 + FB))
                        last = nc.tensor.matmul(bank[4 + u % 2][:, 0:D], act_r[u % 2][:, k, :], w2_blocks(tile_w[u % 3], k),
                                                start=(k == 0), stop=(k == FB - 1))
                    last.then_inc(r_out, 1)

        def routed_act(act):
            with act.Fori(0, TURNS) as i:
                for u in range(STEPS):
                    act.wait_ge(r_mm, i * STEPS + u + 1)
                    act.wait_ge(r_out, i * STEPS + u + 1)
                    for k in range(FB):
                        nc.scalar.activation(act_r[u % 2][:, k, :], bank[2 + u % 2][:, k * 128:(k + 1) * 128], ACT.Gelu,
                                             bias=tile_w[u % 3][:, 2 * HIDDEN + k:2 * HIDDEN + k + 1]).then_inc(r_act, 1)

        def routed_dve(dve):
            dve.sem_inc(r_act, FB)
            dve.sem_inc(r_ev, 2)
            dve.sem_inc(r_out, 2)
            dve.wait_ge(late_w, LATE_W)

            def weights_of(c, tile):
                e = dve.value_load(expert_of[0:1, tile], min_val=0, max_val=ALL_EXPERTS - 1)
                nc.vector.tensor_copy(tile_w[c % 3].unsqueeze(1), expert_w[:, bass.ds(e, 1), :]).then_inc(w_ready, 1)

            def turn_out(c):
                nc.vector.tensor_copy(slot_xT[c % 2], bank[c % 2][:, 0:128]).then_inc(turn_ev, 1)
            for c in range(2):
                weights_of(c, slice(c, c + 1))
                dve.wait_ge(turned, c + 1)
                turn_out(c)
            def steps(i, first):
                for u in range(STEPS):
                    dve.wait_ge(r_out, i * STEPS + u + 2)
                    weights_of(u + 2, bass.ds(i * STEPS + (u + 2), 1))
                    dve.wait_ge(turned, i * STEPS + u + 3)
                    dve.wait_ge(r_mm, i * STEPS + u + 1)
                    turn_out(u + 2)
                    if not first:
                        dve.wait_ge(y_sent[u], i * 16)
                    nc.vector.tensor_copy(y_to[u], slot_x[u].bitcast(U32)[:, D:ROW]).then_inc(to_ready, 1)
                    dve.wait_ge(r_out, i * STEPS + u + 3)
                    nc.vector.tensor_copy(y_row[u], bank[4 + u % 2][:, 0:D]).then_inc(r_ev, 1)
            steps(0, True)
            with dve.Fori(1, TURNS) as i:
                steps(i, False)

        def routed_pool(pool):
            with pool.Fori(0, TURNS) as i:
                for u in range(STEPS):
                    pool.wait_ge(to_ready, i * STEPS + u + 1)
                    pool.wait_ge(r_ev, i * STEPS + u + 3)
                    settle(pool)
                    nc.gpsimd.indirect_dma_start(routed_rows, bass.IndirectOffsetOnAxis(ap=y_to[u], axis=0),
                                                 y_row[u], None).then_inc(y_sent[u], 16)

        xk[0] = 0
        ZR, OR = 3, 4
        z_in = [carve_x(CT * TOPK * D).rearrange("p (t k d) -> p t k d", t=CT, k=TOPK) for _ in range(ZR)]
        obuf = [carve_x(CT * D).rearrange("p (t d) -> p t d", t=CT) for _ in range(OR)]
        combT = [carve_x(CT * 128, ALL_EXPERTS) for _ in range(2)]
        z_got = [sem(f"z_got{r}") for r in range(ZR)]
        y_out = [sem(f"y_out{r}") for r in range(OR)]
        comb_const, comb_mm, comb_ev, y_mm, y_add = (sem(n) for n in ("comb_const", "comb_mm", "comb_ev", "y_mm", "y_add"))
        out_rows = out.rearrange("b s d -> (b s) d")
        choices = routed_rows.rearrange("(n k) d -> n (k d)", k=TOPK)

        def group(j):
            return range(j * CT, min((j + 1) * CT, TILES))

        def final_pe(pe):
            def weights_turned(j):
                if j >= 2:
                    pe.wait_ge(comb_ev, j - 1)
                for t in group(j):
                    last = nc.tensor.transpose(bank[2 + j % 2][0:EXPERTS, (t - j * CT) * 128:(t - j * CT + 1) * 128],
                                               combine[:, t, :], ident[:, :])
                last.then_inc(comb_mm, 1)
            pe.wait_ge(sh_add, PASSES + 2)
            pe.wait_ge(r_act, FB * (SLOT_TILES + 1))
            weights_turned(0)
            for j in range(CGROUPS):
                if j < CGROUPS - 1:
                    weights_turned(j + 1)
                pe.wait_ge(comb_ev, j + 1)
                if j >= 2:
                    pe.wait_ge(y_add, j - 1)
                for t in group(j):
                    at_t = slice((t - j * CT) * 128, (t - j * CT + 1) * 128)
                    nc.tensor.matmul(bank[j % 2][:, at_t], hT[:, t * 128:(t + 1) * 128], ident[:, :], start=True, stop=False)
                    last = nc.tensor.matmul(bank[j % 2][:, at_t], combT[j % 2][:, at_t], b2_rows[:, :], start=False, stop=True)
                last.then_inc(y_mm, 1)

        def final_act(act):
            act.wait_ge(comb_const, 2)
            for j in range(CGROUPS):
                act.wait_ge(comb_mm, j + 1)
                if j >= 2:
                    act.wait_ge(y_mm, j - 1)
                m = len(group(j)) * 128
                nc.scalar.copy(combT[j % 2][0:EXPERTS, 0:m], bank[2 + j % 2][0:EXPERTS, 0:m]).then_inc(comb_ev, 1)

        y_step = sem("y_step")

        def final_dve(dve):
            dve.wait_ge(r_out, SLOT_TILES + 2)
            for u in range(STEPS):
                dve.wait_ge(y_sent[u], 16 * TURNS)
            for r in range(2):
                nc.vector.memset(combT[r], 1.0 / SHARED).then_inc(comb_const, 1)
            done = 0
            for j in range(CGROUPS):
                dve.wait_ge(y_mm, j + 1)
                dve.wait_ge(z_got[j % ZR], 16 * (j // ZR + 1))
                if j >= OR:
                    dve.wait_ge(y_out[j % OR], 16 * (j // OR))
                for k in range(TOPK):
                    if k:
                        dve.wait_ge(y_step, done)
                    for t in group(j):
                        a = t - j * CT
                        o = obuf[j % OR][:, a, :]
                        base = o if k else bank[j % 2][:, a * 128:(a + 1) * 128]
                        ins = nc.vector.scalar_tensor_tensor(o, z_in[j % ZR][:, a, k, :], top_w[:, t, k:k + 1], base, ALU.mult, ALU.add)
                        if k < TOPK - 1:
                            ins.then_inc(y_step, 1)
                            done += 1
                ins.then_inc(y_add, 1)

        def final_sp(sp):
            def load(j):
                n = len(group(j))
                sp.dma_start(z_in[j % ZR][:, 0:n, :, :].rearrange("p t k d -> p t (k d)"),
                             choices[j * CT * 128:(j * CT + n) * 128, :].rearrange("(t p) c -> p t c", p=128)).then_inc(z_got[j % ZR], 16)
            for u in range(STEPS):
                sp.wait_ge(y_sent[u], 16 * TURNS)
            sp.wait_ge(r_out, SLOT_TILES + 2)
            for j in range(ZR):
                load(j)
            for j in range(CGROUPS):
                n = len(group(j))
                sp.wait_ge(y_add, j + 1)
                sp.dma_start(out_rows[j * CT * 128:(j * CT + n) * 128, :].rearrange("(t p) d -> p t d", p=128),
                             obuf[j % OR][:, 0:n, :]).then_inc(y_out[j % OR], 16)
                if j + ZR < CGROUPS:
                    load(j + ZR)
            for r in range(OR):
                sp.wait_ge(y_out[r], 16 * (-(-(CGROUPS - r) // OR)))


        block = ctx.enter_context(nc.Block())

        @block.sync
        def _(sp):
            setup_loads(sp)
            tree_sp(sp)
            patch_sp(sp)
            weights_sp(sp)
            routed_sp(sp)
            final_sp(sp)

        @block.gpsimd
        def _(pool):
            setup_pool(pool)
            attn_masks_pool(pool)
            fill_pool(pool)
            norm1.pool(pool)
            attn_pool(pool)
            gate_pool(pool)
            norm2.pool(pool)
            dispatch_pool(pool)
            routed_pool(pool)

        @block.scalar
        def _(act):
            tree_act(act)
            norm1.act(act)
            attn_act(act)
            norm2.act(act)
            gate_act(act)
            shared_act(act)
            routed_act(act)
            final_act(act)

        @block.vector
        def _(dve):
            setup_dve_rows(dve)
            tree_rows_dve(dve)
            setup_dve(dve)
            tree_dve(dve)
            patch_dve(dve)
            dve.wait_ge(cls_done, 1)
            norm1.dve(dve)
            attn_dve(dve)
            norm2.dve(dve)
            gate_dve(dve)
            shared_dve(dve)
            routed_dve(dve)
            final_dve(dve)

        @block.tensor
        def _(pe):
            setup_pe(pe)
            tree_pe(pe)
            patch_pe(pe)
            for u in range(2):
                pe.wait_ge(tree_h[u], IMAGES // (2 * HALF) + 1)
                pe.wait_ge(patch_ev[u], CHUNKS // 2 + 1)
            pe.wait_ge(cls_done, 1)
            norm1.pe(pe)
            attn_pe(pe)
            pe.wait_ge(resid, IMAGES + 1)
            norm2.pe(pe)
            gate_pe(pe)
            shared_pe(pe)
            routed_pe(pe)
            final_pe(pe)


_INS = ['x', 'x_txt', 'L0_tok_W', 'L0_tok_b', 'L0_tok_class_token', 'L0_tok_pos_embed', 'L0_txt_p', 'L0_attn_Wl',
        'L0_attn_bl', 'L0_attn_Wq', 'L0_attn_Wk', 'L0_attn_Wv', 'L0_attn_Wo', 'L0_attn_bo', 'L0_ffn_gate_w',
        'L0_ffn_re_w1', 'L0_ffn_re_b1', 'L0_ffn_re_w2', 'L0_ffn_re_b2', 'L0_ffn_se_w1', 'L0_ffn_se_b1',
        'L0_ffn_se_w2', 'L0_ffn_se_b2']


def kernel(**inputs):
    import numpy as _np
    import concourse.bacc as _bacc
    from concourse import mybir as _mybir
    from concourse.bass_utils import run_bass_kernel_spmd as _run

    nc = _bacc.Bacc("TRN2", target_bir_lowering=False, num_devices=1)
    arrays, args = {}, []
    for name in _INS:
        a = _np.ascontiguousarray(inputs[name])
        arrays[f"in_{name}_dram"] = a
        args.append(nc.dram_tensor(f"in_{name}_dram", a.shape, _mybir.dt.from_np(a.dtype), kind="ExternalInput").ap())
    args.append(nc.dram_tensor("out_0_dram", (IMAGES, SEQ, D), _mybir.dt.float32, kind="ExternalOutput").ap())
    build(nc, *args)
    r = _run(nc, [arrays], core_ids=[0])
    return r.results[0]["out_0_dram"]
```

```python
import concourse.bass as bass
from concourse import mybir
from contextlib import ExitStack

F32 = mybir.dt.float32
BF16 = mybir.dt.bfloat16
I32 = mybir.dt.int32
U32 = mybir.dt.uint32
ALU = mybir.AluOpType
ACT = mybir.ActivationFunctionType
AX = mybir.AxisListType

IMAGES, CHANNELS, SIDE = 64, 3, 224
GRID, PATCH = 8, 28
D = 128
PATCHES = GRID * GRID
TEXT = 77
SEQ = 1 + PATCHES + TEXT
TOKENS = IMAGES * SEQ
ROWS = CHANNELS * PATCH
PE_ROWS = 96
END_TOKEN = 2
HEADS, HD = 16, 32
QUADS, QH = 4, 4
MAIN = 128
TAIL = SEQ - MAIN
EXPERTS, SHARED, HIDDEN, TOPK = 16, 2, 512, 4
ALL_EXPERTS = EXPERTS + SHARED
FB = HIDDEN // 128
TILES = TOKENS // 128
PASS = 2 * 128
PASSES = -(-TOKENS // PASS)
PADDED = PASSES * PASS
DISPATCHED = PADDED // 128
STEPS = 6
SLOT_TILES = -(-(TOKENS * TOPK // 128 + EXPERTS) // STEPS) * STEPS
FILL_TILES = SLOT_TILES + 4
FILLS = 16
SLOTS = FILL_TILES * 128
ASSIGNED = PADDED * TOPK
ROW = D + 1
MASKED = -1e30
LN_EPS = 1e-5
TREE_LEVELS = 6


def build(nc, x, x_txt, tok_W, tok_b, tok_cls, tok_pos, txt_p, Wl, bl, Wq, Wk, Wv, Wo, bo,
          gate_w, re_w1, re_b1, re_w2, re_b2, se_w1, se_b1, se_w2, se_b2, out):
    ctx = ExitStack()
    with ctx:
        def sb(name, shape, dt=F32):
            return ctx.enter_context(nc.sbuf_tensor(name, shape, dt))

        def sem(name):
            return ctx.enter_context(nc.semaphore(name))

        bank = [ctx.enter_context(nc.psum_tensor(f"bank{i}", [128, 512], F32)) for i in range(8)]

        hT = sb("hT", [D, PADDED])
        xT = sb("xT", [D, TOKENS + 2 * SEQ])
        EW = 2 * HIDDEN + FB
        W_ELEMS = ALL_EXPERTS * EW
        patch_wT = xT[0:PE_ROWS, 5000:5000 + PATCH * D].rearrange("r (k d) -> r k d", k=PATCH)
        region = sb("region", [128, W_ELEMS])
        ident = sb("ident", [128, 128])
        identb = sb("identb", [128, 128], BF16)
        centre = sb("centre", [128, 128])
        mean_of = sb("mean_of", [128, 128])
        eps_col = sb("eps_col", [128, 1])
        posT = sb("posT", [D, 1 + PATCHES])
        patch_b = sb("patch_b", [D, 1])
        poly = sb("poly", [D, 1])
        qkv_w = sb("qkv_w", [D, 3, HEADS, HD])
        qkv_b = sb("qkv_b", [128, 3 * QUADS])
        woT = sb("woT", [128, QUADS, D])
        out_b = sb("out_b", [D, 1])
        head_rows = sb("head_rows", [128, QH])
        gate_wT = sb("gate_wT", [D, EXPERTS])
        b1T = sb("b1T", [128, ALL_EXPERTS * FB])
        b2_rows = sb("b2_rows", [ALL_EXPERTS, D])
        work = sb("work", [128, 9600])

        CHUNK_IMAGES = 4
        XT = CHUNK_IMAGES * GRID * SIDE
        x_tile = [region[0:PE_ROWS, u * XT:(u + 1) * XT] for u in range(2)]
        o = 2 * XT
        wl_sb = region[:, o:o + HEADS * D].rearrange("p (h i) -> p h i", h=HEADS)
        o += HEADS * D
        wqkv_sb = region[:, o:o + HEADS * 3 * HD].rearrange("p (h c d) -> p h c d", h=HEADS, c=3)
        o += HEADS * 3 * HD
        wo_sb = region[:, o:o + HEADS * HD]
        assert o + HEADS * HD <= W_ELEMS

        tokens_in, patchw_in, attnw_in, ffnb_in = (sem(n) for n in ("tokens_in", "patchw_in", "attnw_in", "ffnb_in"))
        pool_const = sem("pool_const")
        dve_const = sem("dve_const")
        zero_rows = sem("zero_rows")
        setup_mm = sem("setup_mm")
        setup_ev = sem("setup_ev")
        fold_mm = sem("fold_mm")
        fold_ev = sem("fold_ev")

        passed = sem("passed")

        def settle(eng):
            eng.sem_inc(passed, 1)

        w_raw = hT[:, 0:CHANNELS * PATCH * PATCH]
        small = hT[:, 2400:2400 + 1024]
        pos_raw = small[0:1 + PATCHES, 0:128]
        cls_raw = small[0:1, 128:256]
        bl_raw = small[0:HEADS, 256:384]
        gate_raw = small[0:EXPERTS, 384:512]
        b1_raw = small[0:ALL_EXPERTS * FB, 512:640]
        blT = small[:, 768:784]
        clsT_src = small[0:1, 800:928]
        bo_col = sb("bo_col", [D, 1])
        p_row = sb("p_row", [1, 1])
        poly_row = sb("poly_row", [1, D])
        posc = sb("posc", [D, 2])

        def setup_loads(sp):
            sp.dma_start(tok_i[:, :], x_txt).then_inc(tokens_in, 16)
            sp.dma_start(p_row[:, :], txt_p.rearrange("(a n) -> a n", a=1)).then_inc(tokens_in, 16)
            sp.dma_start(w_raw, tok_W).then_inc(patchw_in, 16)
            sp.dma_start(pos_raw, tok_pos).then_inc(patchw_in, 16)
            sp.dma_start(cls_raw, tok_cls).then_inc(patchw_in, 16)
            sp.dma_start(patch_b[:, :], tok_b.rearrange("(p a) -> p a", a=1)).then_inc(patchw_in, 16)
            sp.dma_start(wl_sb, Wl.rearrange("h o i -> o h i")).then_inc(attnw_in, 16)
            for c, w in enumerate((Wq, Wk, Wv)):
                sp.dma_start(wqkv_sb[:, :, c, :], w.rearrange("h i d -> i h d")).then_inc(attnw_in, 16)
            sp.dma_start(wo_sb, Wo).then_inc(attnw_in, 16)
            sp.dma_start(bl_raw, bl).then_inc(attnw_in, 16)
            sp.dma_start(bo_col[:, :], bo.rearrange("(p a) -> p a", a=1)).then_inc(attnw_in, 16)
            sp.dma_start(gate_raw, gate_w).then_inc(ffnb_in, 16)
            sp.dma_start(b1_raw[0:EXPERTS * FB, :], re_b1.rearrange("e (f p) -> (e f) p", p=128)).then_inc(ffnb_in, 16)
            sp.dma_start(b1_raw[EXPERTS * FB:ALL_EXPERTS * FB, :],
                         se_b1.rearrange("e (f p) -> (e f) p", p=128)).then_inc(ffnb_in, 16)
            sp.dma_start(b2_rows[0:EXPERTS, :], re_b2).then_inc(ffnb_in, 16)
            sp.dma_start(b2_rows[EXPERTS:ALL_EXPERTS, :], se_b2).then_inc(ffnb_in, 16)

        def setup_pool(pool):
            nc.gpsimd.memset(ident[:, :], 0.0).then_inc(pool_const, 1)
            pool.wait_ge(pool_const, 1)
            nc.gpsimd.affine_select(out=ident[:, :], in_=ident[:, :], compare_op=ALU.not_equal, fill=1.0,
                                    base=0, pattern=[[-1, 128]], channel_multiplier=1).then_inc(pool_const, 1)
            nc.gpsimd.memset(mean_of[:, :], 1.0 / D).then_inc(pool_const, 1)
            nc.gpsimd.memset(eps_col[:, :], LN_EPS).then_inc(pool_const, 1)
            pool.wait_ge(pool_const, 4)
            nc.gpsimd.tensor_copy(identb[:, :], ident[:, :]).then_inc(pool_const, 1)
            nc.gpsimd.tensor_tensor(centre[:, :], ident[:, :], mean_of[:, :], ALU.subtract).then_inc(pool_const, 1)
            pool.wait_ge(pool_const, POOL_CONST)
            nc.gpsimd.memset(xT[64:PE_ROWS, 5000:5000 + PATCH * D], 0.0).then_inc(zero_rows, 1)
            pool.wait_ge(zero_rows, 1)
            nc.gpsimd.memset(region[64:PE_ROWS, 0:2 * XT], 0.0).then_inc(zero_rows, 1)
            pool.wait_ge(zero_rows, 2)
        POOL_CONST = 6

        W_BANKS = PATCH // 4

        def setup_pe(pe):
            pe.wait_ge(pool_const, POOL_CONST)
            pe.wait_ge(patchw_in, 64)
            wv = w_raw.rearrange("p (r c) -> p c r", c=PATCH)
            for j in range(W_BANKS):
                for k in range(4):
                    last = nc.tensor.transpose(bank[j][0:ROWS, k * 128:(k + 1) * 128], wv[:, 4 * j + k, :], ident[:, :])
                last.then_inc(setup_mm, 1)
            pe.wait_ge(dve_const, SETUP_ROWS)
            nc.tensor.transpose(bank[7][:, 0:65], pos_raw, ident[0:65, 0:65])
            nc.tensor.transpose(bank[7][:, 65:66], clsT_src, ident[0:1, 0:1])
            nc.tensor.transpose(bank[7][:, 66:67], poly_row[:, :], ident[0:1, 0:1])
            pe.wait_ge(attnw_in, 112)
            nc.tensor.transpose(bank[7][:, 68:84], bl_raw, ident[0:HEADS, 0:HEADS])
            pe.wait_ge(ffnb_in, 80)
            nc.tensor.transpose(bank[7][:, 84:100], gate_raw, ident[0:EXPERTS, 0:EXPERTS])
            nc.tensor.transpose(bank[7][:, 100:172], b1_raw, ident[0:ALL_EXPERTS * FB, 0:ALL_EXPERTS * FB]).then_inc(setup_mm, 1)
            pe.wait_ge(setup_ev, W_BANKS)
            for j in range(QUADS):
                for k in range(QH):
                    last = nc.tensor.matmul(bank[j][:, k * 96:(k + 1) * 96], wl_sb[:, 4 * j + k, :],
                                            wqkv_sb[:, 4 * j + k, :, :], start=True, stop=True)
                last.then_inc(fold_mm, 1)
            for k in range(QUADS):
                last = nc.tensor.transpose(bank[4][:, k * 128:(k + 1) * 128], wo_sb[:, k * 128:(k + 1) * 128], ident[:, :])
            last.then_inc(fold_mm, 1)
            pe.wait_ge(setup_ev, W_BANKS + 1)
            for c in range(3):
                for h in range(HEADS):
                    q = 32 * (h % QH)
                    last = nc.tensor.matmul(bank[5][q:q + 32, c * QUADS + h // QH:c * QUADS + h // QH + 1],
                                            wqkv_sb[:, h, c, :], blT[:, h:h + 1], start=True, stop=True)
            last.then_inc(fold_mm, 1)
            pe.wait_ge(fold_ev, QUADS + 2)
            for k in range(QUADS):
                last = nc.tensor.matmul(bank[6][:, 0:1], woT[:, k, :], qkv_b[:, 2 * QUADS + k:2 * QUADS + k + 1],
                                        start=(k == 0), stop=(k == QUADS - 1))
            last.then_inc(fold_mm, 1)

        SETUP_ROWS = 16

        def setup_dve_rows(dve):
            dve.wait_ge(tokens_in, 32)
            nc.vector.memset(poly_row[:, 0:1], 1.0).then_inc(dve_const, 1)
            nc.vector.tensor_copy(poly_row[:, 1:2], p_row[:, :]).then_inc(dve_const, 1)
            n, done = 2, 2
            while n < D:
                dve.wait_ge(dve_const, done)
                nc.vector.tensor_tensor(poly_row[:, n:n + 1], poly_row[:, n // 2:n // 2 + 1],
                                        poly_row[:, n // 2:n // 2 + 1], ALU.mult).then_inc(dve_pow, 1)
                dve.wait_ge(dve_pow, done - 1)
                nc.vector.tensor_scalar(poly_row[:, n + 1:2 * n], poly_row[:, 1:n], poly_row[:, n:n + 1], None,
                                        ALU.mult).then_inc(dve_const, 1)
                n, done = 2 * n, done + 1
            dve.wait_ge(patchw_in, 64)
            nc.vector.tensor_tensor(clsT_src, cls_raw, pos_raw[0:1, :], ALU.mult).then_inc(dve_const, 1)
            nc.vector.memset(head_rows[:, :], 0.0).then_inc(dve_const, 1)
            dve.wait_ge(dve_const, done + 2)
            for h in range(QH):
                nc.vector.memset(head_rows[32 * h:32 * h + 32, h:h + 1], 1.0).then_inc(dve_const, 1)
            nc.vector.memset(xT[:, TOKENS:], 0.0).then_inc(dve_const, 1)
            nc.vector.memset(hT[:, TOKENS:], 0.0).then_inc(dve_const, 1)
            assert done + 4 + QH == SETUP_ROWS, done

        dve_pow = sem("dve_pow")

        def setup_dve(dve):
            dve.wait_ge(zero_rows, 1)
            for j in range(W_BANKS):
                dve.wait_ge(setup_mm, j + 1)
                nc.vector.tensor_copy(patch_wT[0:ROWS, 4 * j:4 * j + 4, :],
                                      bank[j][0:ROWS, :].rearrange("p (k d) -> p k d", k=4)).then_inc(setup_ev, 1)
            dve.wait_ge(setup_mm, W_BANKS + 1)
            nc.vector.tensor_copy(blT, bank[7][:, 68:84]).then_inc(setup_ev, 1)
            nc.vector.tensor_copy(posT[:, :], bank[7][:, 0:65]).then_inc(setup_ev, 1)
            nc.vector.tensor_copy(posc[:, :], bank[7][:, 65:67]).then_inc(setup_ev, 1)
            nc.vector.tensor_copy(gate_wT[:, :], bank[7][:, 84:100]).then_inc(setup_ev, 1)
            nc.vector.tensor_copy(b1T[:, :], bank[7][:, 100:172]).then_inc(setup_ev, 1)
            for j in range(QUADS):
                dve.wait_ge(fold_mm, j + 1)
                nc.vector.tensor_copy(qkv_w[:, :, QH * j:QH * j + QH, :],
                                      bank[j][:, 0:QH * 96].rearrange("p (h c d) -> p c h d", h=QH, c=3)).then_inc(fold_ev, 1)
            dve.wait_ge(fold_mm, QUADS + 1)
            nc.vector.tensor_copy(woT[:, :, :], bank[4][:, :].rearrange("p (k d) -> p k d", k=QUADS)).then_inc(fold_ev, 1)
            dve.wait_ge(fold_mm, QUADS + 2)
            nc.vector.tensor_copy(qkv_b[:, :], bank[5][:, 0:3 * QUADS]).then_inc(fold_ev, 1)
            dve.wait_ge(fold_mm, QUADS + 3)
            nc.vector.tensor_tensor(out_b[:, :], bank[6][:, 0:1], bo_col[:, :], ALU.add).then_inc(fold_ev, 1)
        SETUP_EV = W_BANKS + 5
        FOLD_EV = QUADS + 3

        tok_i = sb("tok_i", [IMAGES, TEXT], I32)
        wk = [0]

        def carve(n, parts=128):
            a = work[0:parts, wk[0]:wk[0] + n]
            wk[0] += n
            return a
        tok_f = carve(TEXT, IMAGES)
        push = carve(TEXT, IMAGES)
        qlen = carve(TEXT, IMAGES)
        pushes = carve(TEXT, IMAGES)
        step = carve(TEXT, IMAGES)
        ones_row = carve(TEXT, IMAGES)
        tree_rows = carve(4 * TEXT, IMAGES).rearrange("p (k t) -> p k t", k=4)
        head_i = carve(TEXT, IMAGES).bitcast(I32)
        par_i = carve(TEXT, IMAGES).bitcast(I32)
        bit_i = carve(TEXT, IMAGES).bitcast(I32)
        tree_rows_b = carve(TEXT, IMAGES).bitcast(BF16).rearrange("p (k t) -> p k t", k=2)
        tree_cols = carve(4 * IMAGES, TEXT).rearrange("p (k b) -> p k b", k=4)
        lr_cols = carve(IMAGES, TEXT).bitcast(BF16).rearrange("p (b k) -> p b k", k=2)
        HALF = 4
        TURNS_1 = IMAGES // (2 * HALF)
        SW = TEXT + 128 + 1
        seq_t = [carve(HALF * SW // 2, TEXT).bitcast(BF16).rearrange("p (b c) -> p b c", c=SW) for _ in range(2)]
        par_t = [carve(HALF * 78 // 2, TEXT).bitcast(BF16).rearrange("p (b c) -> p b c", c=78) for _ in range(2)]
        tree_bc = xT[0:TEXT, 0:IMAGES * TEXT].bitcast(BF16).rearrange("p (k b t) -> p k b t", k=2, t=TEXT)
        tree_dram = nc.dram_tensor("tree_dram", (2, IMAGES, TEXT), BF16, kind="Internal").ap()

        tree_row = sem("tree_row")
        tree_out = sem("tree_out")
        tree_in = sem("tree_in")
        tree_colmm = sem("tree_colmm")
        tree_col = sem("tree_col")
        tree_start = [sem(f"tree_start{u}") for u in range(2)]
        tree_mm = [sem(f"tree_mm{u}") for u in range(2)]
        tree_ev = [sem(f"tree_ev{u}") for u in range(2)]
        tree_pw = [sem(f"tree_pw{u}") for u in range(2)]
        tree_h = [sem(f"tree_h{u}") for u in range(2)]

        def tree_rows_dve(dve):
            n = [0]

            def link(ins):
                n[0] += 1
                ins.then_inc(tree_row, 1)
                dve.wait_ge(tree_row, n[0])
            nc.vector.memset(ones_row, 1.0)
            link(nc.vector.tensor_copy(tok_f, tok_i[:, :]))
            link(nc.vector.tensor_scalar(push, tok_f, float(END_TOKEN), None, ALU.not_equal))
            link(nc.vector.memset(push[:, 0:1], 1.0))
            link(nc.vector.tensor_scalar(step, push, 2.0, -1.0, ALU.mult, ALU.add))
            link(nc.vector.memset(qlen[:, 0:1], 2.0))
            link(nc.vector.tensor_tensor_scan(qlen[:, 1:], step[:, 1:], ones_row[:, 1:], 2.0, ALU.add, ALU.max))
            link(nc.vector.tensor_tensor_scan(pushes, push, push, 0.0, ALU.add, ALU.max))
            link(nc.vector.memset(tree_rows[:, 0:1, :], 0.0))
            link(nc.vector.scalar_tensor_tensor(tree_rows[:, 0, 1:], pushes[:, 0:TEXT - 1], 2.0, qlen[:, 0:TEXT - 1],
                                                ALU.mult, ALU.subtract))
            link(nc.vector.tensor_copy(head_i, tree_rows[:, 0, :]))
            link(nc.vector.tensor_scalar(par_i, head_i, 1, None, ALU.arith_shift_right))
            link(nc.vector.tensor_scalar(bit_i, head_i, 1, None, ALU.bitwise_and))
            link(nc.vector.tensor_copy(tree_rows[:, 0, :], par_i))
            link(nc.vector.tensor_copy(tree_rows[:, 3, :], bit_i))
            link(nc.vector.tensor_scalar(tree_rows[:, 2, :], tree_rows[:, 3, :], -1.0, 1.0, ALU.mult, ALU.add))
            link(nc.vector.memset(tree_rows[:, 0, 0:1], -2.0))
            link(nc.vector.memset(tree_rows[:, 2, 0:1], 0.0))
            link(nc.vector.memset(tree_rows[:, 3, 0:1], 0.0))
            link(nc.vector.tensor_tensor(tree_rows[:, 1, :], push, pushes, ALU.mult))
            link(nc.vector.tensor_scalar(tree_rows[:, 1, :], tree_rows[:, 1, :], -1.0, None, ALU.add))
            link(nc.vector.tensor_copy(tree_rows_b, tree_rows[:, 0:2, :]))
            assert n[0] == TREE_ROW, n[0]
        TREE_ROW = 21

        def tree_sp(sp):
            sp.wait_ge(tree_row, TREE_ROW)
            sp.dma_start(tree_dram.rearrange("k b t -> b k t"), tree_rows_b).then_inc(tree_out, 16)
            sp.wait_ge(tree_out, 16)
            for k in range(2):
                src = tree_dram[k:k + 1, :, :].rearrange("k b t -> k (b t)").to_broadcast([TEXT, IMAGES * TEXT])
                sp.dma_start(xT[0:TEXT, 0:IMAGES * TEXT].bitcast(BF16)[:, k * IMAGES * TEXT:(k + 1) * IMAGES * TEXT],
                             src).then_inc(tree_in, 16)

        def tree_pe(pe):
            pe.wait_ge(pool_const, POOL_CONST)
            pe.wait_ge(tree_row, TREE_ROW)
            for k in range(4):
                last = nc.tensor.transpose(bank[0][0:TEXT, k * IMAGES:(k + 1) * IMAGES], tree_rows[:, k, :],
                                           ident[0:IMAGES, 0:IMAGES])
            last.then_inc(tree_colmm, 1)
            pe.wait_ge(tree_col, 2)
            with pe.Fori(0, TURNS_1) as i:
                patch_part(pe, i, 0)
                for lv in range(TREE_LEVELS):
                    w = 2 << lv
                    lo, hi = (0, TEXT + w) if lv < TREE_LEVELS - 1 else (TEXT, TEXT + w)
                    for u in range(2):
                        if lv == 0:
                            pe.wait_ge(tree_start[u], 3 * (i + 1))
                            pe.wait_ge(tree_h[u], i + 1)
                        else:
                            pe.wait_ge(tree_ev[u], i * 11 + 2 * lv)
                            pe.wait_ge(tree_pw[u], i * 5 + lv)
                        for b in range(HALF):
                            last = nc.tensor.matmul(bank[2 * u][0:TEXT, b * (hi - lo):(b + 1) * (hi - lo)],
                                                    par_t[u][:, b, 0:TEXT], seq_t[u][:, b, lo:hi], start=True, stop=True)
                        if lv < TREE_LEVELS - 1:
                            for b in range(HALF):
                                last = nc.tensor.matmul(bank[2 * u + 1][0:TEXT, b * TEXT:(b + 1) * TEXT],
                                                        seq_t[u][:, b, 0:TEXT], par_t[u][:, b, 0:TEXT], start=True, stop=True)
                        last.then_inc(tree_mm[u], 1)
                    patch_part(pe, i, lv + 1)
                for u in range(2):
                    pe.wait_ge(tree_ev[u], i * 11 + 11)
                    for b in range(HALF):
                        last = nc.tensor.matmul(bank[2 * u + 1][:, b * TEXT:(b + 1) * TEXT], seq_t[u][:, b, TEXT:TEXT + D],
                                                identb[0:TEXT, 0:TEXT], start=True, stop=True)
                    last.then_inc(tree_mm[u], 1)

        hT_img = hT[:, 0:TOKENS].rearrange("p (b s) -> p b s", s=SEQ)

        def tree_dve(dve):
            for u in range(2):
                dve.sem_inc(tree_h[u], 1)
            dve.wait_ge(tree_colmm, 1)
            nc.vector.tensor_copy(tree_cols, bank[0][0:TEXT, 0:4 * IMAGES].rearrange("p (k b) -> p k b", k=4)).then_inc(tree_col, 1)
            dve.wait_ge(tree_col, 1)
            nc.vector.tensor_copy(lr_cols, tree_cols[:, 2:4, :].rearrange("p k b -> p b k")).then_inc(tree_col, 1)
            dve.wait_ge(tree_col, 2)
            dve.wait_ge(tree_in, 32)
            dve.wait_ge(setup_ev, SETUP_EV)
            dve.wait_ge(fold_ev, FOLD_EV)
            patch_dve(dve)
            with dve.Fori(0, TURNS_1) as i:
                for u in range(2):
                    b0 = i * (2 * HALF) + u * HALF
                    nc.vector.tensor_tensor(par_t[u][:, :, 0:TEXT], tree_bc[:, 0, bass.ds(b0, HALF), :],
                                            tree_cols[:, 1, bass.ds(b0, HALF)].unsqueeze(2).to_broadcast([TEXT, HALF, TEXT]),
                                            ALU.is_equal).then_inc(tree_start[u], 1)
                    nc.vector.tensor_tensor(seq_t[u][:, :, 0:TEXT], tree_bc[:, 1, bass.ds(b0, HALF), :],
                                            tree_cols[:, 0, bass.ds(b0, HALF)].unsqueeze(2).to_broadcast([TEXT, HALF, TEXT]),
                                            ALU.is_equal).then_inc(tree_start[u], 1)
                    nc.vector.tensor_copy(seq_t[u][:, :, TEXT:TEXT + 2], lr_cols[:, bass.ds(b0, HALF), :]).then_inc(tree_start[u], 1)
                for lv in range(TREE_LEVELS):
                    w = 2 << lv
                    for u in range(2):
                        dve.wait_ge(tree_mm[u], i * 7 + lv + 1)
                        if lv < TREE_LEVELS - 1:
                            src = bank[2 * u][0:TEXT, 0:HALF * (TEXT + w)].rearrange("p (b c) -> p b c", b=HALF)
                            nc.vector.tensor_copy(seq_t[u][:, :, 0:TEXT], src[:, :, 0:TEXT]).then_inc(tree_ev[u], 1)
                            nc.vector.tensor_copy(seq_t[u][:, :, TEXT + w:TEXT + 2 * w],
                                                  src[:, :, TEXT:TEXT + w]).then_inc(tree_ev[u], 1)
                        else:
                            src = bank[2 * u][0:TEXT, 0:HALF * w].rearrange("p (b c) -> p b c", b=HALF)
                            nc.vector.tensor_copy(seq_t[u][:, :, TEXT + w:TEXT + 2 * w], src).then_inc(tree_ev[u], 1)
                patch_out(dve, i, 0)
                patch_out(dve, i, 1)
                for u in range(2):
                    dve.wait_ge(tree_mm[u], i * 7 + 7)
                    nc.vector.tensor_scalar(hT_img[:, bass.ds(i * (2 * HALF) + u * HALF, HALF), 1 + PATCHES:SEQ],
                                            bank[2 * u + 1][:, 0:HALF * TEXT].rearrange("p (b t) -> p b t", b=HALF),
                                            posc[:, 1:2], None, ALU.mult).then_inc(tree_h[u], 1)

        def tree_act(act):
            with act.Fori(0, IMAGES // (2 * HALF)) as i:
                for lv in range(TREE_LEVELS - 1):
                    for u in range(2):
                        act.wait_ge(tree_mm[u], i * 7 + lv + 1)
                        nc.scalar.copy(par_t[u][:, :, 0:TEXT],
                                       bank[2 * u + 1][0:TEXT, 0:HALF * TEXT].rearrange("p (b t) -> p b t", b=HALF)).then_inc(tree_pw[u], 1)

        CHUNKS = IMAGES // CHUNK_IMAGES
        assert CHUNKS // 2 == TURNS_1
        CP = CHUNK_IMAGES * PATCHES
        x_in = [sem(f"x_in{u}") for u in range(2)]
        patch_mm = [sem(f"patch_mm{u}") for u in range(2)]
        patch_ev = [sem(f"patch_ev{u}") for u in range(2)]
        x_v = x.rearrange("b c (g r) w -> b c r g w", r=PATCH)

        def patch_sp(sp):
            def load(u, b0):
                for b in range(CHUNK_IMAGES):
                    for c in range(CHANNELS):
                        sp.dma_start(x_tile[u][c * PATCH:(c + 1) * PATCH, b * GRID * SIDE:(b + 1) * GRID * SIDE],
                                     x_v[bass.ds(b0 + b, 1), c, :, :, :]).then_inc(x_in[u], 16)
            sp.wait_ge(zero_rows, 2)
            for u in range(2):
                load(u, u * CHUNK_IMAGES)
            with sp.Fori(1, CHUNKS // 2) as i:
                for u in range(2):
                    sp.wait_ge(patch_mm[u], i)
                    load(u, i * (2 * CHUNK_IMAGES) + u * CHUNK_IMAGES)

        PARTS = TREE_LEVELS + 1
        PART = 2 * PATCH // PARTS

        def patch_part(pe, i, part):
            for n in range(part * PART, (part + 1) * PART):
                u, k = divmod(n, PATCH)
                if k == 0:
                    pe.wait_ge(x_in[u], (i + 1) * (16 * CHANNELS * CHUNK_IMAGES))
                    pe.wait_ge(patch_ev[u], i + 1)
                    settle(pe)
                xv = x_tile[u].rearrange("r (n k) -> r k n", k=PATCH)
                ins = nc.tensor.matmul(bank[4 + u][:, 0:CP], patch_wT[:, k, :], xv[:, k, :],
                                       start=(k == 0), stop=(k == PATCH - 1))
                if k == PATCH - 1:
                    ins.then_inc(patch_mm[u], 1)

        def patch_dve(dve):
            dve.sem_inc(patch_ev[0], 1)
            dve.sem_inc(patch_ev[1], 1)
            nc.vector.tensor_copy(hT_img[:, :, 0:1].rearrange("p b s -> p (b s)"),
                                  posc[:, 0:1].to_broadcast([D, IMAGES])).then_inc(cls_done, 1)

        def patch_out(dve, i, u):
            dve.wait_ge(patch_mm[u], i + 1)
            nc.vector.scalar_tensor_tensor(
                hT_img[:, bass.ds(i * (2 * CHUNK_IMAGES) + u * CHUNK_IMAGES, CHUNK_IMAGES), 1:1 + PATCHES],
                bank[4 + u][:, 0:CP].rearrange("p (b t) -> p b t", b=CHUNK_IMAGES), patch_b[:, :],
                posT[:, 1:1 + PATCHES].unsqueeze(1).to_broadcast([D, CHUNK_IMAGES, PATCHES]),
                ALU.add, ALU.mult).then_inc(patch_ev[u], 1)
        cls_done = sem("cls_done")

        slot_rows = nc.dram_tensor("slot_rows", (SLOTS + 128 * TOPK, ROW), F32, kind="Internal").ap()
        FT = FILL_TILES // FILLS
        fill = region[:, 0:FT * ROW].rearrange("p (j c) -> p j c", c=ROW)
        fill_ready, fill_out = sem("fill_ready"), sem("fill_out")
        SPARE = 128 * FT

        def fill_pool(pool):
            for u in range(2):
                pool.wait_ge(patch_mm[u], CHUNKS // 2)
            nc.gpsimd.memset(fill, 0.0).then_inc(fill_ready, 1)
            pool.wait_ge(fill_ready, 1)
            nc.gpsimd.iota(fill.bitcast(I32)[:, :, D], pattern=[[1, FT]], base=ASSIGNED,
                           channel_multiplier=FT).then_inc(fill_ready, 1)

        def fill_sp(sp):
            sp.wait_ge(fill_ready, 2)
            rows = slot_rows[0:SLOTS, :].rearrange("(f p j) c -> f p j c", p=128, j=FT)
            for f in range(FILLS):
                sp.dma_start(rows[f, :, :, :], fill).then_inc(fill_out, 16)
            sp.wait_ge(fill_out, 16 * FILLS)

        LW = 2 * SEQ
        LCHUNKS = TOKENS // LW

        NU = 4

        norm_sems = [[sem(f"norm_{n}{u}") for u in range(NU)] for n in ("centred", "copied", "squared", "var", "sd", "rs", "done")]

        class Norm:
            def __init__(self, turns_before):
                self.before = turns_before
                self.over = turns_before + LCHUNKS // NU + 1
                self.centred, self.copied, self.squared, self.var, self.sd, self.rs, self.done = norm_sems
                self.cx, self.sq, self.sdev, self.rstd = (
                    [work[:, (NU * k + u) * LW:(NU * k + u + 1) * LW] for u in range(NU)] for k in range(4))

            def pe_turn(self, pe, i):
                for u in range(NU):
                    pe.wait_ge(self.sd[u], i + (self.before + 1))
                    nc.tensor.matmul(bank[u][:, 0:LW], centre[:, :], hT[:, bass.ds(i * (NU * LW) + u * LW, LW)],
                                     start=True, stop=True).then_inc(self.centred[u], 1)
                for u in range(NU):
                    pe.wait_ge(self.squared[u], i + (self.before + 1))
                    nc.tensor.matmul(bank[u][:, 0:LW], mean_of[:, :], self.sq[u], start=True, stop=True).then_inc(self.var[u], 1)

            def pe(self, pe):
                with pe.Fori(0, LCHUNKS // NU) as i:
                    self.pe_turn(pe, i)

            def act(self, act):
                if not self.before:
                    for u in range(NU):
                        act.sem_inc(self.copied[u], 1)
                        act.sem_inc(self.sd[u], 1)
                with act.Fori(0, LCHUNKS // NU) as i:
                    for u in range(NU):
                        act.wait_ge(self.centred[u], i + (self.before + 1))
                        act.wait_ge(self.done[u], i + (self.before + 1))
                        nc.scalar.copy(self.cx[u], bank[u][:, 0:LW]).then_inc(self.copied[u], 1)
                    for u in range(NU):
                        act.wait_ge(self.var[u], i + (self.before + 1))
                        nc.scalar.activation(self.sdev[u], bank[u][:, 0:LW], ACT.Sqrt, bias=eps_col[:, :]).then_inc(self.sd[u], 1)

            def pool(self, pool):
                with pool.Fori(0, LCHUNKS // NU) as i:
                    for u in range(NU):
                        pool.wait_ge(self.copied[u], i + (self.before + 2))
                        nc.gpsimd.tensor_tensor(self.sq[u], self.cx[u], self.cx[u], ALU.mult).then_inc(self.squared[u], 1)

            def dve(self, dve):
                if not self.before:
                    for u in range(NU):
                        dve.sem_inc(self.done[u], 1)

                def scale(i, u):
                    dve.wait_ge(self.rs[u], i + (self.before + 1))
                    nc.vector.tensor_tensor(xT[:, bass.ds(i * (NU * LW) + u * LW, LW)], self.cx[u], self.rstd[u],
                                            ALU.mult).then_inc(self.done[u], 1)
                with dve.Fori(0, LCHUNKS // NU) as i:
                    for u in range(NU):
                        dve.wait_ge(self.sd[u], i + (self.before + 2))
                        nc.vector.reciprocal(self.rstd[u], self.sdev[u]).then_inc(self.rs[u], 1)
                        if u:
                            scale(i, u - 1)
                    scale(i, NU - 1)

        norm1 = Norm(0)
        norm2 = Norm(LCHUNKS // NU)

        wk[0] = 0
        xs = [carve(SEQ) for _ in range(2)]
        qk = [carve(8 * SEQ).rearrange("p (k s) -> p k s", k=8) for _ in range(2)]
        v_main = [carve(HEADS * HD) for _ in range(2)]
        v_tail = [carve(HEADS * HD, TAIL) for _ in range(2)]
        nmax = [carve(HEADS) for _ in range(2)]
        rsum = [carve(HEADS) for _ in range(2)]
        rinv = carve(HEADS)
        probs = [carve(QH * MAIN) for _ in range(2)]
        probsT = [carve(QH * MAIN) for _ in range(2)]
        catT = carve(QUADS * SEQ).rearrange("p (g s) -> p g s", g=QUADS)
        TR = QH * TAIL
        nmax_t = carve(QUADS, TR)
        rsum_t = carve(QUADS, TR)
        rinv_t = carve(QUADS, TR)
        probs_t = carve(QUADS * SEQ, TR).rearrange("p (g s) -> p g s", g=QUADS)
        probsT_a = carve(QUADS * TR).rearrange("p (g r) -> p g r", g=QUADS)
        probsT_b = carve(QUADS * TR, TAIL).rearrange("p (g r) -> p g r", g=QUADS)
        assert wk[0] <= 9600, wk[0]
        QZ_AT = W_ELEMS - 2 * HEADS * SEQ
        qz = [region[:, QZ_AT + u * HEADS * MAIN:QZ_AT + (u + 1) * HEADS * MAIN].rearrange("p (g h s) -> p g h s", g=QUADS, h=QH)
              for u in range(2)]
        QT_AT = QZ_AT + 2 * HEADS * MAIN
        qz_t = [region[:, QT_AT + u * HEADS * TAIL:QT_AT + (u + 1) * HEADS * TAIL].rearrange("p (g h s) -> p g h s", g=QUADS, h=QH)
                for u in range(2)]
        mask_main = sb("mask_main", [128, QH, MAIN], BF16)
        mask_tail = sb("mask_tail", [TR, 2, SEQ], BF16)

        mask_ready, mask_dma = sem("mask_ready"), sem("mask_dma")
        qk_mm, qk_ev, v_mm, v_ev = sem("qk_mm"), sem("qk_ev"), sem("v_mm"), sem("v_ev")
        xs_ready, qz_ready = sem("xs_ready"), sem("qz_ready")
        s_mm, max_done, exp_done, t_mm, t_ev, f_mm, norm_done = (sem(n) for n in (
            "s_mm", "max_done", "exp_done", "t_mm", "t_ev", "f_mm", "norm_done"))
        st_mm, maxt_done, expt_done, normt_done, tt_mm, tt_ev, tf_mm, tf_ev = (sem(n) for n in (
            "st_mm", "maxt_done", "expt_done", "normt_done", "tt_mm", "tt_ev", "tf_mm", "tf_ev"))
        ft_ev, o_mm, resid = sem("ft_ev"), sem("o_mm"), sem("resid")
        rinv_done, rinvt_done = sem("rinv_done"), sem("rinvt_done")

        def at(i, u, per, c):
            return i * (2 * per) + (u * per + c)

        def attn_masks_pool(pool):
            nc.gpsimd.memset(mask_main[:, :, :], 0.0).then_inc(mask_ready, 1)
            nc.gpsimd.memset(mask_tail[:, :, :], 0.0).then_inc(mask_ready, 1)
            pool.wait_ge(mask_ready, 2)
            nc.gpsimd.affine_select(out=mask_main[:, :, :], in_=mask_main[:, :, :], compare_op=ALU.is_ge, fill=MASKED,
                                    base=0, pattern=[[0, QH], [-1, MAIN]], channel_multiplier=1).then_inc(mask_ready, 1)
            pool.wait_ge(mask_ready, 3)
            for h in range(QH):
                for k in range(2):
                    pool.dma_start(mask_tail[h * TAIL:(h + 1) * TAIL, k, MAIN:SEQ],
                                   mask_main[0:TAIL, 0, 0:TAIL]).then_inc(mask_dma, 16)
        MASK_DMA = 16 * 2 * QH

        def qk_fill(pe, u, j, b):
            for k in range(3 * j, min(3 * j + 3, 8)):
                c, g = divmod(k, QUADS)
                last = nc.tensor.matmul(b[:, (k - 3 * j) * SEQ:(k - 3 * j + 1) * SEQ],
                                        qkv_w[:, c, QH * g:QH * g + QH, :], xs[u], start=True, stop=True)
            last.then_inc(qk_mm, 1)

        def v_fill(pe, u, part, b):
            lo, n = ((0, MAIN), (MAIN, TAIL))[part]
            nc.tensor.matmul(b[0:n, :], xs[u][:, lo:lo + n], qkv_w[:, 2, :, :], start=True, stop=True).then_inc(v_mm, 1)

        def s_fill(pe, u, g):
            nc.tensor.matmul(bank[g % 2][:, :], identb[:, :], mask_main[:, :, :], start=True, stop=False)
            for h in range(QH):
                last = nc.tensor.matmul(bank[g % 2][:, h * MAIN:(h + 1) * MAIN], qz[u][:, g, h, 0:MAIN],
                                        qk[u][:, QUADS + g, 0:MAIN], start=False, stop=(h == QH - 1))
            last.then_inc(s_mm, 1)

        def attn_pe(pe):
            pe.wait_ge(mask_dma, MASK_DMA)
            pe.wait_ge(fold_ev, FOLD_EV)
            pe.wait_ge(xs_ready, 1)
            qk_fill(pe, 0, 0, bank[5])
            qk_fill(pe, 0, 1, bank[6])
            pe.wait_ge(qk_ev, 1)
            qk_fill(pe, 0, 2, bank[5])
            pe.wait_ge(qk_ev, 2)
            v_fill(pe, 0, 0, bank[6])
            pe.wait_ge(qk_ev, 3)
            v_fill(pe, 0, 1, bank[5])
            pe.wait_ge(qz_ready, 8)
            s_fill(pe, 0, 0)
            s_fill(pe, 0, 1)
            with pe.Fori(0, IMAGES // 2) as i:
                for u in range(2):
                    w = 1 - u

                    def st_fill(p):
                        settle(pe)
                        nc.tensor.matmul(bank[7][0:TR, 0:2 * SEQ], identb[0:TR, 0:TR], mask_tail[:, :, :], start=True, stop=False)
                        for k in range(2):
                            last = nc.tensor.matmul(bank[7][0:TR, k * SEQ:(k + 1) * SEQ], qz_t[u][:, 2 * p + k, :, :],
                                                    qk[u][:, QUADS + 2 * p + k, :], start=False, stop=(k == 1))
                        last.then_inc(st_mm, 1)

                    def t_fill(g):
                        pe.wait_ge(norm_done, at(i, u, 4, g + 1))
                        pe.wait_ge(t_ev, at(i, u, 4, g - 2 + 4 + 1))
                        for h in range(QH):
                            last = nc.tensor.transpose(bank[2 + g % 2][:, h * MAIN:(h + 1) * MAIN],
                                                       probs[g % 2][:, h * MAIN:(h + 1) * MAIN], ident[:, :])
                        last.then_inc(t_mm, 1)

                    def f_fill(g):
                        pe.wait_ge(t_ev, at(i, u, 4, g + 4 + 1))
                        if g == 0:
                            pe.wait_ge(resid, at(i, u, 1, 1))
                            pe.wait_ge(v_ev, at(i, u, 2, 1))
                        for h in range(QH):
                            c = (QH * g + h) * HD
                            last = nc.tensor.matmul(bank[4][h * HD:(h + 1) * HD, g * MAIN:(g + 1) * MAIN], v_main[u][:, c:c + HD],
                                                    probsT[g % 2][:, h * MAIN:(h + 1) * MAIN], start=True, stop=True)
                        last.then_inc(f_mm, 1)

                    def tt_fill(p):
                        settle(pe)
                        for k in range(2):
                            g = 2 * p + k
                            nc.tensor.transpose(bank[6][:, k * TR:(k + 1) * TR], probs_t[:, g, 0:MAIN], ident[0:TR, 0:TR])
                            last = nc.tensor.transpose(bank[6][0:TAIL, (2 + k) * TR:(3 + k) * TR], probs_t[:, g, MAIN:SEQ],
                                                       ident[0:TR, 0:TR])
                        last.then_inc(tt_mm, 1)

                    pe.wait_ge(expt_done, at(i, u, 4, 4))
                    st_fill(0)
                    pe.wait_ge(xs_ready, at(i, u, 1, 2))
                    pe.wait_ge(v_ev, at(i, u, 2, 2))
                    pe.wait_ge(tf_ev, at(i, u, 1, 1))
                    qk_fill(pe, w, 0, bank[5])
                    pe.wait_ge(tt_ev, at(i, u, 4, 4))
                    qk_fill(pe, w, 1, bank[6])
                    t_fill(0)
                    s_fill(pe, u, 2)
                    f_fill(0)
                    pe.wait_ge(qk_ev, at(i, u, 3, 4))
                    qk_fill(pe, w, 2, bank[5])
                    pe.wait_ge(qk_ev, at(i, u, 3, 5))
                    v_fill(pe, w, 0, bank[6])
                    t_fill(1)
                    s_fill(pe, u, 3)
                    pe.wait_ge(expt_done, at(i, u, 4, 2 + 4))
                    st_fill(1)
                    f_fill(1)
                    pe.wait_ge(qk_ev, at(i, u, 3, 6))
                    v_fill(pe, w, 1, bank[5])
                    t_fill(2)
                    pe.wait_ge(qz_ready, at(i, u, 8, 16))
                    s_fill(pe, w, 0)
                    pe.wait_ge(normt_done, at(i, u, 2, 1))
                    pe.wait_ge(v_ev, at(i, u, 2, 3))
                    tt_fill(0)
                    f_fill(2)
                    t_fill(3)
                    s_fill(pe, w, 1)
                    pe.wait_ge(normt_done, at(i, u, 2, 2))
                    pe.wait_ge(tt_ev, at(i, u, 4, 2 + 4))
                    tt_fill(1)
                    f_fill(3)
                    pe.wait_ge(v_ev, at(i, u, 2, 4))
                    pe.wait_ge(tt_ev, at(i, u, 4, 4 + 4))
                    for g in range(QUADS):
                        for h in range(QH):
                            o = bank[5][h * HD:(h + 1) * HD, g * TAIL:(g + 1) * TAIL]
                            c, q = (QH * g + h) * HD, h * TAIL
                            nc.tensor.matmul(o, v_main[u][:, c:c + HD], probsT_a[:, g, q:q + TAIL], start=True, stop=False)
                            last = nc.tensor.matmul(o, v_tail[u][:, c:c + HD], probsT_b[:, g, q:q + TAIL], start=False, stop=True)
                    last.then_inc(tf_mm, 1)
                    pe.wait_ge(ft_ev, at(i, u, 1, 1))
                    for lo, hi in ((0, MAIN), (MAIN, SEQ)):
                        if lo:
                            pe.wait_ge(tf_ev, at(i, u, 1, 2))
                        for g in range(QUADS):
                            last = nc.tensor.matmul(bank[4][:, lo:hi], woT[:, g, :], catT[:, g, lo:hi],
                                                    start=(g == 0), stop=(g == QUADS - 1))
                    last.then_inc(o_mm, 1)

        def attn_pool(pool):
            def stage(u, at_col):
                nc.gpsimd.tensor_copy(xs[u], xT[:, at_col]).then_inc(xs_ready, 1)

            def spread(u):
                for h in range(QH):
                    nc.gpsimd.tensor_scalar(qz[u][:, :, h, :], qk[u][:, 0:QUADS, 0:MAIN], head_rows[:, h:h + 1], 0.0, ALU.mult, ALU.add).then_inc(qz_ready, 1)
                    nc.gpsimd.tensor_scalar(qz_t[u][:, :, h, :], qk[u][:, 0:QUADS, MAIN:SEQ], head_rows[:, h:h + 1], 0.0, ALU.mult, ALU.add).then_inc(qz_ready, 1)
            for u in range(NU):
                pool.wait_ge(norm1.done[u], norm1.over)
            stage(0, slice(0, SEQ))
            stage(1, slice(SEQ, 2 * SEQ))
            pool.wait_ge(dve_const, SETUP_ROWS)
            pool.wait_ge(qk_ev, 3)
            spread(0)
            with pool.Fori(0, IMAGES // 2) as i:
                for u in range(2):
                    pool.wait_ge(v_mm, at(i, u, 2, 2))
                    settle(pool)
                    stage(u, bass.ds(i * (2 * SEQ) + (u + 2) * SEQ, SEQ))
                    pool.wait_ge(qk_ev, at(i, u, 3, 5))
                    settle(pool)
                    spread(1 - u)

        def attn_act(act):
            def v_evac(u, part, b):
                n = (MAIN, TAIL)[part]
                nc.scalar.copy((v_main, v_tail)[part][u][0:n, :], b[0:n, :]).then_inc(v_ev, 1)

            def exps_of(u, g):
                for h in range(QH):
                    n = QH * g + h
                    nc.scalar.activation(probs[g % 2][:, h * MAIN:(h + 1) * MAIN], bank[g % 2][:, h * MAIN:(h + 1) * MAIN],
                                         ACT.Exp, bias=nmax[u][:, n:n + 1], accum_out=rsum[u][:, n:n + 1]).then_inc(exp_done, 1)
            act.wait_ge(v_mm, 1)
            v_evac(0, 0, bank[6])
            act.wait_ge(v_mm, 2)
            v_evac(0, 1, bank[5])
            act.wait_ge(max_done, 1)
            exps_of(0, 0)
            with act.Fori(0, IMAGES // 2) as i:
                for u in range(2):
                    def exps(g):
                        act.wait_ge(max_done, at(i, u, 4, g + 1))
                        act.wait_ge(t_mm, at(i, u, 4, g - 2 + 4 + 1))
                        exps_of(u if g < QUADS else 1 - u, g % QUADS)

                    def tail_exps(p):
                        act.wait_ge(maxt_done, at(i, u, 2, p + 1))
                        act.wait_ge(tt_mm, at(i, u, 2, p + 1))
                        for k in range(2):
                            g = 2 * p + k
                            nc.scalar.activation(probs_t[:, g, :], bank[7][0:TR, k * SEQ:(k + 1) * SEQ], ACT.Exp,
                                                 bias=nmax_t[:, g:g + 1], accum_out=rsum_t[:, g:g + 1]).then_inc(expt_done, 1)
                    exps(1)
                    tail_exps(0)
                    act.wait_ge(v_mm, at(i, u, 2, 3))
                    v_evac(1 - u, 0, bank[6])
                    exps(2)
                    exps(3)
                    tail_exps(1)
                    act.wait_ge(v_mm, at(i, u, 2, 4))
                    v_evac(1 - u, 1, bank[5])
                    exps(4)
                    act.wait_ge(f_mm, at(i, u, 4, 4 + 4))
                    act.wait_ge(o_mm, at(i, u, 1, 1))
                    nc.scalar.copy(catT[:, :, 0:MAIN], bank[4][:, :].rearrange("p (g s) -> p g s", g=QUADS)).then_inc(ft_ev, 1)

        def attn_dve(dve):
            dve.sem_inc(t_ev, 4)
            dve.sem_inc(t_mm, 4)
            dve.sem_inc(tt_mm, 2)
            dve.sem_inc(expt_done, 4)
            dve.sem_inc(f_mm, 4)
            dve.sem_inc(tf_mm, 1)
            dve.sem_inc(tt_ev, 4)
            dve.sem_inc(tf_ev, 1)
            dve.sem_inc(resid, 1)
            dve.sem_inc(o_mm, 1)

            def qk_evac(u, j, b):
                n = min(3, 8 - 3 * j)
                nc.vector.tensor_tensor(qk[u][:, 3 * j:3 * j + n, :], b[:, 0:n * SEQ].rearrange("p (k s) -> p k s", k=n),
                                        qkv_b[:, 3 * j:3 * j + n].unsqueeze(2).to_broadcast([128, n, SEQ]),
                                        ALU.add).then_inc(qk_ev, 1)
            for j in range(3):
                dve.wait_ge(qk_mm, j + 1)
                qk_evac(0, j, bank[5 + j % 2])

            def maxes_into(u, g):
                nc.vector.tensor_reduce(nmax[u][:, QH * g:QH * g + QH], bank[g % 2][:, :].rearrange("p (h s) -> p h s", h=QH),
                                        AX.X, ALU.max, negate=True).then_inc(max_done, 1)

            def inverse_of(u, g):
                nc.vector.reciprocal(rinv[:, QH * g:QH * g + QH], rsum[u][:, QH * g:QH * g + QH]).then_inc(rinv_done, 1)

            def norm_of(g):
                p = probs[g % 2].rearrange("p (h s) -> p h s", h=QH)
                r = rinv[:, QH * g:QH * g + QH]
                nc.vector.tensor_tensor(p, p, r.unsqueeze(2).to_broadcast([128, QH, MAIN]), ALU.mult).then_inc(norm_done, 1)
            for g in range(2):
                dve.wait_ge(s_mm, g + 1)
                maxes_into(0, g)
            dve.wait_ge(exp_done, QH)
            inverse_of(0, 0)
            dve.wait_ge(rinv_done, 1)
            norm_of(0)
            with dve.Fori(0, IMAGES // 2) as i:
                for u in range(2):
                    def maxes(g):
                        dve.wait_ge(s_mm, at(i, u, 4, g + 1))
                        maxes_into(u if g < QUADS else 1 - u, g % QUADS)

                    def tail_maxes(p):
                        dve.wait_ge(st_mm, at(i, u, 2, p + 1))
                        nc.vector.tensor_reduce(nmax_t[:, 2 * p:2 * p + 2], bank[7][0:TR, 0:2 * SEQ].rearrange("p (k s) -> p k s", k=2),
                                                AX.X, ALU.max, negate=True).then_inc(maxt_done, 1)

                    def tail_inv(p):
                        dve.wait_ge(expt_done, at(i, u, 4, 2 * p + 2 + 4))
                        nc.vector.reciprocal(rinv_t[:, 2 * p:2 * p + 2], rsum_t[:, 2 * p:2 * p + 2]).then_inc(rinvt_done, 1)

                    def tail_norm(p):
                        dve.wait_ge(rinvt_done, at(i, u, 2, p + 1))
                        t = probs_t[:, 2 * p:2 * p + 2, :]
                        nc.vector.tensor_tensor(t, t, rinv_t[:, 2 * p:2 * p + 2].unsqueeze(2).to_broadcast([TR, 2, SEQ]),
                                                ALU.mult).then_inc(normt_done, 1)

                    def t_evac(g):
                        dve.wait_ge(t_mm, at(i, u, 4, g + 1 + 4))
                        dve.wait_ge(f_mm, at(i, u, 4, g - 2 + 4 + 1))
                        nc.vector.tensor_copy(probsT[g % 2], bank[2 + g % 2][:, :]).then_inc(t_ev, 1)

                    def tt_evac(p):
                        dve.wait_ge(tt_mm, at(i, u, 2, p + 1 + 2))
                        if p == 0:
                            dve.wait_ge(tf_mm, at(i, u, 1, 1))
                        nc.vector.tensor_copy(probsT_a[:, 2 * p:2 * p + 2, :],
                                              bank[6][:, 0:2 * TR].rearrange("p (k r) -> p k r", k=2)).then_inc(tt_ev, 1)
                        nc.vector.tensor_copy(probsT_b[:, 2 * p:2 * p + 2, :],
                                              bank[6][0:TAIL, 2 * TR:4 * TR].rearrange("p (k r) -> p k r", k=2)).then_inc(tt_ev, 1)
                    def norm(g):
                        dve.wait_ge(exp_done, at(i, u, 16, 4 * g + 4))
                        inverse_of(u if g < QUADS else 1 - u, g % QUADS)
                        dve.wait_ge(rinv_done, at(i, u, 4, g + 1))
                        norm_of(g % QUADS)
                    tail_maxes(0)
                    dve.wait_ge(qk_mm, at(i, u, 3, 4))
                    qk_evac(1 - u, 0, bank[5])
                    dve.wait_ge(qk_mm, at(i, u, 3, 5))
                    qk_evac(1 - u, 1, bank[6])
                    tail_inv(0)
                    t_evac(0)
                    norm(1)
                    maxes(2)
                    tail_norm(0)
                    dve.wait_ge(qk_mm, at(i, u, 3, 6))
                    qk_evac(1 - u, 2, bank[5])
                    t_evac(1)
                    maxes(3)
                    norm(2)
                    tail_maxes(1)
                    t_evac(2)
                    norm(3)
                    tail_inv(1)
                    tt_evac(0)
                    tail_norm(1)
                    maxes(4)
                    t_evac(3)
                    tt_evac(1)
                    dve.wait_ge(tf_mm, at(i, u, 1, 1 + 1))
                    nc.vector.tensor_copy(catT[:, :, MAIN:SEQ],
                                          bank[5][:, 0:QUADS * TAIL].rearrange("p (g s) -> p g s", g=QUADS)).then_inc(tf_ev, 1)
                    norm(4)
                    maxes(5)
                    dve.wait_ge(o_mm, at(i, u, 1, 1 + 1))
                    here = hT[:, bass.ds(i * (2 * SEQ) + u * SEQ, SEQ)]
                    nc.vector.scalar_tensor_tensor(here, bank[4][:, 0:SEQ], out_b[:, :], here, ALU.add, ALU.add).then_inc(resid, 1)

        expert_w = region[:, :].rearrange("p (e w) -> p e w", w=EW)
        LATE = QZ_AT // EW
        early_w, late_w = sem("early_w"), sem("late_w")
        EARLY_W, LATE_W = 32 * LATE, 32 * (ALL_EXPERTS - LATE)

        def w1_blocks(w, k):
            return w[:, k * 128:(k + 1) * 128]

        def w2_blocks(w, k):
            return w[:, HIDDEN + k * 128:HIDDEN + (k + 1) * 128]

        def weights_sp(sp):
            for u in range(2):
                sp.wait_ge(patch_mm[u], CHUNKS // 2)
            sp.wait_ge(fold_mm, QUADS + 3)
            fill_sp(sp)
            for e in range(ALL_EXPERTS):
                if e == LATE:
                    sp.wait_ge(o_mm, IMAGES + 1)
                got = early_w if e < LATE else late_w
                w1, w2 = (se_w1[e, :, :], se_w2[e, :, :]) if e < SHARED else (re_w1[e - SHARED, :, :], re_w2[e - SHARED, :, :])
                sp.dma_start(expert_w[:, e, 0:HIDDEN], w1).then_inc(got, 16)
                sp.dma_start(expert_w[:, e, HIDDEN:2 * HIDDEN].rearrange("p (k h) -> p k h", k=FB),
                             w2.rearrange("(k p) h -> p k h", p=128)).then_inc(got, 16)

        TE = TILES * EXPERTS
        KEEP = TE + TILES * TOPK + 2 * DISPATCHED * TOPK + 2 * FILL_TILES + EXPERTS + 128
        wk[0] = 9600 - KEEP
        combine = carve(TE).rearrange("p (t e) -> p t e", e=EXPERTS)
        top_w = carve(TILES * TOPK).rearrange("p (t k) -> p t k", k=TOPK)
        slot_of = carve(DISPATCHED * TOPK).bitcast(I32).rearrange("p (t k) -> p t k", k=TOPK)
        row_of = carve(DISPATCHED * TOPK).bitcast(I32).rearrange("p (t k) -> p t k", k=TOPK)
        expert_of = carve(FILL_TILES).bitcast(I32)
        tile_iota = carve(FILL_TILES)
        e_iota = carve(EXPERTS)
        before = carve(64).bitcast(BF16)
        ones_b = carve(64).bitcast(BF16)
        assert wk[0] <= 9600, wk[0]
        wk[0] = 0
        logits = carve(TE).rearrange("p (t e) -> p t e", e=EXPERTS)
        hit = carve(TE).rearrange("p (t e) -> p t e", e=EXPERTS)
        slots = carve(TE).rearrange("p (t e) -> p t e", e=EXPERTS)
        counts = carve(TE).rearrange("p (e t) -> p e t", e=EXPERTS)
        running = logits.rearrange("p t e -> p (t e)").rearrange("p (e t) -> p e t", e=EXPERTS)
        chosen = carve(TE // 2).bitcast(BF16)
        top_flat = carve(TILES * 8)
        top_v = top_flat.rearrange("p (t k) -> p t k", k=8)
        top_i = carve(TILES * 8).rearrange("p (t k) -> p t k", k=8).bitcast(U32)
        top_f = carve(TILES * TOPK).rearrange("p (t k) -> p t k", k=TOPK)
        row1 = carve(TILES)
        row2 = carve(TILES)
        ends, starts, n_tiles, last_tile, tiles_f = (carve(EXPERTS) for _ in range(5))
        n_up, n_shift = (carve(EXPERTS).bitcast(I32) for _ in range(2))
        expert_f = top_flat[:, 0:FILL_TILES]
        assert wk[0] <= 9600 - KEEP, (wk[0], 9600 - KEEP)

        gate_mm, gate_v, gate_e, tables_ready, chosen_ready, rank_mm, gate_done = (sem(n) for n in (
            "gate_mm", "gate_v", "gate_e", "tables_ready", "chosen_ready", "rank_mm", "gate_done"))
        GB = 512 // EXPERTS
        GBANKS = -(-TILES // GB)
        CT = 4
        CGROUPS = -(-TILES // CT)
        GATE_TABLES = 9

        def norm2_gate_pe(pe):
            turns, t = LCHUNKS // NU, 0
            for i in range(turns + 1):
                if i < turns:
                    norm2.pe_turn(pe, i)
                if i:
                    for u in range(NU):
                        pe.wait_ge(norm2.done[u], norm2.before + i + 1)
                while (t + 1) * 128 <= i * NU * LW:
                    j, n = divmod(t, GB)
                    ins = nc.tensor.matmul(bank[4 + j][:, n * EXPERTS:(n + 1) * EXPERTS],
                                           xT[:, t * 128:(t + 1) * 128], gate_wT[:, :], start=True, stop=True)
                    t += 1
                    if t % GB == 0 or t == TILES:
                        ins.then_inc(gate_mm, 1)
            assert t == TILES

        def ranks_pe(pe):
            pe.wait_ge(tables_ready, GATE_TABLES)
            pe.wait_ge(chosen_ready, 1)
            for b, lhs in ((0, before), (3, ones_b)):
                for j in range(GBANKS):
                    n = min(GB, TILES - j * GB) * EXPERTS
                    last = nc.tensor.matmul(bank[b + j][:, 0:n], lhs, chosen[:, j * GB * EXPERTS:j * GB * EXPERTS + n],
                                            start=True, stop=True)
            last.then_inc(rank_mm, 1)

        def gate_pool(pool):
            pool.wait_ge(fill_out, 16 * FILLS)
            pool.wait_ge(resid, IMAGES + 1)
            pool.wait_ge(o_mm, IMAGES + 1)
            nc.gpsimd.iota(e_iota, pattern=[[1, EXPERTS]], base=0, channel_multiplier=0,
                           allow_small_or_imprecise_dtypes=True).then_inc(tables_ready, 1)
            nc.gpsimd.iota(tile_iota, pattern=[[1, FILL_TILES]], base=0, channel_multiplier=0,
                           allow_small_or_imprecise_dtypes=True).then_inc(tables_ready, 1)
            nc.gpsimd.iota(row_of, pattern=[[128 * TOPK, DISPATCHED], [1, TOPK]], base=0,
                           channel_multiplier=TOPK).then_inc(tables_ready, 1)
            nc.gpsimd.iota(slot_of[:, TILES:DISPATCHED, :], pattern=[[0, DISPATCHED - TILES], [1, TOPK]], base=SLOTS,
                           channel_multiplier=TOPK).then_inc(tables_ready, 1)
            nc.gpsimd.memset(ones_b, 1.0).then_inc(tables_ready, 1)
            nc.gpsimd.memset(before, 1.0).then_inc(tables_ready, 1)
            pool.wait_ge(tables_ready, 6)
            nc.gpsimd.affine_select(out=before, in_=before, compare_op=ALU.is_gt, fill=0.0, base=0,
                                    pattern=[[1, 128]], channel_multiplier=-1).then_inc(tables_ready, 1)
            b1 = b1T[:, :].rearrange("p (e k) -> p e k", k=FB)
            nc.gpsimd.tensor_copy(expert_w[:, SHARED:, 2 * HIDDEN:], b1[:, 0:EXPERTS, :]).then_inc(tables_ready, 1)
            nc.gpsimd.tensor_copy(expert_w[:, 0:SHARED, 2 * HIDDEN:], b1[:, EXPERTS:, :]).then_inc(tables_ready, 1)

        def gate_dve(dve):
            n = [0]

            def link(ins):
                n[0] += 1
                ins.then_inc(gate_v, 1)
                dve.wait_ge(gate_v, n[0])
            for j in range(GBANKS):
                dve.wait_ge(gate_mm, j + 1)
                m = min(GB, TILES - j * GB)
                link(nc.vector.tensor_copy(logits[:, j * GB:j * GB + m, :],
                                           bank[4 + j][:, 0:m * EXPERTS].rearrange("p (t e) -> p t e", e=EXPERTS)))
            bc = [128, TILES, EXPERTS]
            link(nc.vector.tensor_reduce(row1, logits, AX.X, ALU.max))
            link(nc.vector.tensor_tensor(logits, logits, row1.unsqueeze(2).to_broadcast(bc), ALU.subtract))
            dve.wait_ge(gate_e, 1)
            link(nc.vector.tensor_reduce(row1, logits, AX.X, ALU.add))
            link(nc.vector.reciprocal(row2, row1))
            link(nc.vector.tensor_tensor(logits, logits, row2.unsqueeze(2).to_broadcast(bc), ALU.mult))
            for t in range(TILES):
                n[0] += 1
                nc.vector.max(top_v[:, t, :], logits[:, t, :]).then_inc(gate_v, 1)
            dve.wait_ge(gate_v, n[0])
            for t in range(TILES):
                n[0] += 1
                nc.vector.max_index(top_i[:, t, :], top_v[:, t, :], logits[:, t, :]).then_inc(gate_v, 1)
            dve.wait_ge(gate_v, n[0])
            link(nc.vector.tensor_tensor(top_w, top_v[:, :, 0:TOPK], top_v[:, :, 0:1].to_broadcast([128, TILES, TOPK]), ALU.subtract))
            dve.wait_ge(gate_e, 2)
            link(nc.vector.tensor_reduce(row1, top_w, AX.X, ALU.add))
            link(nc.vector.reciprocal(row2, row1))
            link(nc.vector.tensor_tensor(top_w, top_w, row2.unsqueeze(2).to_broadcast([128, TILES, TOPK]), ALU.mult))
            link(nc.vector.tensor_copy(top_f, top_i[:, :, 0:TOPK]))
            dve.wait_ge(tables_ready, GATE_TABLES)

            def hits(k):
                link(nc.vector.tensor_tensor(hit, top_f[:, :, k:k + 1].to_broadcast(bc), e_iota.unsqueeze(1).to_broadcast(bc), ALU.is_equal))
            for k in range(TOPK):
                hits(k)
                tgt = combine if k == 0 else hit
                link(nc.vector.tensor_tensor(tgt, hit, top_w[:, :, k:k + 1].to_broadcast(bc), ALU.mult))
                if k:
                    link(nc.vector.tensor_tensor(combine, combine, hit, ALU.add))
            nc.vector.tensor_scalar(chosen.rearrange("p (t e) -> p t e", e=EXPERTS), combine, 0.0, None, ALU.is_gt).then_inc(chosen_ready, 1)
            dve.wait_ge(rank_mm, 1)
            for j in range(GBANKS):
                m = min(GB, TILES - j * GB)
                link(nc.vector.tensor_copy(counts[:, :, j * GB:j * GB + m].rearrange("p e t -> p t e"),
                                           bank[3 + j][:, 0:m * EXPERTS].rearrange("p (t e) -> p t e", e=EXPERTS)))
            flat = counts.rearrange("p e t -> p (e t)")
            link(nc.vector.tensor_tensor_scan(running.rearrange("p e t -> p (e t)"), flat, flat, 0.0, ALU.add, ALU.max))
            ends3, starts3 = ends.unsqueeze(2), starts.unsqueeze(2)
            link(nc.vector.memset(starts, 0.0))
            link(nc.vector.tensor_copy(starts3[:, 1:EXPERTS, :], running[:, 0:EXPERTS - 1, TILES - 1:TILES]))
            link(nc.vector.tensor_copy(ends3, running[:, :, TILES - 1:TILES]))
            link(nc.vector.tensor_tensor(n_tiles, ends, starts, ALU.subtract))
            link(nc.vector.tensor_scalar(n_up, n_tiles, 127.0, None, ALU.add))
            link(nc.vector.tensor_scalar(n_shift, n_up, 7, None, ALU.arith_shift_right))
            link(nc.vector.tensor_copy(tiles_f, n_shift))
            link(nc.vector.tensor_tensor_scan(last_tile, tiles_f, tiles_f, 0.0, ALU.add, ALU.max))
            link(nc.vector.tensor_tensor(running, running, counts, ALU.subtract))
            link(nc.vector.tensor_tensor(n_tiles, last_tile, tiles_f, ALU.subtract))
            link(nc.vector.scalar_tensor_tensor(starts, n_tiles, 128.0, starts, ALU.mult, ALU.subtract))
            link(nc.vector.tensor_tensor(running, running, starts3.to_broadcast([128, EXPERTS, TILES]), ALU.add))
            for j in range(GBANKS):
                m = min(GB, TILES - j * GB)
                link(nc.vector.tensor_tensor(slots[:, j * GB:j * GB + m, :],
                                             bank[j][:, 0:m * EXPERTS].rearrange("p (t e) -> p t e", e=EXPERTS),
                                             running[:, :, j * GB:j * GB + m].rearrange("p e t -> p t e"), ALU.add))
            for k in range(TOPK):
                hits(k)
                link(nc.vector.tensor_tensor(hit, hit, slots, ALU.mult))
                link(nc.vector.tensor_reduce(row1, hit, AX.X, ALU.add))
                link(nc.vector.tensor_copy(slot_of[:, 0:TILES, k:k + 1], row1.unsqueeze(2)))
            nc.vector.memset(row1, 0.0).then_inc(gate_done, 1)

        def tile_experts_dve(dve):
            nc.vector.memset(expert_f, float(SHARED)).then_inc(gate_done, 1)
            for e in range(EXPERTS - 1):
                dve.wait_ge(gate_done, 2 + e)
                nc.vector.scalar_tensor_tensor(expert_f, tile_iota, last_tile[:, e:e + 1], expert_f, ALU.is_ge, ALU.add).then_inc(gate_done, 1)
            dve.wait_ge(gate_done, 1 + EXPERTS)
            nc.vector.tensor_copy(expert_of, expert_f).then_inc(gate_done, 1)
            dve.wait_ge(gate_done, 2 + EXPERTS)

        def gate_act(act):
            act.wait_ge(gate_v, GBANKS + 2)
            nc.scalar.activation(logits, logits, ACT.Exp).then_inc(gate_e, 1)
            act.wait_ge(gate_v, GBANKS + 5 + 2 * TILES + 1)
            nc.scalar.activation(top_w, top_w, ACT.Exp).then_inc(gate_e, 1)

        wk[0] = 0
        x_pass = [carve(PASS) for _ in range(2)]
        act_s = [carve(FB * PASS).rearrange("p (k s) -> p k s", k=FB) for _ in range(SHARED)]
        send = [carve(TOPK * ROW).rearrange("p (k c) -> p k c", k=TOPK) for _ in range(2)]
        send_to = [carve(TOPK).bitcast(U32) for _ in range(2)]
        assert wk[0] <= 9600 - KEEP
        pass_in, sh_mm, sh_act, sh_out, sh_add = (sem(n) for n in ("pass_in", "sh_mm", "sh_act", "sh_out", "sh_add"))
        turn_mm = [sem(f"turn_mm{a}") for a in range(2)]
        send_row = [sem(f"send_row{a}") for a in range(2)]
        sent = [sem(f"sent{a}") for a in range(2)]
        HIDDENS = SHARED * FB

        def shared_act(act):
            act.wait_ge(gate_done, 1)
            with act.Fori(0, PASSES // 2) as i:
                for v in range(2):
                    act.wait_ge(sh_mm, i * (2 * HIDDENS) + (v + 1) * HIDDENS)
                    nc.scalar.copy(x_pass[v], xT[:, bass.ds(i * (2 * PASS) + v * PASS, PASS)]).then_inc(pass_in, 1)
                    for e in range(SHARED):
                        for k in range(FB):
                            act.wait_ge(sh_mm, i * (2 * HIDDENS) + (v * HIDDENS + e * FB + k + 1 + 2 * HIDDENS))
                            if k == 0:
                                act.wait_ge(sh_out, i * (2 * SHARED) + (v * SHARED + e + 1))
                            nc.scalar.activation(act_s[e][:, k, :], bank[k][:, 0:PASS], ACT.Gelu,
                                                 bias=b1T[:, (EXPERTS + e) * FB + k:(EXPERTS + e) * FB + k + 1]).then_inc(sh_act, 1)

        def shared_pe(pe):
            pe.wait_ge(early_w, EARLY_W)
            with pe.Fori(0, PASSES // 2) as i:
                for v in range(2):
                    pe.wait_ge(pass_in, i * 2 + v + 1)
                    for a in range(2):
                        pe.wait_ge(send_row[a], i * 6 + (3 * v + 3))
                        nc.tensor.transpose(bank[6 + a][:, 0:128], x_pass[v][:, a * 128:(a + 1) * 128], ident[:, :]).then_inc(turn_mm[a], 1)
                    for e in range(SHARED):
                        for k in range(FB):
                            pe.wait_ge(sh_act, i * (2 * HIDDENS) + (v * HIDDENS + e * FB + k + 1))
                            nc.tensor.matmul(bank[k][:, 0:PASS], w1_blocks(expert_w[:, e, :], k), x_pass[v],
                                             start=True, stop=True).then_inc(sh_mm, 1)
                    pe.wait_ge(sh_add, i * 2 + v + 1)
                    for e in range(SHARED):
                        for k in range(FB):
                            pe.wait_ge(sh_act, i * (2 * HIDDENS) + (v * HIDDENS + e * FB + k + 1 + FB))
                            last = nc.tensor.matmul(bank[4 + v][:, 0:PASS], w2_blocks(expert_w[:, e, :], k), act_s[e][:, k, :],
                                                    start=(e == 0 and k == 0), stop=(e == SHARED - 1 and k == FB - 1))
                        last.then_inc(sh_out, 1)

        def shared_dve(dve):
            dve.sem_inc(sh_mm, 2 * HIDDENS)
            dve.sem_inc(sh_act, FB)
            dve.sem_inc(sh_out, SHARED)
            dve.sem_inc(sh_add, 2)
            for a in range(2):
                dve.sem_inc(send_row[a], 3)
            def turn(i, first):
                for v in range(2):
                    for a in range(2):
                        tile = bass.ds(i * 4 + (2 * v + a), 1)
                        if not first or v:
                            dve.wait_ge(sent[a], i * (2 * 16 * TOPK) + v * (16 * TOPK))
                        dve.wait_ge(turn_mm[a], i * 2 + v + 1)
                        nc.vector.tensor_copy(send[a][:, :, 0:D], bank[6 + a][:, 0:128].unsqueeze(1).to_broadcast([128, TOPK, D])).then_inc(send_row[a], 1)
                        nc.vector.tensor_copy(send[a].bitcast(I32)[:, :, D:ROW].rearrange("p k c -> p c k"), row_of[:, tile, :]).then_inc(send_row[a], 1)
                        nc.vector.tensor_copy(send_to[a].unsqueeze(1), slot_of[:, tile, :]).then_inc(send_row[a], 1)
                    dve.wait_ge(sh_out, i * (2 * SHARED) + ((v + 1) * SHARED + SHARED))
                    here = hT[:, bass.ds(i * (2 * PASS) + v * PASS, PASS)]
                    nc.vector.scalar_tensor_tensor(here, bank[4 + v][:, 0:PASS], 1.0 / SHARED, here, ALU.mult, ALU.add).then_inc(sh_add, 1)
            turn(0, True)
            with dve.Fori(1, PASSES // 2) as i:
                turn(i, False)

        def dispatch_pool(pool):
            with pool.Fori(0, PASSES // 2) as i:
                for v in range(2):
                    for a in range(2):
                        pool.wait_ge(send_row[a], i * 6 + (3 * v + 6))
                        settle(pool)
                        for k in range(TOPK):
                            nc.gpsimd.indirect_dma_start(slot_rows, bass.IndirectOffsetOnAxis(ap=send_to[a][:, k:k + 1], axis=0),
                                                         send[a][:, k, :], None).then_inc(sent[a], 16)
        SENT = 16 * TOPK * PASSES

        xk = [0]

        def carve_x(n, parts=128):
            a = xT[0:parts, xk[0]:xk[0] + n]
            xk[0] += n
            return a
        slot_x = [carve_x(ROW) for _ in range(STEPS)]
        slot_xT = [carve_x(128) for _ in range(2)]
        tile_w = [carve_x(EW) for _ in range(3)]
        act_r = [carve_x(FB * 128).rearrange("p (k s) -> p k s", k=FB) for _ in range(2)]
        y_row = [carve_x(D) for _ in range(STEPS)]
        y_to = [carve_x(1).bitcast(U32) for _ in range(STEPS)]
        assert xk[0] <= TOKENS
        routed_rows = nc.dram_tensor("routed_rows", (ASSIGNED + SPARE, D), F32, kind="Internal").ap()
        slot_in = [sem(f"slot_in{r}") for r in range(STEPS)]
        y_sent = [sem(f"y_sent{r}") for r in range(STEPS)]
        turned, turn_ev, to_ready, w_ready, r_mm, r_act, r_out, r_ev = (sem(n) for n in (
            "turned", "turn_ev", "to_ready", "w_ready", "r_mm", "r_act", "r_out", "r_ev"))
        TURNS = SLOT_TILES // STEPS

        def routed_sp(sp):
            def load(r, first):
                sp.dma_start(slot_x[r], slot_rows[bass.ds(first * 128, 128), :]).then_inc(slot_in[r], 16)
            for a in range(2):
                sp.wait_ge(sent[a], SENT)
            sp.wait_ge(pass_in, PASSES)
            for r in range(STEPS):
                load(r, r)
            with sp.Fori(0, TURNS - 1) as i:
                for r in range(STEPS):
                    sp.wait_ge(turn_ev, i * STEPS + r + 1)
                    sp.wait_ge(to_ready, i * STEPS + r + 1)
                    load(r, i * STEPS + (STEPS + r))
            for r in range(2):
                sp.wait_ge(turn_ev, (TURNS - 1) * STEPS + r + 1)
                sp.wait_ge(to_ready, (TURNS - 1) * STEPS + r + 1)
                load(r, SLOT_TILES + r)

        def routed_pe(pe):
            def turn(c, got):
                pe.wait_ge(slot_in[c % STEPS], got)
                nc.tensor.transpose(bank[c % 2][:, 0:128], slot_x[c % STEPS][:, 0:D], ident[:, :]).then_inc(turned, 1)

            def hidden(c):
                for k in range(FB):
                    last = nc.tensor.matmul(bank[2 + c % 2][:, k * 128:(k + 1) * 128], w1_blocks(tile_w[c % 3], k), slot_xT[c % 2],
                                            start=True, stop=True)
                last.then_inc(r_mm, 1)
            turn(0, 16)
            turn(1, 16)
            pe.wait_ge(turn_ev, 1)
            pe.wait_ge(w_ready, 1)
            hidden(0)
            with pe.Fori(0, TURNS) as i:
                for u in range(STEPS):
                    pe.wait_ge(turn_ev, i * STEPS + u + 1)
                    turn(u + 2, (i + (u + 2) // STEPS) * 16 + 16)
                    pe.wait_ge(turn_ev, i * STEPS + u + 2)
                    pe.wait_ge(w_ready, i * STEPS + u + 2)
                    pe.wait_ge(r_act, i * (STEPS * FB) + (u * FB + FB))
                    hidden(u + 1)
                    pe.wait_ge(r_ev, i * STEPS + u + 1)
                    for k in range(FB):
                        pe.wait_ge(r_act, i * (STEPS * FB) + (u * FB + k + 1 + FB))
                        last = nc.tensor.matmul(bank[4 + u % 2][:, 0:D], act_r[u % 2][:, k, :], w2_blocks(tile_w[u % 3], k),
                                                start=(k == 0), stop=(k == FB - 1))
                    last.then_inc(r_out, 1)

        def routed_act(act):
            with act.Fori(0, TURNS) as i:
                for u in range(STEPS):
                    act.wait_ge(r_mm, i * STEPS + u + 1)
                    act.wait_ge(r_out, i * STEPS + u + 1)
                    for k in range(FB):
                        nc.scalar.activation(act_r[u % 2][:, k, :], bank[2 + u % 2][:, k * 128:(k + 1) * 128], ACT.Gelu,
                                             bias=tile_w[u % 3][:, 2 * HIDDEN + k:2 * HIDDEN + k + 1]).then_inc(r_act, 1)

        def routed_dve(dve):
            dve.sem_inc(r_act, FB)
            dve.sem_inc(r_ev, 2)
            dve.sem_inc(r_out, 2)
            dve.wait_ge(late_w, LATE_W)

            def weights_of(c, tile):
                e = dve.value_load(expert_of[0:1, tile], min_val=0, max_val=ALL_EXPERTS - 1)
                nc.vector.tensor_copy(tile_w[c % 3].unsqueeze(1), expert_w[:, bass.ds(e, 1), :]).then_inc(w_ready, 1)

            def output_of(r):
                nc.vector.tensor_copy(y_row[r], bank[4 + r % 2][:, 0:D]).then_inc(r_ev, 1)

            def turn_out(c):
                nc.vector.tensor_copy(slot_xT[c % 2], bank[c % 2][:, 0:128]).then_inc(turn_ev, 1)
            for c in range(2):
                weights_of(c, slice(c, c + 1))
                dve.wait_ge(turned, c + 1)
                turn_out(c)
            def steps(i, first):
                for u in range(STEPS):
                    dve.wait_ge(r_out, i * STEPS + u + 2)
                    weights_of(u + 2, bass.ds(i * STEPS + (u + 2), 1))
                    dve.wait_ge(turned, i * STEPS + u + 3)
                    dve.wait_ge(r_mm, i * STEPS + u + 1)
                    turn_out(u + 2)
                    if u or not first:
                        output_of((u - 1) % STEPS)
                    if not first:
                        dve.wait_ge(y_sent[u], i * 16)
                    nc.vector.tensor_copy(y_to[u], slot_x[u].bitcast(U32)[:, D:ROW]).then_inc(to_ready, 1)
            steps(0, True)
            with dve.Fori(1, TURNS) as i:
                steps(i, False)
            dve.wait_ge(r_out, SLOT_TILES + 2)
            output_of(STEPS - 1)

        def routed_pool(pool):
            with pool.Fori(0, TURNS) as i:
                for u in range(STEPS):
                    pool.wait_ge(to_ready, i * STEPS + u + 1)
                    pool.wait_ge(r_ev, i * STEPS + u + 3)
                    settle(pool)
                    nc.gpsimd.indirect_dma_start(routed_rows, bass.IndirectOffsetOnAxis(ap=y_to[u], axis=0),
                                                 y_row[u], None).then_inc(y_sent[u], 16)

        xk[0] = 0
        ZR, OR = 3, 4
        z_in = [carve_x(CT * TOPK * D).rearrange("p (t k d) -> p t k d", t=CT, k=TOPK) for _ in range(ZR)]
        obuf = [carve_x(CT * D).rearrange("p (t d) -> p t d", t=CT) for _ in range(OR)]
        combT = [carve_x(CT * 128, ALL_EXPERTS) for _ in range(2)]
        z_got = [sem(f"z_got{r}") for r in range(ZR)]
        y_out = [sem(f"y_out{r}") for r in range(OR)]
        comb_const, comb_mm, comb_ev, y_mm, y_add = (sem(n) for n in ("comb_const", "comb_mm", "comb_ev", "y_mm", "y_add"))
        out_rows = out.rearrange("b s d -> (b s) d")
        choices = routed_rows.rearrange("(n k) d -> n (k d)", k=TOPK)

        def group(j):
            return range(j * CT, min((j + 1) * CT, TILES))

        def final_pe(pe):
            def weights_turned(j):
                if j >= 2:
                    pe.wait_ge(comb_ev, j - 1)
                for t in group(j):
                    last = nc.tensor.transpose(bank[2 + j % 2][0:EXPERTS, (t - j * CT) * 128:(t - j * CT + 1) * 128],
                                               combine[:, t, :], ident[:, :])
                last.then_inc(comb_mm, 1)
            pe.wait_ge(sh_add, PASSES + 2)
            pe.wait_ge(r_act, FB * (SLOT_TILES + 1))
            weights_turned(0)
            for j in range(CGROUPS):
                if j < CGROUPS - 1:
                    weights_turned(j + 1)
                pe.wait_ge(comb_ev, j + 1)
                if j >= 2:
                    pe.wait_ge(y_add, j - 1)
                for t in group(j):
                    at_t = slice((t - j * CT) * 128, (t - j * CT + 1) * 128)
                    nc.tensor.matmul(bank[j % 2][:, at_t], hT[:, t * 128:(t + 1) * 128], ident[:, :], start=True, stop=False)
                    last = nc.tensor.matmul(bank[j % 2][:, at_t], combT[j % 2][:, at_t], b2_rows[:, :], start=False, stop=True)
                last.then_inc(y_mm, 1)

        def final_act(act):
            act.wait_ge(comb_const, 2)
            for j in range(CGROUPS):
                act.wait_ge(comb_mm, j + 1)
                if j >= 2:
                    act.wait_ge(y_mm, j - 1)
                m = len(group(j)) * 128
                nc.scalar.copy(combT[j % 2][0:EXPERTS, 0:m], bank[2 + j % 2][0:EXPERTS, 0:m]).then_inc(comb_ev, 1)

        y_step = sem("y_step")

        def final_dve(dve):
            dve.wait_ge(r_out, SLOT_TILES + 2)
            for u in range(STEPS):
                dve.wait_ge(y_sent[u], 16 * TURNS)
            for r in range(2):
                nc.vector.memset(combT[r], 1.0 / SHARED).then_inc(comb_const, 1)
            done = 0
            for j in range(CGROUPS):
                dve.wait_ge(y_mm, j + 1)
                dve.wait_ge(z_got[j % ZR], 16 * (j // ZR + 1))
                if j >= OR:
                    dve.wait_ge(y_out[j % OR], 16 * (j // OR))
                for k in range(TOPK):
                    if k:
                        dve.wait_ge(y_step, done)
                    for t in group(j):
                        a = t - j * CT
                        o = obuf[j % OR][:, a, :]
                        base = o if k else bank[j % 2][:, a * 128:(a + 1) * 128]
                        ins = nc.vector.scalar_tensor_tensor(o, z_in[j % ZR][:, a, k, :], top_w[:, t, k:k + 1], base, ALU.mult, ALU.add)
                        if k < TOPK - 1:
                            ins.then_inc(y_step, 1)
                            done += 1
                ins.then_inc(y_add, 1)

        def final_sp(sp):
            def load(j):
                n = len(group(j))
                sp.dma_start(z_in[j % ZR][:, 0:n, :, :].rearrange("p t k d -> p t (k d)"),
                             choices[j * CT * 128:(j * CT + n) * 128, :].rearrange("(t p) c -> p t c", p=128)).then_inc(z_got[j % ZR], 16)
            for u in range(STEPS):
                sp.wait_ge(y_sent[u], 16 * TURNS)
            sp.wait_ge(r_out, SLOT_TILES + 2)
            for j in range(ZR):
                load(j)
            for j in range(CGROUPS):
                n = len(group(j))
                sp.wait_ge(y_add, j + 1)
                sp.dma_start(out_rows[j * CT * 128:(j * CT + n) * 128, :].rearrange("(t p) d -> p t d", p=128),
                             obuf[j % OR][:, 0:n, :]).then_inc(y_out[j % OR], 16)
                if j + ZR < CGROUPS:
                    load(j + ZR)
            for r in range(OR):
                sp.wait_ge(y_out[r], 16 * (-(-(CGROUPS - r) // OR)))

        block = ctx.enter_context(nc.Block())

        @block.sync
        def _(sp):
            setup_loads(sp)
            tree_sp(sp)
            patch_sp(sp)
            weights_sp(sp)
            routed_sp(sp)
            final_sp(sp)

        @block.gpsimd
        def _(pool):
            setup_pool(pool)
            attn_masks_pool(pool)
            fill_pool(pool)
            norm1.pool(pool)
            attn_pool(pool)
            gate_pool(pool)
            norm2.pool(pool)
            dispatch_pool(pool)
            routed_pool(pool)

        @block.scalar
        def _(act):
            tree_act(act)
            norm1.act(act)
            attn_act(act)
            norm2.act(act)
            gate_act(act)
            shared_act(act)
            routed_act(act)
            final_act(act)

        @block.vector
        def _(dve):
            setup_dve_rows(dve)
            tree_rows_dve(dve)
            setup_dve(dve)
            tree_dve(dve)
            dve.wait_ge(cls_done, 1)
            norm1.dve(dve)
            attn_dve(dve)
            norm2.dve(dve)
            gate_dve(dve)
            shared_dve(dve)
            tile_experts_dve(dve)
            routed_dve(dve)
            final_dve(dve)

        @block.tensor
        def _(pe):
            setup_pe(pe)
            tree_pe(pe)
            for u in range(2):
                pe.wait_ge(tree_h[u], IMAGES // (2 * HALF) + 1)
                pe.wait_ge(patch_ev[u], CHUNKS // 2 + 1)
            pe.wait_ge(cls_done, 1)
            norm1.pe(pe)
            attn_pe(pe)
            pe.wait_ge(resid, IMAGES + 1)
            norm2_gate_pe(pe)
            ranks_pe(pe)
            shared_pe(pe)
            routed_pe(pe)
            final_pe(pe)


_INS = ['x', 'x_txt', 'L0_tok_W', 'L0_tok_b', 'L0_tok_class_token', 'L0_tok_pos_embed', 'L0_txt_p', 'L0_attn_Wl',
        'L0_attn_bl', 'L0_attn_Wq', 'L0_attn_Wk', 'L0_attn_Wv', 'L0_attn_Wo', 'L0_attn_bo', 'L0_ffn_gate_w',
        'L0_ffn_re_w1', 'L0_ffn_re_b1', 'L0_ffn_re_w2', 'L0_ffn_re_b2', 'L0_ffn_se_w1', 'L0_ffn_se_b1',
        'L0_ffn_se_w2', 'L0_ffn_se_b2']


def kernel(**inputs):
    import numpy as _np
    import concourse.bacc as _bacc
    from concourse import mybir as _mybir
    from concourse.bass_utils import run_bass_kernel_spmd as _run

    nc = _bacc.Bacc("TRN2", target_bir_lowering=False, num_devices=1)
    arrays, args = {}, []
    for name in _INS:
        a = _np.ascontiguousarray(inputs[name])
        arrays[f"in_{name}_dram"] = a
        args.append(nc.dram_tensor(f"in_{name}_dram", a.shape, _mybir.dt.from_np(a.dtype), kind="ExternalInput").ap())
    args.append(nc.dram_tensor("out_0_dram", (IMAGES, SEQ, D), _mybir.dt.float32, kind="ExternalOutput").ap())
    build(nc, *args)
    r = _run(nc, [arrays], core_ids=[0])
    return r.results[0]["out_0_dram"]
```
